# Optimizing a Trainium2 kernel written in Bass

```python
import numpy as np
import jax
import jax.numpy as jnp

def _softmax(x, axis=-1):
    return jax.nn.softmax(x, axis=axis)

def _gelu(x):
    return jax.nn.gelu(x, approximate=True)

def _silu(x):
    return jax.nn.silu(x)

def _sigmoid(x):
    return jax.nn.sigmoid(x)

def _layernorm(x, axis=-1, eps=1e-05):
    m = jnp.mean(x, axis=axis, keepdims=True)
    v = jnp.var(x, axis=axis, keepdims=True)
    return (x - m) / jnp.sqrt(v + eps)

def _scatter_add(tgt, idx, src, axis=0):
    return tgt.at[idx].add(src)

def _segment_sum(src, seg, n):
    return jax.ops.segment_sum(src, seg, n)
kernel_name = 'mk_gnn_ffn_d4_gnn_r32_4947c1'

def setup_inputs(seed: int=0):
    np.random.seed(seed)
    _w = jnp.asarray

    def _rec_inputs():
        import jax
        import jax.numpy as jnp
        _gk = jax.random.key(seed)
        x = -0.0002117 + 1 * jax.random.normal(jax.random.fold_in(_gk, 1), (3125, 256), jnp.float32)
        src = jax.random.randint(jax.random.fold_in(_gk, 2), (50000,), 0, 3125, jnp.int32)
        dst = jnp.minimum((3125 * jax.random.uniform(jax.random.fold_in(_gk, 3), (50000,)) ** 2.0).astype(jnp.int32), 99999)
        _o = jnp.argsort(dst, stable=True)
        src = src[_o]
        dst = dst[_o]
        edge_weight = jax.random.uniform(jax.random.fold_in(_gk, 13), (50000,), jnp.float32, 0.0, 1)
        node_vec = jax.random.uniform(jax.random.fold_in(_gk, 14), (3125,), jnp.float32, 0.0, 0.999833)
        return (x, src, dst, edge_weight, node_vec)
    x, src, dst, edge_weight, node_vec = _rec_inputs()

    def _L0_gnn_setup():
        import jax, jax.numpy as jnp
        import numpy as np
        N_NODES = 3125
        N_EDGES = 100000
        D_IN = 256
        D_OUT = 256
        key = jax.random.key(seed)
        k1, k2, k3, k4, k5 = jax.random.split(key, 5)
        x = jax.random.normal(k1, (N_NODES, D_IN), dtype=jnp.float32)
        W = jax.random.normal(k2, (D_OUT, D_IN), dtype=jnp.float32) * (1.0 / np.sqrt(D_IN))
        edge_row = jax.random.randint(k3, (N_EDGES,), 0, N_NODES, dtype=jnp.int32)
        edge_col = jax.random.randint(k4, (N_EDGES,), 0, N_NODES, dtype=jnp.int32)
        edge_val = jax.random.uniform(k5, (N_EDGES,), dtype=jnp.float32)
        return {'x': x, 'W': W, 'edge_row': edge_row, 'edge_col': edge_col, 'edge_val': edge_val}
    _L0_gnn_all = _L0_gnn_setup()
    _L0_gnn_in = {k: v for k, v in _L0_gnn_all.items() if k in ('W',)}
    del _L0_gnn_all

    def _L0_ffn_setup():
        import math
        import jax, jax.numpy as jnp
        import numpy as np
        CAPACITY_FACTOR = 1.25
        key = jax.random.key(seed)
        ks = jax.random.split(key, 5)
        B, L, D, F, E = (8, 256, 256, 1024, 8)
        h = jax.random.normal(ks[0], (B, L, D), dtype=jnp.float32)
        gate_w = jax.random.normal(ks[1], (D, E), dtype=jnp.float32) * 0.02
        gate_b = jnp.zeros((E,), dtype=jnp.float32)
        w1 = jax.random.normal(ks[2], (E, D, F), dtype=jnp.float32) * (1.0 / math.sqrt(D))
        b1 = jnp.zeros((E, F), dtype=jnp.float32)
        w2 = jax.random.normal(ks[3], (E, F, D), dtype=jnp.float32) * (1.0 / math.sqrt(F))
        b2 = jnp.zeros((E, D), dtype=jnp.float32)
        return {'h': h, 'gate_w': gate_w, 'gate_b': gate_b, 'w1': w1, 'b1': b1, 'w2': w2, 'b2': b2}
    _L0_ffn_all = _L0_ffn_setup()
    _L0_ffn_in = {k: v for k, v in _L0_ffn_all.items() if k in ('gate_w', 'gate_b', 'w1', 'b1', 'w2', 'b2')}
    del _L0_ffn_all

    def _L1_gnn_setup():
        import jax, jax.numpy as jnp
        import numpy as np
        N_NODES, N_EDGES, D_IN, D_HID, N_LAYERS = (50000, 25000, 256, 256, 3)
        key = jax.random.key(seed)
        k_x, k_e, k_w = jax.random.split(key, 3)
        x = jax.random.normal(k_x, (N_NODES, D_IN), dtype=jnp.float32)
        edge_index = jax.random.randint(k_e, (2, N_EDGES), 0, N_NODES, dtype=jnp.int32)
        W = jax.random.normal(k_w, (N_LAYERS, D_IN, D_HID), dtype=jnp.float32) * (1.0 / np.sqrt(D_IN))
        b = jnp.zeros((N_LAYERS, D_HID), dtype=jnp.float32)
        return {'x': x, 'edge_index': edge_index, 'W': W, 'b': b}
    _L1_gnn_all = _L1_gnn_setup()
    _L1_gnn_in = {k: v for k, v in _L1_gnn_all.items() if k in ('W', 'b')}
    del _L1_gnn_all

    def _L1_ffn_setup():
        import jax, jax.numpy as jnp
        import numpy as np
        B, S, D, F, E, K = (8, 64, 256, 1024, 8, 2)
        key = jax.random.key(seed)
        ks = jax.random.split(key, 10)
        s = 0.02
        return {'x': jax.random.normal(ks[0], (B, S, D), dtype=jnp.float32), 'Wr': jax.random.normal(ks[1], (D, E), dtype=jnp.float32) * s, 'W1s': jax.random.normal(ks[2], (D, F), dtype=jnp.float32) * s, 'b1s': jnp.zeros((F,), dtype=jnp.float32), 'W2s': jax.random.normal(ks[3], (F, D), dtype=jnp.float32) * s, 'b2s': jnp.zeros((D,), dtype=jnp.float32), 'W1p': jax.random.normal(ks[4], (E, D, F), dtype=jnp.float32) * s, 'b1p': jnp.zeros((E, F), dtype=jnp.float32), 'W2p': jax.random.normal(ks[5], (E, F, D), dtype=jnp.float32) * s, 'b2p': jnp.zeros((E, D), dtype=jnp.float32)}
    _L1_ffn_all = _L1_ffn_setup()
    _L1_ffn_in = {k: v for k, v in _L1_ffn_all.items() if k in ('Wr', 'W1s', 'b1s', 'W2s', 'b2s', 'W1p', 'b1p', 'W2p', 'b2p')}
    del _L1_ffn_all

    def _L2_gnn_setup():
        import jax, jax.numpy as jnp
        import numpy as np
        N_NODES = 50000
        N_EDGES = 25000
        D_IN = 256
        D_OUT = 256
        BN_EPS = 1e-05
        key = jax.random.key(seed)
        k1, k2, k3, k4 = jax.random.split(key, 4)
        x = jax.random.normal(k1, (N_NODES, D_IN), dtype=jnp.float32)
        edge_index = jax.random.randint(k2, (2, N_EDGES), 0, N_NODES, dtype=jnp.int64)
        W = jax.random.normal(k3, (D_OUT, D_IN), dtype=jnp.float32) / np.sqrt(D_IN)
        b = jnp.zeros((D_OUT,), dtype=jnp.float32)
        gamma = jnp.ones((D_OUT,), dtype=jnp.float32)
        beta = jnp.zeros((D_OUT,), dtype=jnp.float32)
        return {'x': x, 'edge_index': edge_index, 'W': W, 'b': b, 'gamma': gamma, 'beta': beta}
    _L2_gnn_all = _L2_gnn_setup()
    _L2_gnn_in = {k: v for k, v in _L2_gnn_all.items() if k in ('W', 'b', 'gamma', 'beta')}
    del _L2_gnn_all

    def _L2_ffn_setup():
        import jax, jax.numpy as jnp
        import numpy as np
        E, D, H, TOP_K = (6, 256, 256, 2)
        ROUTER_H = D // 2
        key = jax.random.key(seed)
        ks = jax.random.split(key, 12)
        s = 1.0 / np.sqrt(D)
        sh = 1.0 / np.sqrt(H)
        sr = 1.0 / np.sqrt(ROUTER_H)
        return {'features': jax.random.normal(ks[0], (8, 128, D), dtype=jnp.float32), 'router_w1': jax.random.uniform(ks[1], (D, ROUTER_H), jnp.float32, -s, s), 'router_b1': jnp.zeros((ROUTER_H,), jnp.float32), 'router_w2': jax.random.uniform(ks[2], (ROUTER_H, E), jnp.float32, -sr, sr), 'router_b2': jnp.zeros((E,), jnp.float32), 'expert_w1': jax.random.uniform(ks[3], (E, D, H), jnp.float32, -s, s), 'expert_b1': jnp.zeros((E, H), jnp.float32), 'expert_w2': jax.random.uniform(ks[4], (E, H, H), jnp.float32, -sh, sh), 'expert_b2': jnp.zeros((E, H), jnp.float32), 'expert_w3': jax.random.uniform(ks[5], (E, H, D), jnp.float32, -sh, sh), 'expert_b3': jnp.zeros((E, D), jnp.float32)}
    _L2_ffn_all = _L2_ffn_setup()
    _L2_ffn_in = {k: v for k, v in _L2_ffn_all.items() if k in ('router_w1', 'router_b1', 'router_w2', 'router_b2', 'expert_w1', 'expert_b1', 'expert_w2', 'expert_b2', 'expert_w3', 'expert_b3')}
    del _L2_ffn_all

    def _L3_gnn_setup():
        import jax, jax.numpy as jnp
        import numpy as np
        from jax import lax
        N, E, D = (256, 8192, 256)
        NH, FOUT = (4, 64)
        D_STATE, D_CONV, DT_RANK = (16, 4, 16)

        def _layer_norm(x, g, b, eps=1e-05):
            mu = jnp.mean(x, -1, keepdims=True)
            var = jnp.var(x, -1, keepdims=True)
            return (x - mu) * lax.rsqrt(var + eps) * g + b

        def _mamba(xs, in_proj_w, conv_w, conv_b, x_proj_w, dt_proj_w, dt_proj_b, A_log, D_param, out_proj_w):
            n = xs.shape[0]
            xz = xs @ in_proj_w.T
            xc, z = jnp.split(xz, 2, axis=-1)
            K = conv_w.shape[1]
            xp = jnp.pad(xc, ((K - 1, 0), (0, 0)))
            xc = sum((xp[k:k + n] * conv_w[:, k] for k in range(K))) + conv_b
            xc = jax.nn.silu(xc)
            dbc = xc @ x_proj_w.T
            dt = jax.nn.softplus(dbc[:, :DT_RANK] @ dt_proj_w.T + dt_proj_b)
            Bm = dbc[:, DT_RANK:DT_RANK + D_STATE]
            Cm = dbc[:, DT_RANK + D_STATE:]
            A = -jnp.exp(A_log)
            dA = jnp.exp(dt[:, :, None] * A)
            dBx = (dt * xc)[:, :, None] * Bm[:, None, :]

            def step(h, t):
                dA_t, dBx_t, C_t = t
                h = dA_t * h + dBx_t
                return (h, h @ C_t)
            _, y = lax.scan(step, jnp.zeros((xc.shape[1], D_STATE), xs.dtype), (dA, dBx, Cm))
            y = y + xc * D_param
            y = y * jax.nn.silu(z)
            return y @ out_proj_w.T

        def _forward(x, edge_index, deg_noise, gat_w, gat_a_src, gat_a_tgt, gat_b, ln_local_g, ln_local_b, ln_global_g, ln_global_b, ln2_g, ln2_b, in_proj_w, conv_w, conv_b, x_proj_w, dt_proj_w, dt_proj_b, A_log, D_param, out_proj_w, wl, wg, ff1_w, ff1_b, ff2_w, ff2_b):
            n = x.shape[0]
            src, tgt = (edge_index[0], edge_index[1])
            proj = (x @ gat_w.T).reshape(n, NH, FOUT)
            s_src = jnp.sum(proj * gat_a_src, -1)
            s_tgt = jnp.sum(proj * gat_a_tgt, -1)
            e = jax.nn.leaky_relu(s_src[src] + s_tgt[tgt], 0.2)
            exp_e = jnp.exp(e - jnp.max(e))
            denom = jax.ops.segment_sum(exp_e, tgt, num_segments=n)
            attn = exp_e / (denom[tgt] + 1e-16)
            agg = jax.ops.segment_sum(proj[src] * attn[:, :, None], tgt, num_segments=n)
            h_local = jax.nn.elu((agg + x.reshape(n, NH, FOUT)).reshape(n, NH * FOUT) + gat_b)
            h_local = _layer_norm(h_local, ln_local_g, ln_local_b)
            deg = jax.ops.segment_sum(jnp.ones((src.shape[0],), x.dtype), src, num_segments=n)
            perm = jnp.argsort(deg + deg_noise, stable=True)
            inv = jnp.argsort(perm)
            y = _mamba(x[perm], in_proj_w, conv_w, conv_b, x_proj_w, dt_proj_w, dt_proj_b, A_log, D_param, out_proj_w)
            h_attn = _layer_norm(x + y[inv], ln_global_g, ln_global_b)
            gate = jax.nn.sigmoid(h_local @ wl.T + h_attn @ wg.T)
            h = gate * h_local + (1.0 - gate) * h_attn
            ff = jax.nn.relu(h @ ff1_w.T + ff1_b) @ ff2_w.T + ff2_b
            return _layer_norm(h + ff, ln2_g, ln2_b)
        key = jax.random.key(seed)
        ks = jax.random.split(key, 24)
        w = lambda i, shape, s=0.05: jax.random.normal(ks[i], shape, dtype=jnp.float32) * s
        return {'x': jax.random.normal(ks[0], (N, D), dtype=jnp.float32), 'edge_index': jax.random.randint(ks[1], (2, E), 0, N, dtype=jnp.int32), 'edge_prob': jax.random.uniform(ks[2], (E,), dtype=jnp.float32), 'deg_noise': jax.random.uniform(ks[3], (N,), dtype=jnp.float32), 'gat_w': w(4, (NH * FOUT, D)), 'gat_a_src': w(5, (NH, FOUT)), 'gat_a_tgt': w(6, (NH, FOUT)), 'gat_b': jnp.zeros((NH * FOUT,), jnp.float32), 'ln_local_g': jnp.ones((D,), jnp.float32), 'ln_local_b': jnp.zeros((D,), jnp.float32), 'ln_global_g': jnp.ones((D,), jnp.float32), 'ln_global_b': jnp.zeros((D,), jnp.float32), 'ln2_g': jnp.ones((D,), jnp.float32), 'ln2_b': jnp.zeros((D,), jnp.float32), 'in_proj_w': w(7, (2 * D, D)), 'conv_w': w(8, (D, D_CONV), 0.2), 'conv_b': jnp.zeros((D,), jnp.float32), 'x_proj_w': w(9, (DT_RANK + 2 * D_STATE, D)), 'dt_proj_w': w(10, (D, DT_RANK)), 'dt_proj_b': w(11, (D,), 0.1) - 4.0, 'A_log': jnp.log(jnp.tile(jnp.arange(1, D_STATE + 1, dtype=jnp.float32), (D, 1))), 'D_param': jnp.ones((D,), jnp.float32), 'out_proj_w': w(12, (D, D)), 'wl': w(13, (D, D)), 'wg': w(14, (D, D)), 'ff1_w': w(15, (2 * D, D)), 'ff1_b': jnp.zeros((2 * D,), jnp.float32), 'ff2_w': w(16, (D, 2 * D)), 'ff2_b': jnp.zeros((D,), jnp.float32)}
    _L3_gnn_all = _L3_gnn_setup()
    _L3_gnn_in = {k: v for k, v in _L3_gnn_all.items() if k in ('gat_w', 'gat_a_src', 'gat_a_tgt', 'gat_b', 'ln_local_g', 'ln_local_b', 'ln_global_g', 'ln_global_b', 'ln2_g', 'ln2_b', 'in_proj_w', 'conv_w', 'conv_b', 'x_proj_w', 'dt_proj_w', 'dt_proj_b', 'A_log', 'D_param', 'out_proj_w', 'wl', 'wg', 'ff1_w', 'ff1_b', 'ff2_w', 'ff2_b')}
    del _L3_gnn_all

    def _L3_ffn_setup():
        import jax, jax.numpy as jnp
        import numpy as np
        C = 256
        HID = 1024
        E = 8
        TEMP = 1.0
        key = jax.random.key(seed)
        ks = jax.random.split(key, 7)
        x = jax.random.normal(ks[0], (8, 512, C), dtype=jnp.float32)
        W1 = jax.random.normal(ks[1], (C, HID), dtype=jnp.float32) * 0.02
        b1 = jnp.zeros((HID,), dtype=jnp.float32)
        Wg = jax.random.normal(ks[2], (HID, E), dtype=jnp.float32) * 0.02
        bg = jnp.zeros((E,), dtype=jnp.float32)
        Wd = jax.random.normal(ks[3], (E, HID, C), dtype=jnp.float32) * 0.02
        bd = jnp.zeros((E, C), dtype=jnp.float32)
        return {'x': x, 'W1': W1, 'b1': b1, 'Wg': Wg, 'bg': bg, 'Wd': Wd, 'bd': bd}
    _L3_ffn_all = _L3_ffn_setup()
    _L3_ffn_in = {k: v for k, v in _L3_ffn_all.items() if k in ('W1', 'b1', 'Wg', 'bg', 'Wd', 'bd')}
    del _L3_ffn_all
    return {'x': x, 'src': src, 'dst': dst, 'edge_weight': edge_weight, 'node_vec': node_vec, 'L0_gnn_W': _L0_gnn_in['W'], 'L0_ffn_gate_w': _L0_ffn_in['gate_w'], 'L0_ffn_gate_b': _L0_ffn_in['gate_b'], 'L0_ffn_w1': _L0_ffn_in['w1'], 'L0_ffn_b1': _L0_ffn_in['b1'], 'L0_ffn_w2': _L0_ffn_in['w2'], 'L0_ffn_b2': _L0_ffn_in['b2'], 'L1_gnn_W': _L1_gnn_in['W'], 'L1_gnn_b': _L1_gnn_in['b'], 'L1_ffn_Wr': _L1_ffn_in['Wr'], 'L1_ffn_W1s': _L1_ffn_in['W1s'], 'L1_ffn_b1s': _L1_ffn_in['b1s'], 'L1_ffn_W2s': _L1_ffn_in['W2s'], 'L1_ffn_b2s': _L1_ffn_in['b2s'], 'L1_ffn_W1p': _L1_ffn_in['W1p'], 'L1_ffn_b1p': _L1_ffn_in['b1p'], 'L1_ffn_W2p': _L1_ffn_in['W2p'], 'L1_ffn_b2p': _L1_ffn_in['b2p'], 'L2_gnn_W': _L2_gnn_in['W'], 'L2_gnn_b': _L2_gnn_in['b'], 'L2_gnn_gamma': _L2_gnn_in['gamma'], 'L2_gnn_beta': _L2_gnn_in['beta'], 'L2_ffn_router_w1': _L2_ffn_in['router_w1'], 'L2_ffn_router_b1': _L2_ffn_in['router_b1'], 'L2_ffn_router_w2': _L2_ffn_in['router_w2'], 'L2_ffn_router_b2': _L2_ffn_in['router_b2'], 'L2_ffn_expert_w1': _L2_ffn_in['expert_w1'], 'L2_ffn_expert_b1': _L2_ffn_in['expert_b1'], 'L2_ffn_expert_w2': _L2_ffn_in['expert_w2'], 'L2_ffn_expert_b2': _L2_ffn_in['expert_b2'], 'L2_ffn_expert_w3': _L2_ffn_in['expert_w3'], 'L2_ffn_expert_b3': _L2_ffn_in['expert_b3'], 'L3_gnn_gat_w': _L3_gnn_in['gat_w'], 'L3_gnn_gat_a_src': _L3_gnn_in['gat_a_src'], 'L3_gnn_gat_a_tgt': _L3_gnn_in['gat_a_tgt'], 'L3_gnn_gat_b': _L3_gnn_in['gat_b'], 'L3_gnn_ln_local_g': _L3_gnn_in['ln_local_g'], 'L3_gnn_ln_local_b': _L3_gnn_in['ln_local_b'], 'L3_gnn_ln_global_g': _L3_gnn_in['ln_global_g'], 'L3_gnn_ln_global_b': _L3_gnn_in['ln_global_b'], 'L3_gnn_ln2_g': _L3_gnn_in['ln2_g'], 'L3_gnn_ln2_b': _L3_gnn_in['ln2_b'], 'L3_gnn_in_proj_w': _L3_gnn_in['in_proj_w'], 'L3_gnn_conv_w': _L3_gnn_in['conv_w'], 'L3_gnn_conv_b': _L3_gnn_in['conv_b'], 'L3_gnn_x_proj_w': _L3_gnn_in['x_proj_w'], 'L3_gnn_dt_proj_w': _L3_gnn_in['dt_proj_w'], 'L3_gnn_dt_proj_b': _L3_gnn_in['dt_proj_b'], 'L3_gnn_A_log': _L3_gnn_in['A_log'], 'L3_gnn_D_param': _L3_gnn_in['D_param'], 'L3_gnn_out_proj_w': _L3_gnn_in['out_proj_w'], 'L3_gnn_wl': _L3_gnn_in['wl'], 'L3_gnn_wg': _L3_gnn_in['wg'], 'L3_gnn_ff1_w': _L3_gnn_in['ff1_w'], 'L3_gnn_ff1_b': _L3_gnn_in['ff1_b'], 'L3_gnn_ff2_w': _L3_gnn_in['ff2_w'], 'L3_gnn_ff2_b': _L3_gnn_in['ff2_b'], 'L3_ffn_W1': _L3_ffn_in['W1'], 'L3_ffn_b1': _L3_ffn_in['b1'], 'L3_ffn_Wg': _L3_ffn_in['Wg'], 'L3_ffn_bg': _L3_ffn_in['bg'], 'L3_ffn_Wd': _L3_ffn_in['Wd'], 'L3_ffn_bd': _L3_ffn_in['bd']}

def reference(x, src, dst, edge_weight, node_vec, L0_gnn_W, L0_ffn_gate_w, L0_ffn_gate_b, L0_ffn_w1, L0_ffn_b1, L0_ffn_w2, L0_ffn_b2, L1_gnn_W, L1_gnn_b, L1_ffn_Wr, L1_ffn_W1s, L1_ffn_b1s, L1_ffn_W2s, L1_ffn_b2s, L1_ffn_W1p, L1_ffn_b1p, L1_ffn_W2p, L1_ffn_b2p, L2_gnn_W, L2_gnn_b, L2_gnn_gamma, L2_gnn_beta, L2_ffn_router_w1, L2_ffn_router_b1, L2_ffn_router_w2, L2_ffn_router_b2, L2_ffn_expert_w1, L2_ffn_expert_b1, L2_ffn_expert_w2, L2_ffn_expert_b2, L2_ffn_expert_w3, L2_ffn_expert_b3, L3_gnn_gat_w, L3_gnn_gat_a_src, L3_gnn_gat_a_tgt, L3_gnn_gat_b, L3_gnn_ln_local_g, L3_gnn_ln_local_b, L3_gnn_ln_global_g, L3_gnn_ln_global_b, L3_gnn_ln2_g, L3_gnn_ln2_b, L3_gnn_in_proj_w, L3_gnn_conv_w, L3_gnn_conv_b, L3_gnn_x_proj_w, L3_gnn_dt_proj_w, L3_gnn_dt_proj_b, L3_gnn_A_log, L3_gnn_D_param, L3_gnn_out_proj_w, L3_gnn_wl, L3_gnn_wg, L3_gnn_ff1_w, L3_gnn_ff1_b, L3_gnn_ff2_w, L3_gnn_ff2_b, L3_ffn_W1, L3_ffn_b1, L3_ffn_Wg, L3_ffn_bg, L3_ffn_Wd, L3_ffn_bd):
    import jax
    import jax.numpy as jnp

    def _L0_gnn_ref(x, W, edge_row, edge_col, edge_val):
        import jax, jax.numpy as jnp
        import numpy as np
        N_NODES = 3125
        N_EDGES = 100000
        D_IN = 256
        D_OUT = 256
        h = jnp.einsum('nd,od->no', x, W)
        msgs = edge_val[:, None] * h[edge_col]
        out = jax.ops.segment_sum(msgs, edge_row, num_segments=N_NODES)
        return out

    def _L0_ffn_ref(h, gate_w, gate_b, w1, b1, w2, b2):
        import math
        import jax, jax.numpy as jnp
        import numpy as np
        CAPACITY_FACTOR = 1.25
        B, L, D = h.shape
        E = gate_w.shape[1]
        T = B * L
        C = max(1, math.ceil(CAPACITY_FACTOR * T / E))
        x = h.reshape(T, D)
        logits = x @ gate_w + gate_b
        probs = jax.nn.softmax(logits, axis=-1)
        idx = jnp.argmax(probs, axis=-1)
        prb = jnp.take_along_axis(probs, idx[:, None], axis=1)[:, 0]
        one_hot = jax.nn.one_hot(idx, E, dtype=jnp.float32)
        pos = (jnp.cumsum(one_hot, axis=0) * one_hot).sum(-1).astype(jnp.int32) - 1
        kept = pos < C
        pos_safe = jnp.where(kept, pos, C)
        buf = jnp.zeros((E, C, D), dtype=h.dtype).at[idx, pos_safe].set(x, mode='drop')
        hmid = jax.nn.relu(jnp.einsum('ecd,edf->ecf', buf, w1) + b1[:, None, :])
        ybuf = jnp.einsum('ecf,efd->ecd', hmid, w2) + b2[:, None, :]
        pos_g = jnp.minimum(pos, C - 1)
        y_tok = ybuf[idx, pos_g] * (prb * kept)[:, None]
        y = y_tok.reshape(B, L, D)
        y = jnp.nan_to_num(y, nan=0.0, posinf=10000.0, neginf=-10000.0)
        return y

    def _L1_gnn_ref(x, edge_index, W, b):
        import jax, jax.numpy as jnp
        import numpy as np
        N_NODES, N_EDGES, D_IN, D_HID, N_LAYERS = (50000, 25000, 256, 256, 3)
        'Stacked GCNConv (PyG semantics: self-loops + symmetric norm) with ReLU.\n            Dropout is identity (eval mode) for a deterministic baseline.'
        N = x.shape[0]
        loops = jnp.arange(N, dtype=edge_index.dtype)
        src = jnp.concatenate([edge_index[0], loops])
        dst = jnp.concatenate([edge_index[1], loops])
        deg = jax.ops.segment_sum(jnp.ones(dst.shape, jnp.float32), dst, num_segments=N)
        dinv = jnp.where(deg > 0, jax.lax.rsqrt(deg), 0.0)
        norm = (dinv[src] * dinv[dst])[:, None]
        h = x
        for l in range(W.shape[0]):
            t = h @ W[l]
            msg = t[src] * norm
            agg = jax.ops.segment_sum(msg, dst, num_segments=N)
            h = jax.nn.relu(agg + b[l])
        return h

    def _L1_ffn_ref(x, Wr, W1s, b1s, W2s, b2s, W1p, b1p, W2p, b2p):
        import jax, jax.numpy as jnp
        import numpy as np
        B, S, D, F, E, K = (8, 64, 256, 1024, 8, 2)
        gelu = lambda t: jax.nn.gelu(t, approximate=False)
        shared = gelu(x @ W1s + b1s) @ W2s + b2s
        rw = jax.nn.softmax(x @ Wr, axis=-1)
        topw, topi = jax.lax.top_k(rw, K)
        topw = topw / jnp.sum(topw, axis=-1, keepdims=True)
        mask = jnp.sum(jax.nn.one_hot(topi, E, dtype=topw.dtype) * topw[..., None], axis=-2)
        h = gelu(jnp.einsum('bsd,edf->bsef', x, W1p) + b1p)
        priv = jnp.einsum('bsef,efd->bsed', h, W2p) + b2p
        routed = jnp.einsum('bsed,bse->bsd', priv, mask)
        return shared + routed

    def _L2_gnn_ref(x, edge_index, W, b, gamma, beta):
        import jax, jax.numpy as jnp
        import numpy as np
        N_NODES = 50000
        N_EDGES = 25000
        D_IN = 256
        D_OUT = 256
        BN_EPS = 1e-05
        n = x.shape[0]
        loop = jnp.arange(n, dtype=edge_index.dtype)
        src = jnp.concatenate([edge_index[0], loop])
        dst = jnp.concatenate([edge_index[1], loop])
        ones = jnp.ones(src.shape[0], dtype=x.dtype)
        deg = jax.ops.segment_sum(ones, dst, num_segments=n)
        dinv = jnp.where(deg > 0, jax.lax.rsqrt(deg), 0.0)
        norm = dinv[src] * dinv[dst]
        h = x @ W.T
        msgs = h[src] * norm[:, None]
        agg = jax.ops.segment_sum(msgs, dst, num_segments=n) + b
        mean = jnp.mean(agg, axis=0)
        var = jnp.var(agg, axis=0)
        y = (agg - mean) * jax.lax.rsqrt(var + BN_EPS) * gamma + beta
        return jax.nn.relu(y)

    def _L2_ffn_ref(features, router_w1, router_b1, router_w2, router_b2, expert_w1, expert_b1, expert_w2, expert_b2, expert_w3, expert_b3):
        import jax, jax.numpy as jnp
        import numpy as np
        E, D, H, TOP_K = (6, 256, 256, 2)
        ROUTER_H = D // 2
        rh = jax.nn.relu(features @ router_w1 + router_b1)
        expert_logits = jax.nn.softmax(rh @ router_w2 + router_b2, axis=-1)
        top_w, top_i = jax.lax.top_k(expert_logits, TOP_K)
        routing_weights = jax.nn.softmax(top_w, axis=-1)
        h1 = jax.nn.relu(jnp.einsum('bsd,edh->bseh', features, expert_w1) + expert_b1)
        h2 = jax.nn.relu(jnp.einsum('bseh,ehf->bsef', h1, expert_w2) + expert_b2)
        expert_out = jnp.einsum('bsef,efo->bseo', h2, expert_w3) + expert_b3
        sel = jnp.take_along_axis(expert_out, top_i[:, :, :, None], axis=2)
        combined = jnp.sum(sel * routing_weights[..., None], axis=2)
        return combined

    def _L3_gnn_ref(x, edge_index, edge_prob, deg_noise, gat_w, gat_a_src, gat_a_tgt, gat_b, ln_local_g, ln_local_b, ln_global_g, ln_global_b, ln2_g, ln2_b, in_proj_w, conv_w, conv_b, x_proj_w, dt_proj_w, dt_proj_b, A_log, D_param, out_proj_w, wl, wg, ff1_w, ff1_b, ff2_w, ff2_b):
        import jax, jax.numpy as jnp
        import numpy as np
        from jax import lax
        N, E, D = (256, 8192, 256)
        NH, FOUT = (4, 64)
        D_STATE, D_CONV, DT_RANK = (16, 4, 16)

        def _layer_norm(x, g, b, eps=1e-05):
            mu = jnp.mean(x, -1, keepdims=True)
            var = jnp.var(x, -1, keepdims=True)
            return (x - mu) * lax.rsqrt(var + eps) * g + b

        def _mamba(xs, in_proj_w, conv_w, conv_b, x_proj_w, dt_proj_w, dt_proj_b, A_log, D_param, out_proj_w):
            n = xs.shape[0]
            xz = xs @ in_proj_w.T
            xc, z = jnp.split(xz, 2, axis=-1)
            K = conv_w.shape[1]
            xp = jnp.pad(xc, ((K - 1, 0), (0, 0)))
            xc = sum((xp[k:k + n] * conv_w[:, k] for k in range(K))) + conv_b
            xc = jax.nn.silu(xc)
            dbc = xc @ x_proj_w.T
            dt = jax.nn.softplus(dbc[:, :DT_RANK] @ dt_proj_w.T + dt_proj_b)
            Bm = dbc[:, DT_RANK:DT_RANK + D_STATE]
            Cm = dbc[:, DT_RANK + D_STATE:]
            A = -jnp.exp(A_log)
            dA = jnp.exp(dt[:, :, None] * A)
            dBx = (dt * xc)[:, :, None] * Bm[:, None, :]

            def step(h, t):
                dA_t, dBx_t, C_t = t
                h = dA_t * h + dBx_t
                return (h, h @ C_t)
            _, y = lax.scan(step, jnp.zeros((xc.shape[1], D_STATE), xs.dtype), (dA, dBx, Cm))
            y = y + xc * D_param
            y = y * jax.nn.silu(z)
            return y @ out_proj_w.T

        def _forward(x, edge_index, deg_noise, gat_w, gat_a_src, gat_a_tgt, gat_b, ln_local_g, ln_local_b, ln_global_g, ln_global_b, ln2_g, ln2_b, in_proj_w, conv_w, conv_b, x_proj_w, dt_proj_w, dt_proj_b, A_log, D_param, out_proj_w, wl, wg, ff1_w, ff1_b, ff2_w, ff2_b):
            n = x.shape[0]
            src, tgt = (edge_index[0], edge_index[1])
            proj = (x @ gat_w.T).reshape(n, NH, FOUT)
            s_src = jnp.sum(proj * gat_a_src, -1)
            s_tgt = jnp.sum(proj * gat_a_tgt, -1)
            e = jax.nn.leaky_relu(s_src[src] + s_tgt[tgt], 0.2)
            exp_e = jnp.exp(e - jnp.max(e))
            denom = jax.ops.segment_sum(exp_e, tgt, num_segments=n)
            attn = exp_e / (denom[tgt] + 1e-16)
            agg = jax.ops.segment_sum(proj[src] * attn[:, :, None], tgt, num_segments=n)
            h_local = jax.nn.elu((agg + x.reshape(n, NH, FOUT)).reshape(n, NH * FOUT) + gat_b)
            h_local = _layer_norm(h_local, ln_local_g, ln_local_b)
            deg = jax.ops.segment_sum(jnp.ones((src.shape[0],), x.dtype), src, num_segments=n)
            perm = jnp.argsort(deg + deg_noise, stable=True)
            inv = jnp.argsort(perm)
            y = _mamba(x[perm], in_proj_w, conv_w, conv_b, x_proj_w, dt_proj_w, dt_proj_b, A_log, D_param, out_proj_w)
            h_attn = _layer_norm(x + y[inv], ln_global_g, ln_global_b)
            gate = jax.nn.sigmoid(h_local @ wl.T + h_attn @ wg.T)
            h = gate * h_local + (1.0 - gate) * h_attn
            ff = jax.nn.relu(h @ ff1_w.T + ff1_b) @ ff2_w.T + ff2_b
            return _layer_norm(h + ff, ln2_g, ln2_b)
        return _forward(x, edge_index, deg_noise, gat_w, gat_a_src, gat_a_tgt, gat_b, ln_local_g, ln_local_b, ln_global_g, ln_global_b, ln2_g, ln2_b, in_proj_w, conv_w, conv_b, x_proj_w, dt_proj_w, dt_proj_b, A_log, D_param, out_proj_w, wl, wg, ff1_w, ff1_b, ff2_w, ff2_b)

    def _L3_ffn_ref(x, W1, b1, Wg, bg, Wd, bd):
        import jax, jax.numpy as jnp
        import numpy as np
        C = 256
        HID = 1024
        E = 8
        TEMP = 1.0
        orig_shape = x.shape
        xf = x.reshape(-1, orig_shape[-1])
        H = jax.nn.gelu(xf @ W1 + b1, approximate=False)
        probs = jax.nn.softmax((H @ Wg + bg) / TEMP, axis=-1)
        assign = jnp.argmax(probs, axis=-1)
        out = jnp.zeros_like(xf)
        for e in range(Wd.shape[0]):
            y = H @ Wd[e] + bd[e]
            sel = (assign == e)[:, None]
            out = out + jnp.where(sel, probs[:, e:e + 1] * y, 0.0)
        return out.reshape(orig_shape)
    edge_index = jnp.stack([src, dst])
    x = x + _L0_gnn_ref(_layernorm(x, axis=-1), L0_gnn_W, src, dst, edge_weight)
    x = x + _L0_ffn_ref(_layernorm(x, axis=-1)[None], L0_ffn_gate_w, L0_ffn_gate_b, L0_ffn_w1, L0_ffn_b1, L0_ffn_w2, L0_ffn_b2)[0]
    x = x + _L1_gnn_ref(_layernorm(x, axis=-1), edge_index, L1_gnn_W, L1_gnn_b)
    x = x + _L1_ffn_ref(_layernorm(x, axis=-1)[None], L1_ffn_Wr, L1_ffn_W1s, L1_ffn_b1s, L1_ffn_W2s, L1_ffn_b2s, L1_ffn_W1p, L1_ffn_b1p, L1_ffn_W2p, L1_ffn_b2p)[0]
    x = x + _L2_gnn_ref(_layernorm(x, axis=-1), edge_index, L2_gnn_W, L2_gnn_b, L2_gnn_gamma, L2_gnn_beta)
    x = x + _L2_ffn_ref(_layernorm(x, axis=-1)[None], L2_ffn_router_w1, L2_ffn_router_b1, L2_ffn_router_w2, L2_ffn_router_b2, L2_ffn_expert_w1, L2_ffn_expert_b1, L2_ffn_expert_w2, L2_ffn_expert_b2, L2_ffn_expert_w3, L2_ffn_expert_b3)[0]
    x = x + _L3_gnn_ref(_layernorm(x, axis=-1), edge_index, edge_weight, node_vec, L3_gnn_gat_w, L3_gnn_gat_a_src, L3_gnn_gat_a_tgt, L3_gnn_gat_b, L3_gnn_ln_local_g, L3_gnn_ln_local_b, L3_gnn_ln_global_g, L3_gnn_ln_global_b, L3_gnn_ln2_g, L3_gnn_ln2_b, L3_gnn_in_proj_w, L3_gnn_conv_w, L3_gnn_conv_b, L3_gnn_x_proj_w, L3_gnn_dt_proj_w, L3_gnn_dt_proj_b, L3_gnn_A_log, L3_gnn_D_param, L3_gnn_out_proj_w, L3_gnn_wl, L3_gnn_wg, L3_gnn_ff1_w, L3_gnn_ff1_b, L3_gnn_ff2_w, L3_gnn_ff2_b)
    x = x + _L3_ffn_ref(_layernorm(x, axis=-1)[None], L3_ffn_W1, L3_ffn_b1, L3_ffn_Wg, L3_ffn_bg, L3_ffn_Wd, L3_ffn_bd)[0]
    return x

_drawn_inputs = setup_inputs


def setup_inputs(seed=0):
    import zlib

    import numpy as np

    out = dict(_drawn_inputs(seed))
    spreads = {'L0_ffn_gate_b': (0.0, 0.1),
     'L0_ffn_b1': (0.0, 0.8),
     'L0_ffn_b2': (0.0, 0.8),
     'L1_gnn_b': (0.0, 0.1),
     'L1_ffn_b1s': (0.0, 0.629),
     'L1_ffn_b2s': (0.0, 0.1),
     'L1_ffn_b1p': (0.0, 0.8),
     'L1_ffn_b2p': (0.0, 0.305),
     'L2_gnn_b': (0.0, 0.8),
     'L2_gnn_gamma': (1.0, 0.2),
     'L2_gnn_beta': (0.0, 0.305),
     'L2_ffn_router_b1': (0.0, 0.641),
     'L2_ffn_router_b2': (0.0, 0.48),
     'L2_ffn_expert_b1': (0.0, 0.8),
     'L2_ffn_expert_b2': (0.0, 0.8),
     'L2_ffn_expert_b3': (0.0, 0.331),
     'L3_gnn_gat_b': (0.0, 0.591),
     'L3_gnn_ln_local_g': (1.0, 0.577),
     'L3_gnn_ln_local_b': (0.0, 0.529),
     'L3_gnn_ln_global_g': (1.0, 0.2),
     'L3_gnn_ln_global_b': (0.0, 0.519),
     'L3_gnn_ln2_g': (1.0, 0.2),
     'L3_gnn_ln2_b': (0.0, 0.319),
     'L3_gnn_conv_b': (0.0, 0.8),
     'L3_gnn_D_param': (1.0, 0.6),
     'L3_gnn_ff1_b': (0.0, 0.444),
     'L3_gnn_ff2_b': (0.0, 0.335),
     'L3_ffn_b1': (0.0, 0.8),
     'L3_ffn_bg': (0.0, 0.8),
     'L3_ffn_bd': (0.0, 0.8)}
    factors = {'node_vec': 7.268,
     'L2_ffn_expert_w1': 3.256,
     'L2_ffn_expert_w2': 2.824,
     'L3_gnn_gat_a_src': 6.869,
     'L3_gnn_gat_a_tgt': 8.0,
     'L3_gnn_in_proj_w': 5.823,
     'L3_gnn_conv_w': 6.302,
     'L3_gnn_x_proj_w': 8.0,
     'L3_gnn_dt_proj_w': 8.0,
     'L3_gnn_dt_proj_b': 8.0,
     'L3_gnn_A_log': 8.0,
     'L3_gnn_out_proj_w': 5.767,
     'L3_ffn_W1': 8.0,
     'L3_ffn_Wg': 8.0,
     'L3_ffn_Wd': 8.0}
    for name, (base, spread) in spreads.items():
        noise = np.random.default_rng([zlib.crc32(name.encode()), seed]).standard_normal(out[name].shape)
        drawn = base * np.exp(spread * noise) if base else spread * noise
        out[name] = jnp.asarray(drawn.astype(out[name].dtype))
    for name, factor in factors.items():
        out[name] = (out[name] * factor).astype(out[name].dtype)
    return out
```

```python
from contextlib import ExitStack

import concourse.bass as bass
from concourse import mybir

ALU = mybir.AluOpType
ACT = mybir.ActivationFunctionType
F32 = mybir.dt.float32
BF16 = mybir.dt.bfloat16
I32 = mybir.dt.int32
U32 = mybir.dt.uint32
AX_X = mybir.AxisListType.X
RMAX = bass.bass_isa.ReduceOp.max

P = 128
N_NODES = 3125
D = 256
KD = D // P
NT = (N_NODES + P - 1) // P
NP = NT * P
LAST = N_NODES - (NT - 1) * P
G = 5
NG = NT // G
N_EDGES = 50000
EP, EC = 125, 400
SLOT_TILES = (N_EDGES + NT * (P - 1)) // P
RING = 16
HALF = RING // 2
ST = (SLOT_TILES + RING - 1) // RING * RING
SP_ = ST + RING
REC = 4
CAP = 489
CAP_ROWS = 512
MAX_BLOCKS = 64
HEADS, STATES, TAPS, RANK = 4, 16, 4, 16
ds, ts = bass.ds, bass.ts

SEMAPHORES = {"hardware": range(124, 150), "engine": range(150, 250)}
ROW_DMAS = range(100, 100 + RING)


class Phase:

    def __init__(self, nc, name):
        self.nc, self.name, self.ctx, self.nums = nc, name, ExitStack(), []
        self.free = {kind: iter(numbers) for kind, numbers in SEMAPHORES.items()}

    def __enter__(self):
        return self

    def sem(self, name, kind="engine"):
        s = self.ctx.enter_context(self.nc.semaphore(f"{self.name}_{name}", next(self.free[kind])))
        self.nums.append(s.num)
        return s

    def sems(self, name, n, kind="engine"):
        return [self.sem(f"{name}{i}", kind) for i in range(n)]

    def row_dmas(self, n, each):
        return [RowDma(self.nc, j, each) for j in range(n)]

    def sb(self, name, shape, dt=F32):
        return self.ctx.enter_context(self.nc.sbuf_tensor(f"{self.name}_{name}", shape, dt))

    def ps(self, name, shape, dt=F32):
        return self.ctx.enter_context(self.nc.psum_tensor(f"{self.name}_{name}", shape, dt))

    def __exit__(self, kind, value, tb):
        if kind is None:
            lo, hi = min(self.nums), max(self.nums)
            self.nc.all_engine_barrier(sems_to_clear=range(lo, hi + 1))
            self.ctx.close()
        return False


class RowDma:

    values = {}

    def __init__(self, nc, j, each):
        self.sem = nc.row_dma[j]
        self.start = self.values.get(j, 0)
        self.values[j] = self.start + each

    def wait(self, eng, count):
        eng.wait_ge(self.sem, self.start + count)


class Chain:

    def __init__(self, eng, sem):
        self.eng, self.sem, self.n = eng, sem, 0

    def __call__(self, ins):
        self.n += 1
        ins.then_inc(self.sem, 1)
        self.eng.wait_ge(self.sem, self.n)


def load_constants(nc, k, x):
    with Phase(nc, "init") as ph:
        ld, dv, gp = ph.sems("ld", 2, "hardware"), ph.sem("dv"), ph.sem("gp")
        ii = ph.sb("ii", [P, SP_], I32)
        ei = ph.sb("ei", [P, NT, 9], I32)
        with nc.Block() as b:
            @b.sync
            def _(sp):
                sp.dma_start(k.x[:, 0:NT - 1, :], x[0:(NT - 1) * P, :].rearrange("(t p) d -> p t d", p=P)).then_inc(ld[0], 16)
                sp.wait_ge(dv, 1)
                sp.dma_start(k.x[0:LAST, NT - 1, :], x[(NT - 1) * P:N_NODES, :]).then_inc(ld[1], 16)
                sp.wait_ge(ld[0], 16)
                sp.wait_ge(ld[1], 16)

            @b.vector
            def _(v):
                v.memset(k.x[:, NT - 1, :], 0.0).then_inc(dv, 1)
                v.memset(k.ones[:, :], 1.0)
                v.memset(k.onerow[:, :], 1.0).then_inc(dv, 1)
                v.wait_ge(gp, 5)
                v.tensor_copy(k.iota[:, :], ii[:, 0:SP_]).then_inc(dv, 1)
                v.wait_ge(gp, 7)
                v.tensor_copy(k.expert[:, :, :], ei[:, :, :])
                v.tensor_copy(k.pnum[:, :], k.pnum_i[:, :]).then_inc(dv, 1)
                v.wait_ge(dv, 4)
                v.tensor_scalar(k.lastmask[:, :], k.pnum[:, :], float(LAST), None, ALU.is_lt).then_inc(dv, 1)
                v.wait_ge(dv, 5)
                v.tensor_scalar(k.onesmask[:, :], k.ones[:, :], k.lastmask[:, 0:1], None, ALU.mult).then_inc(dv, 1)

            @b.gpsimd
            def _(g):
                g.memset(k.ident[:, :], 0.0).then_inc(gp, 1)
                g.memset(k.before[:, :], 0.0).then_inc(gp, 1)
                g.wait_ge(gp, 2)
                g.affine_select(out=k.ident[:, :], in_=k.ident[:, :], compare_op=ALU.not_equal, fill=1.0,
                                base=0, pattern=[[-1, P]], channel_multiplier=1).then_inc(gp, 1)
                g.affine_select(out=k.before[:, :], in_=k.before[:, :], compare_op=ALU.is_ge, fill=1.0,
                                base=0, pattern=[[-1, P]], channel_multiplier=1).then_inc(gp, 1)
                g.iota(ii[:, :], pattern=[[1, SP_]], base=0, channel_multiplier=0).then_inc(gp, 1)
                g.wait_ge(gp, 5)
                g.iota(ei[:, :, :], pattern=[[0, NT], [1, 9]], base=0, channel_multiplier=0).then_inc(gp, 1)
                g.iota(k.pnum_i[:, :], pattern=[[0, 1]], base=0, channel_multiplier=1).then_inc(gp, 1)


def sort_edges(nc, name, k, key, val, weight, rec, lists, degree):
    gi, kl, wl, own = lists
    with Phase(nc, name) as ph:
        ld, dve, fill = ph.sems("ld", 3, "hardware"), ph.sem("dve"), ph.sem("fill", "hardware")
        cnt_ready, off_ready, dege = ph.sem("cnt"), ph.sem("off"), ph.sem("dege")
        staged, onehot, counted, placed = ph.sem("staged"), ph.sem("onehot"), ph.sem("counted"), ph.row_dmas(RING, 16 * (EC // RING))
        back, passed = ph.sem("back", "hardware"), ph.sem("passed")
        keyi, vali = ph.sb("keyi", [EP, EC], I32), ph.sb("vali", [EP, EC], I32)
        wt = ph.sb("wt", [EP, EC])
        hi_i, hi, lo = ph.sb("hi_i", [EP, EC], I32), ph.sb("hi", [EP, EC]), ph.sb("lo", [EP, EC])
        recs = ph.sb("recs", [EP, EC, REC], I32)
        oh, sc, tmp, pos = (ph.sb(n, [EP, EC]) for n in ("oh", "sc", "tmp", "pos"))
        pos_i, tgt = ph.sb("pos_i", [EP, EC], I32), ph.sb("tgt", [EP, EC], U32)
        cnt = ph.sb("cnt", [EP, NT])
        offb, nt_i, nt, endt, start = ph.sb("offb", [P, NT]), ph.sb("nt_i", [P, NT], I32), ph.sb("nt", [P, NT]), ph.sb("endt", [P, NT]), ph.sb("start", [P, NT])
        ow = ph.sb("ow", [1, SP_])
        empty = ph.sb("empty", [P, ST, REC], I32)
        tstage, rstage = ph.sb("tstage", [EP, RING], U32), ph.sb("rstage", [EP, RING, REC], I32)
        ohlo, ohhi, zero = ph.sb("ohlo", [EP, RING, P], BF16), ph.sb("ohhi", [EP, RING, NT], BF16), ph.sb("zero", [EP, P], BF16)
        pt = ph.ps("pt", [P, 2, 512])
        pdeg = ph.ps("pdeg", [P, 512])
        iters = EC // RING
        with nc.Block() as b:
            @b.sync
            def _(sp):
                sp.dma_start(keyi[:, :], key).then_inc(ld[0], 16)
                sp.dma_start(vali[:, :], val).then_inc(ld[1], 16)
                sp.dma_start(wt[:, :], weight).then_inc(ld[2], 16)
                sp.wait_ge(dve, 4)
                sp.dma_start(rec.rearrange("(p t) w -> p (t w)", p=P), empty[:, :, :].rearrange("p t w -> p (t w)")).then_inc(fill, 16)
                for q in placed:
                    q.wait(sp, 16 * iters)
                sp.dma_start(empty[:, :, :].rearrange("p t w -> p (t w)"), rec.rearrange("(p t) w -> p (t w)", p=P)).then_inc(back, 16)
                sp.wait_ge(back, 16)

            @b.vector
            def _(v):
                c = Chain(v, dve)
                c(v.memset(empty[:, :, :].rearrange("p t w -> p (t w)"), 0))
                c(v.memset(empty[:, :, 1].bitcast(F32), -1.0))
                c(v.memset(zero[:, :], 0.0))
                c(v.memset(pos[:, :], 0.0))
                c(v.memset(recs[:, :, 3], 0))
                for s in ld:
                    v.wait_ge(s, 16)
                c(v.tensor_scalar(hi_i[:, :], keyi[:, :], 7, None, ALU.arith_shift_right))
                c(v.tensor_copy(hi[:, :], hi_i[:, :]))
                c(v.tensor_scalar(hi_i[:, :], keyi[:, :], P - 1, None, ALU.bitwise_and))
                c(v.tensor_copy(lo[:, :], hi_i[:, :]))
                c(v.tensor_copy(recs[:, :, 0], vali[:, :]))
                c(v.tensor_copy(recs[:, :, 1].bitcast(F32), lo[:, :]))
                c(v.tensor_copy(recs[:, :, 2].bitcast(F32), wt[:, :]))
                with v.Fori(0, NT) as t:
                    v.wait_ge(cnt_ready, t)
                    v.tensor_scalar(oh[:, :], hi[:, :], k.iota[0:EP, ds(t, 1)], None, ALU.is_equal, ALU.add,
                                    accum_out=cnt[:, ds(t, 1)]).then_inc(cnt_ready, 1)
                v.wait_ge(off_ready, 1)
                c(v.tensor_copy(nt[:, :], pt[:, 1, 0:NT]))
                c(v.tensor_scalar(nt[:, :], nt[:, :], float(P - 1), None, ALU.add))
                c(v.tensor_copy(nt_i[:, :], nt[:, :]))
                c(v.tensor_scalar(nt_i[:, :], nt_i[:, :], 7, None, ALU.arith_shift_right))
                c(v.tensor_copy(nt[:, :], nt_i[:, :]))
                c(v.tensor_tensor_scan(endt[:, :], k.ones[:, 0:NT], nt[:, :], 0.0, ALU.mult, ALU.add))
                c(v.tensor_tensor(start[:, :], endt[:, :], nt[:, :], ALU.subtract))
                c(v.tensor_scalar(offb[:, :], start[:, :], float(P), -1.0, ALU.mult, ALU.add))
                c(v.tensor_tensor(offb[:, :], offb[:, :], pt[:, 0, 0:NT], ALU.add))
                c(v.memset(ow[:, :], -1.0))
                n = c.n
                with v.Fori(0, NT) as t:
                    v.wait_ge(dve, n + 4 * t)
                    v.tensor_scalar(oh[:, :], hi[:, :], k.iota[0:EP, ds(t, 1)], None, ALU.is_equal).then_inc(dve, 1)
                    v.wait_ge(dve, n + 4 * t + 1)
                    v.tensor_tensor_scan(sc[:, :], k.onerow[0:EP, 0:EC], oh[:, :], 0.0, ALU.mult, ALU.add).then_inc(dve, 1)
                    v.scalar_tensor_tensor(ow[:, :], k.iota[0:1, :], start[0:1, ds(t, 1)], ow[:, :], ALU.is_ge, ALU.add).then_inc(dve, 1)
                    v.wait_ge(dve, n + 4 * t + 3)
                    v.scalar_tensor_tensor(tmp[:, :], sc[:, :], offb[0:EP, ds(t, 1)], oh[:, :], ALU.add, ALU.mult).then_inc(onehot, 1)
                    v.wait_ge(onehot, t + 1)
                    v.tensor_tensor(pos[:, :], pos[:, :], tmp[:, :], ALU.add).then_inc(dve, 1)
                c.n = n + 4 * NT
                v.wait_ge(dve, c.n)
                c(v.tensor_copy(own[:, :], ow[:, :]))
                c(v.tensor_copy(pos_i[:, :], pos[:, :]))
                c(v.tensor_scalar(hi_i[:, :], pos_i[:, :], P - 1, None, ALU.bitwise_and))
                c(v.tensor_scalar(pos_i[:, :], pos_i[:, :], 7, None, ALU.arith_shift_right))
                c(v.tensor_copy(sc[:, :], hi_i[:, :]))
                c(v.tensor_copy(tmp[:, :], pos_i[:, :]))
                c(v.scalar_tensor_tensor(pos[:, :], sc[:, :], float(ST), tmp[:, :], ALU.mult, ALU.add))
                c(v.tensor_copy(tgt[:, :], pos[:, :]))
                with v.Fori(0, iters) as i:
                    for h in range(2):
                        for j in range(h * HALF, h * HALF + HALF):
                            placed[j].wait(v, 16 * i)
                        v.tensor_copy(tstage[:, h * HALF:(h + 1) * HALF], tgt[:, ds(i * RING + h * HALF, HALF)])
                        v.tensor_copy(rstage[:, h * HALF:(h + 1) * HALF, :], recs[:, ds(i * RING + h * HALF, HALF), :]).then_inc(staged, 1)
                    v.wait_ge(counted, i)
                    for j in range(RING):
                        v.tensor_scalar(ohlo[:, j, :], k.iota[0:EP, 0:P], lo[:, ds(i * RING + j, 1)], None, ALU.is_equal)
                        v.tensor_scalar(ohhi[:, j, :], k.iota[0:EP, 0:NT], hi[:, ds(i * RING + j, 1)], None, ALU.is_equal).then_inc(dege, 1)
                v.wait_ge(counted, iters + 1)
                c(v.tensor_copy(degree[:, :], pdeg[:, 0:NT]))
                v.wait_ge(back, 16)
                c(v.memset(gi[:, ST:SP_], 0))
                c(v.memset(kl[:, ST:SP_], -1.0))
                c(v.tensor_copy(gi[:, 0:ST], empty[:, :, 0]))
                c(v.tensor_copy(kl[:, 0:ST], empty[:, :, 1].bitcast(F32)))
                if wl is not None:
                    c(v.memset(wl[:, ST:SP_], 0.0))
                    c(v.tensor_copy(wl[:, 0:ST], empty[:, :, 2].bitcast(F32)))

            @b.tensor
            def _(pe):
                pe.wait_ge(cnt_ready, NT)
                pe.matmul(pt[0:P, 0, 0:NT], k.before[0:EP, :], cnt[:, :], start=True, stop=True)
                pe.matmul(pt[0:P, 1, 0:NT], k.ones[0:EP, :], cnt[:, :], start=True, stop=True).then_inc(off_ready, 1)
                pe.matmul(pdeg[:, 0:NT], zero[:, :], zero[:, 0:NT], start=True, stop=False)
                with pe.Fori(0, iters) as i:
                    for j in range(RING):
                        pe.wait_ge(dege, i * RING + j + 1)
                        mm = pe.matmul(pdeg[:, 0:NT], ohlo[:, j, :], ohhi[:, j, :], start=False, stop=False)
                    mm.then_inc(counted, 1)
                pe.matmul(pdeg[:, 0:NT], zero[:, :], zero[:, 0:NT], start=False, stop=True).then_inc(counted, 1)

            @b.gpsimd
            def _(g):
                g.wait_ge(fill, 16)
                with g.Fori(0, iters) as i:
                    for j in range(RING):
                        if j % HALF == 0:
                            g.wait_ge(staged, 2 * i + j // HALF + 1)
                            g.sem_inc(passed, 1)
                        g.indirect_dma_start(rec, bass.IndirectOffsetOnAxis(ap=tstage[:, j:j + 1], axis=0),
                                             rstage[:, j, :], None).then_inc(placed[j].sem, 16)


def normalise(nc, name, k, scale=None, table=None, keep=False, dest=None, eps=1e-5):
    with Phase(nc, name) as ph:
        dve, root, ready = ph.sem("dve"), ph.sem("root"), ph.sem("ready")
        tdone, evac, stored = ph.sems("tdone", G), ph.sems("evac", G), ph.sems("stored", G, "hardware")
        st = ph.sb("st", [P, NT, 6])
        mean, var, dif, rstd = (ph.sb(n, [P, NT]) for n in ("mean", "var", "dif", "rstd"))
        stage = ph.sb("stage", [P, G, D])
        pt = ph.ps("pt", [P, G, 512])
        with nc.Block() as b:
            @b.vector
            def _(v):
                with v.Fori(0, NT) as t:
                    v.bn_stats(st[:, ds(t, 1), :], k.x[:, ds(t, 1), :]).then_inc(dve, 1)
                v.wait_ge(dve, NT)
                c = Chain(v, dve)
                c.n = NT
                c(v.tensor_tensor(mean[:, :], st[:, :, 1], st[:, :, 4], ALU.add))
                c(v.tensor_scalar(mean[:, :], mean[:, :], 0.5, None, ALU.mult))
                c(v.tensor_tensor(dif[:, :], st[:, :, 1], st[:, :, 4], ALU.subtract))
                c(v.tensor_tensor(dif[:, :], dif[:, :], dif[:, :], ALU.mult))
                c(v.tensor_scalar(dif[:, :], dif[:, :], 0.25, eps, ALU.mult, ALU.add))
                c(v.tensor_tensor(var[:, :], st[:, :, 2], st[:, :, 5], ALU.add))
                c(v.scalar_tensor_tensor(var[:, :], var[:, :], 1.0 / D, dif[:, :], ALU.mult, ALU.add))
                v.wait_ge(root, 1)
                c(v.reciprocal(rstd[:, :], rstd[:, :]))
                if scale is not None:
                    c(v.tensor_tensor(rstd[:, :], rstd[:, :], scale[:, :], ALU.mult))
                with v.Fori(0, NG) as i:
                    for j in range(G):
                        t = i * G + j
                        if dest is not None:
                            v.wait_ge(tdone[j], i)
                        if table is not None:
                            v.wait_ge(stored[j], 16 * i)
                        if dest is not None or table is not None:
                            v.tensor_scalar(stage[:, j, :], k.x[:, ds(t, 1), :].rearrange("p a d -> p (a d)"), mean[:, ds(t, 1)], rstd[:, ds(t, 1)],
                                            ALU.subtract, ALU.mult).then_inc(ready, 1)
                        if keep:
                            v.tensor_scalar(k.y[:, ds(t, 1), :].rearrange("p a d -> p (a d)"), k.x[:, ds(t, 1), :].rearrange("p a d -> p (a d)"), mean[:, ds(t, 1)], rstd[:, ds(t, 1)],
                                            ALU.subtract, ALU.mult)

            @b.scalar
            def _(a):
                a.wait_ge(dve, NT + 7)
                a.activation(rstd[:, :], var[:, :], ACT.Sqrt).then_inc(root, 1)
                if dest is not None:
                    with a.Fori(0, NG) as i:
                        for j in range(G):
                            a.wait_ge(tdone[j], i + 1)
                            a.copy(dest[:, :, ds((i * G + j) * P, P)], pt[:, j, 0:D].rearrange("p (k n) -> p k n", k=KD)).then_inc(evac[j], 1)

            if dest is not None:
                @b.tensor
                def _(pe):
                    with pe.Fori(0, NG) as i:
                        for j in range(G):
                            pe.wait_ge(ready, i * G + j + 1)
                            pe.wait_ge(evac[j], i)
                            for q in range(KD):
                                mm = pe.transpose(pt[:, j, q * P:(q + 1) * P], stage[:, j, q * P:(q + 1) * P], k.ident[:, :])
                            mm.then_inc(tdone[j], 1)

            if table is not None:
                @b.sync
                def _(sp):
                    with sp.Fori(0, NG) as i:
                        for j in range(G):
                            sp.wait_ge(ready, i * G + j + 1)
                            sp.dma_start(table[ds((i * G + j) * P, P), 0:D], stage[:, j, :]).then_inc(stored[j], 16)
                    for s in stored:
                        sp.wait_ge(s, 16 * NG)


def aggregate(nc, name, k, lists, table, acc, clear):
    gi, kl, wl, own = lists
    iters = ST // RING
    with Phase(nc, name) as ph:
        staged, landed, passed = ph.sem("staged"), ph.row_dmas(RING, 16 * iters), ph.sem("passed")
        oh_ready, summed, added = ph.sem("oh"), ph.sem("summed"), ph.sem("added")
        ix = ph.sb("ix", [P, RING], U32)
        rows, oh = ph.sb("rows", [P, RING, D]), ph.sb("oh", [P, RING, P])
        NB = 4
        pa = ph.ps("pa", [P, NB, 512])
        with nc.Block() as b:
            @b.gpsimd
            def _(g):
                with g.Fori(0, iters) as i:
                    for j in range(RING):
                        if j % HALF == 0:
                            g.wait_ge(staged, 2 * i + j // HALF + 1)
                            g.sem_inc(passed, 1)
                        g.indirect_dma_start(rows[:, j, :], None, table,
                                             bass.IndirectOffsetOnAxis(ap=ix[:, j:j + 1], axis=0)).then_inc(landed[j].sem, 16)

            def one_hots(v, first, h):
                for j in range(h * HALF, (h + 1) * HALF):
                    col = first + j
                    if wl is None:
                        ins = v.tensor_scalar(oh[:, j, :], k.iota[:, 0:P], kl[:, ds(col, 1)], None, ALU.is_equal)
                    else:
                        ins = v.tensor_scalar(oh[:, j, :], k.iota[:, 0:P], kl[:, ds(col, 1)], wl[:, ds(col, 1)],
                                              ALU.is_equal, ALU.mult)
                    ins.then_inc(oh_ready, 1)

            @b.vector
            def _(v):
                if clear:
                    v.memset(acc[:, :, :].rearrange("p k n -> p (k n)"), 0.0).then_inc(added, NB)
                else:
                    v.sem_inc(added, NB)
                v.tensor_copy(ix[:, 0:HALF], gi[:, 0:HALF]).then_inc(staged, 1)
                v.tensor_copy(ix[:, HALF:RING], gi[:, HALF:RING]).then_inc(staged, 1)
                one_hots(v, 0, 0)
                with v.Fori(0, iters) as i:
                    for h in range(2):
                        one_hots(v, i * RING + (RING if h else 0), 1 - h)
                        for j in range(h * HALF, (h + 1) * HALF):
                            tile = v.value_load(own[0:1, ds(i * RING + j, 1)], min_val=0, max_val=NT - 1)
                            v.wait_ge(summed, i * RING + j + 1)
                            v.wait_ge(added, i * RING + j + NB)
                            v.tensor_tensor(acc[:, :, ts(tile, P)], acc[:, :, ts(tile, P)],
                                            pa[:, j % NB, 0:D].rearrange("p (k n) -> p k n", k=KD), ALU.add).then_inc(added, 1)
                        v.tensor_copy(ix[:, h * HALF:(h + 1) * HALF], gi[:, ds(i * RING + RING + h * HALF, HALF)]).then_inc(staged, 1)

            @b.tensor
            def _(pe):
                with pe.Fori(0, iters) as i:
                    for j in range(RING):
                        landed[j].wait(pe, 16 * i + 16)
                        pe.wait_ge(oh_ready, i * RING + j + 1)
                        pe.wait_ge(added, i * RING + j + 1)
                        for q in range(KD):
                            mm = pe.matmul(pa[:, j % NB, q * P:(q + 1) * P], rows[:, j, q * P:(q + 1) * P], oh[:, j, :],
                                           start=True, stop=True)
                        mm.then_inc(summed, 1)


def transform(nc, name, k, acc, w, mode, bias=None, table=None, heads=None):
    with Phase(nc, name) as ph:
        ld, inn, mul, fin, passed = ph.sems("ld", 2, "hardware"), ph.sems("inn", G), ph.sems("mul", G), ph.sem("fin"), ph.sem("passed")
        free, ready = ph.sems("free", G), ph.sem("ready")
        tdone, evac, stored = ph.sems("tdone", G), ph.sem("evac"), ph.sems("stored", G, "hardware")
        wsb = ph.sb("w", [P, KD, D])
        ast = ph.sb("ast", [P, G, KD, P])
        tmp, out = ph.sb("tmp", [P, G, D]), ph.sb("out", [P, G, D])
        bb = ph.sb("bb", [P, D])
        head = ph.sb("head", [P, 2, D]) if mode == "gat" else None
        pz = ph.ps("pz", [P, G, 512])

        def slot(j):
            return pz[:, j, D:2 * D]

        def row(buf, t):
            return buf[:, ds(t, 1), :].rearrange("p a d -> p (a d)")

        with nc.Block() as b:
            @b.sync
            def _(sp):
                sp.dma_start(wsb[:, :, :], w.rearrange("(k p) n -> p k n", p=P)).then_inc(ld[0], 16)
                if bias is not None:
                    sp.dma_start(bb[:, :], bias.partition_broadcast(P)).then_inc(ld[1], 16)
                if mode == "gat":
                    for q in range(2):
                        sp.dma_start(head[:, q, :], heads[q].rearrange("h f -> (h f)").partition_broadcast(P)).then_inc(ld[1], 16)
                if mode in ("next", "rows", "gat"):
                    with sp.Fori(0, NG) as i:
                        for j in range(G):
                            sp.wait_ge(ready, i * G + j + 1)
                            sp.dma_start(table[ds((i * G + j) * P, P), :], out[:, j, :]).then_inc(stored[j], 16)
                    for s in stored:
                        sp.wait_ge(s, 16 * NG)

            @b.scalar
            def _(a):
                with a.Fori(0, NG) as i:
                    for j in range(G):
                        a.wait_ge(mul[j], i)
                        a.copy(ast[:, j, :, :], acc[:, :, ds((i * G + j) * P, P)]).then_inc(inn[j], 1)
                    if mode == "next":
                        for j in range(G):
                            a.wait_ge(tdone[j], i + 1)
                            a.sem_inc(passed, 1)
                            a.copy(acc[:, :, ds((i * G + j) * P, P)], slot(j).rearrange("p (k n) -> p k n", k=KD)).then_inc(evac, 1)

            @b.tensor
            def _(pe):
                pe.wait_ge(ld[0], 16)
                with pe.Fori(0, NG) as i:
                    if mode == "next":
                        pe.wait_ge(evac, i * G)
                    for j in range(G):
                        pe.wait_ge(inn[j], i + 1)
                        pe.wait_ge(free[j], i)
                        for q in range(KD):
                            mm = pe.matmul(pz[:, j, 0:D], ast[:, j, q, :], wsb[:, q, :], start=q == 0, stop=q == KD - 1)
                        mm.then_inc(mul[j], 1)
                    if mode == "next":
                        for j in range(G):
                            pe.wait_ge(ready, i * G + j + 1)
                            for q in range(KD):
                                mm = pe.transpose(slot(j)[:, q * P:(q + 1) * P], out[:, j, q * P:(q + 1) * P], k.ident[:, :])
                            mm.then_inc(tdone[j], 1)

            @b.vector
            def _(v):
                if bias is not None:
                    v.wait_ge(ld[1], 16)
                if mode == "gat":
                    v.wait_ge(ld[1], 32)
                with v.Fori(0, NG) as i:
                    for j in range(G):
                        t = i * G + j
                        v.wait_ge(mul[j], i + 1)
                        if mode == "add":
                            v.tensor_tensor(row(k.x, t), row(k.x, t), pz[:, j, 0:D], ALU.add).then_inc(free[j], 1)
                            continue
                        if mode == "rows":
                            stored_j = stored[j]
                            v.wait_ge(stored_j, 16 * i)
                            v.tensor_copy(out[:, j, :], pz[:, j, 0:D]).then_inc(ready, 1)
                            v.wait_ge(ready, t + 1)
                            v.sem_inc(free[j], 1)
                            continue
                        if mode == "gat":
                            v.wait_ge(stored[j], 16 * i)
                            v.tensor_copy(out[:, j, :], pz[:, j, 0:D]).then_inc(ready, 1)
                            for q in range(2):
                                v.tensor_tensor(tmp[:, j, :], pz[:, j, 0:D], head[:, q, :], ALU.mult).then_inc(fin, 1)
                                v.wait_ge(fin, t * 4 + q * 2 + 1)
                                ins = v.tensor_reduce(k.score[:, ds(t, 1), q, :].rearrange("p a h -> p (a h)"), tmp[:, j, :].rearrange("p (h f) -> p h f", h=HEADS), AX_X, ALU.add)
                                ins.then_inc(fin, 1)
                                v.wait_ge(fin, t * 4 + q * 2 + 2)
                            v.sem_inc(free[j], 1)
                            continue
                        if mode == "keep":
                            v.scalar_tensor_tensor(row(k.y, t), pz[:, j, 0:D], k.dinv[:, ds(t, 1)], bb[:, :],
                                                   ALU.mult, ALU.add).then_inc(free[j], 1)
                            continue
                        v.scalar_tensor_tensor(tmp[:, j, :], pz[:, j, 0:D], k.dinv[:, ds(t, 1)], bb[:, :],
                                               ALU.mult, ALU.add).then_inc(free[j], 1)
                        v.wait_ge(free[j], i + 1)
                        if mode == "next":
                            v.wait_ge(tdone[j], i)
                            v.wait_ge(stored[j], 16 * i)
                            v.tensor_scalar(out[:, j, :], tmp[:, j, :], 0.0, k.dinv[:, ds(t, 1)], ALU.max, ALU.mult).then_inc(ready, 1)
                        else:
                            v.scalar_tensor_tensor(row(k.x, t), tmp[:, j, :], 0.0, row(k.x, t), ALU.max, ALU.add).then_inc(ready, 1)


BLOCK = 2 * P


def spread(ap, n):
    return ap.unsqueeze(2).broadcast_to([ap.shape[0], ap.shape[1], n])


def block_count(pairs, experts):
    n = (pairs + experts * (BLOCK - 1)) // BLOCK
    return n + n % 2


def logits(nc, name, k, hidden, w, bias, E, lg, act=None, w_in=None, b_in=None):
    C = NP // NG
    H = C // 2
    FT = hidden // P
    MB = min(4, 2 * FT)
    with Phase(nc, name) as ph:
        ld = ph.sem("ld", "hardware")
        mid, mid_act = ph.sem("mid"), ph.sem("mid_act")
        passed = ph.sem("passed")
        mul, evac, tr, put = ph.sem("mul"), ph.sem("evac"), ph.sem("tr"), ph.sem("put")
        wsb, bsb = ph.sb("w", [P, FT, E]), ph.sb("b", [E, 1])
        lst = ph.sb("lst", [E, C])
        pl, pt = ph.ps("pl", [P, 2, 512]), ph.ps("pt", [P, 512])
        if w_in is not None:
            win, bin_ = ph.sb("win", [P, KD, hidden]), ph.sb("bin", [P, FT])
            hs = ph.sb("hs", [P, 2, FT, H])
            pm = ph.ps("pm", [P, 4, 512])
        n_ld = 1 + (bias is not None) + 2 * (w_in is not None)
        with nc.Block() as b:
            @b.sync
            def _(sp):
                sp.dma_start(wsb[:, :, :], w.rearrange("(f p) e -> p f e", p=P)).then_inc(ld, 16)
                if bias is not None:
                    sp.dma_start(bsb[:, :], bias.rearrange("(e a) -> e a", a=1)).then_inc(ld, 16)
                if w_in is not None:
                    sp.dma_start(win[:, :, :], w_in.rearrange("(k p) f -> p k f", p=P)).then_inc(ld, 16)
                    sp.dma_start(bin_[:, :], b_in).then_inc(ld, 16)

            @b.tensor
            def _(pe):
                pe.wait_ge(ld, 16 * n_ld)
                with pe.Fori(0, NG) as i:
                    for h in range(2):
                        if w_in is not None:
                            for f in range(FT):
                                pe.wait_ge(mid_act, (2 * i + h) * FT + f + 1)
                                for q in range(KD):
                                    mm = pe.matmul(pm[:, (h * FT + f) % MB, 0:H], win[:, q, f * P:(f + 1) * P], k.t[:, q, ds(i * C + h * H, H)],
                                                   start=q == 0, stop=q == KD - 1)
                                mm.then_inc(mid, 1)
                    pe.wait_ge(put, i)
                    for h in range(2):
                        if w_in is not None:
                            pe.wait_ge(mid_act, (2 * i + h + 1) * FT + MB)
                        for f in range(FT):
                            src = k.t[:, f, ds(i * C + h * H, H)] if w_in is None else hs[:, h, f, :]
                            mm = pe.matmul(pl[0:E, h, 0:H], wsb[:, f, :], src, start=f == 0, stop=f == FT - 1)
                    mm.then_inc(mul, 1)
                    pe.wait_ge(evac, i + 1)
                    pe.sem_inc(passed, 1)
                    for j in range(G):
                        mm = pe.transpose(pt[:, j * E:(j + 1) * E], lst[:, j * P:(j + 1) * P], k.ident[0:E, 0:E])
                    mm.then_inc(tr, 1)

            @b.scalar
            def _(a):
                a.sem_inc(mid_act, MB)
                a.wait_ge(ld, 16 * n_ld)
                with a.Fori(0, NG) as i:
                    if w_in is not None:
                        for h in range(2):
                            for f in range(FT):
                                a.wait_ge(mid, (2 * i + h) * FT + f + 1)
                                a.activation(hs[:, h, f, :], pm[:, (h * FT + f) % MB, 0:H], act, bias=bin_[:, f:f + 1]).then_inc(mid_act, 1)
                    a.wait_ge(mul, i + 1)
                    dst = lst[:, :].rearrange("e (h n) -> e h n", h=2)
                    if bias is not None:
                        a.activation(dst, pl[0:E, :, 0:H], ACT.Identity, bias=bsb[:, 0:1]).then_inc(evac, 1)
                    else:
                        a.copy(dst, pl[0:E, :, 0:H]).then_inc(evac, 1)

            @b.vector
            def _(v):
                with v.Fori(0, NG) as i:
                    v.wait_ge(tr, i + 1)
                    v.tensor_copy(lg[:, ds(i * G, G), :], pt[:, 0:G * E].rearrange("p (t e) -> p t e", e=E)).then_inc(put, 1)


def softmax_steps(c, v, k, lg, E, mx, sm, act_in, act_out):
    c(v.tensor_reduce(mx[:, :], lg[:, :, :], AX_X, ALU.max))
    c(v.tensor_tensor(lg[:, :, :], lg[:, :, :], spread(mx[:, :], E), ALU.subtract))
    v.sem_inc(act_in, 1)
    v.wait_ge(act_out, 1)
    c(v.tensor_reduce(sm[:, :], lg[:, :, :], AX_X, ALU.add))
    c(v.reciprocal(sm[:, :], sm[:, :]))
    c(v.tensor_tensor(lg[:, :, :], lg[:, :, :], spread(sm[:, :], E), ALU.mult))


def pick(c, v, k, pr, E, mx, cand, oh):
    c(v.tensor_reduce(mx[:, :], pr[:, :, :], AX_X, ALU.max))
    c(v.tensor_tensor(cand[:, :, :], pr[:, :, :], spread(mx[:, :], E), ALU.is_equal))
    c(v.scalar_tensor_tensor(cand[:, :, :], cand[:, :, :], -1000.0, k.expert[:, :, 0:E], ALU.mult, ALU.add))
    c(v.tensor_reduce(k.small[:, :], cand[:, :, :], AX_X, ALU.min))
    c(v.tensor_tensor(oh, cand[:, :, :], spread(k.small[:, :], E), ALU.is_equal))


def route(nc, name, k, lg, E, kind, xbuf, nblocks, ybuf_rows=None):
    C = {"capacity": 1, "top1": 1, "shared": 3, "soft2": 2}[kind]
    EE = E + (kind == "shared")
    N = C * NT
    top = EE * CAP_ROWS if kind == "capacity" else nblocks * BLOCK
    with Phase(nc, name) as ph:
        dve, a_in, a_out, cnt, off = ph.sem("dve"), ph.sem("a_in"), ph.sem("a_out"), ph.sem("cnt"), ph.sem("off")
        ready, staged, free, zeroed, zfill, passed = ph.sem("ready"), ph.sem("staged"), ph.row_dmas(G, 16 * C * NG), ph.sem("zeroed"), ph.sem("zfill", "hardware"), ph.sem("passed")
        mx, sm, m2 = ph.sb("mx", [P, NT]), ph.sb("sm", [P, NT]), ph.sb("m2", [P, NT])
        cand = ph.sb("cand", [P, NT, E])
        oh = ph.sb("oh", [P, N, EE])
        before, tot, incl = (ph.sb(n, [P, N, EE]) for n in ("before", "tot", "incl"))
        nb_i, nb, endb, startb = ph.sb("nb_i", [P, EE], I32), ph.sb("nb", [P, EE]), ph.sb("endb", [P, EE]), ph.sb("startb", [P, EE])
        pos, base, kept, tgt = ph.sb("pos", [P, N]), ph.sb("base", [P, N]), ph.sb("kept", [P, N]), ph.sb("tgt", [P, N])
        tgt_u = ph.sb("tgt_u", [P, N], U32)
        trash = ph.sb("trash", [P, N])
        ow = ph.sb("ow", [1, MAX_BLOCKS])
        zero = ph.sb("zero", [P, 2048])
        rows, ix = ph.sb("rows", [P, G, D]), ph.sb("ix", [P, C, G], U32)
        pp = ph.ps("pp", [P, 2 * C, 512])
        probs = lg
        with nc.Block() as b:
            @b.vector
            def _(v):
                c = Chain(v, dve)
                v.memset(zero[:, :], 0.0).then_inc(zeroed, 1)
                softmax_steps(c, v, k, lg, E, mx, sm, a_in, a_out)
                v1 = oh[:, 0:NT, 0:E]
                if kind == "shared":
                    c(v.memset(oh[:, :, :].rearrange("p n e -> p (n e)"), 0.0))
                    c(v.memset(oh[:, 2 * NT:3 * NT, E], 1.0))
                pick(c, v, k, probs, E, mx, cand, v1)
                if kind in ("capacity", "top1"):
                    c(v.tensor_copy(k.coef[:, 0:NT], mx[:, :]))
                else:
                    v2 = oh[:, NT:2 * NT, 0:E]
                    c(v.scalar_tensor_tensor(probs[:, :, :], v1, -4.0, probs[:, :, :], ALU.mult, ALU.add))
                    pick(c, v, k, probs, E, m2, cand, v2)
                    if kind == "shared":
                        c(v.tensor_tensor(sm[:, :], mx[:, :], m2[:, :], ALU.add))
                        c(v.reciprocal(sm[:, :], sm[:, :]))
                        c(v.tensor_tensor(k.coef[:, 0:NT], mx[:, :], sm[:, :], ALU.mult))
                        c(v.tensor_tensor(k.coef[:, NT:2 * NT], m2[:, :], sm[:, :], ALU.mult))
                        c(v.memset(k.coef[:, 2 * NT:3 * NT], 1.0))
                    else:
                        c(v.tensor_tensor(k.coef[:, NT:2 * NT], m2[:, :], mx[:, :], ALU.subtract))
                        v.sem_inc(a_in, 1)
                        v.wait_ge(a_out, 2)
                        c(v.tensor_scalar(sm[:, :], k.coef[:, NT:2 * NT], 1.0, None, ALU.add))
                        c(v.reciprocal(sm[:, :], sm[:, :]))
                        c(v.tensor_copy(k.coef[:, 0:NT], sm[:, :]))
                        c(v.tensor_tensor(k.coef[:, NT:2 * NT], k.coef[:, NT:2 * NT], sm[:, :], ALU.mult))
                for q in range(C):
                    last = oh[:, (q + 1) * NT - 1, :]
                    c(v.tensor_scalar(last, last, k.lastmask[:, 0:1], None, ALU.mult))
                v.sem_inc(cnt, 1)
                v.wait_ge(off, 1)
                for q in range(C):
                    s = slice(q * NT, (q + 1) * NT)
                    c(v.tensor_copy(before[:, s, :], pp[:, 2 * q, 0:NT * EE].rearrange("p (t e) -> p t e", e=EE)))
                    c(v.tensor_copy(tot[:, s, :], pp[:, 2 * q + 1, 0:NT * EE].rearrange("p (t e) -> p t e", e=EE)))
                for e in range(EE):
                    c(v.tensor_tensor_scan(incl[:, :, e], k.onerow[:, 0:N], tot[:, :, e], 0.0, ALU.mult, ALU.add))
                if kind == "capacity":
                    c(v.tensor_scalar(startb[:, :], k.expert[:, 0, 0:EE], float(CAP_ROWS), None, ALU.mult))
                    c(v.memset(ow[:, :], 0.0))
                    for e in range(EE):
                        c(v.memset(ow[:, e * (CAP_ROWS // BLOCK):(e + 1) * (CAP_ROWS // BLOCK)], float(e)))
                else:
                    c(v.tensor_scalar(nb[:, :], incl[:, N - 1, :], float(BLOCK - 1), None, ALU.add))
                    c(v.tensor_copy(nb_i[:, :], nb[:, :]))
                    c(v.tensor_scalar(nb_i[:, :], nb_i[:, :], 8, None, ALU.arith_shift_right))
                    c(v.tensor_copy(nb[:, :], nb_i[:, :]))
                    c(v.tensor_tensor_scan(endb[:, :], k.ones[:, 0:EE], nb[:, :], 0.0, ALU.mult, ALU.add))
                    c(v.tensor_tensor(startb[:, :], endb[:, :], nb[:, :], ALU.subtract))
                    c(v.memset(ow[:, :], -1.0))
                    for e in range(EE):
                        c(v.scalar_tensor_tensor(ow[:, :], k.iota[0:1, 0:MAX_BLOCKS], startb[0:1, e:e + 1], ow[:, :], ALU.is_ge, ALU.add))
                    c(v.tensor_scalar(startb[:, :], startb[:, :], float(BLOCK), None, ALU.mult))
                c(v.tensor_copy(k.block_expert[:, :], ow[:, 0:MAX_BLOCKS]))
                c(v.tensor_tensor(before[:, :, :], before[:, :, :], incl[:, :, :], ALU.add))
                c(v.tensor_tensor(before[:, :, :], before[:, :, :], tot[:, :, :], ALU.subtract))
                c(v.tensor_tensor(before[:, :, :], before[:, :, :], oh[:, :, :], ALU.mult))
                c(v.tensor_reduce(pos[:, :], before[:, :, :], AX_X, ALU.add))
                for e in range(EE):
                    c(v.tensor_scalar(incl[:, :, e], oh[:, :, e], startb[:, e:e + 1], None, ALU.mult))
                c(v.tensor_reduce(base[:, :], incl[:, :, :], AX_X, ALU.add))
                c(v.tensor_reduce(kept[:, :], oh[:, :, :], AX_X, ALU.add))
                c(v.tensor_scalar(trash[:, :], k.iota[:, 0:N], float(P), k.pnum[:, 0:1], ALU.mult, ALU.add))
                c(v.tensor_scalar(trash[:, :], trash[:, :], float(top), None, ALU.add))
                if kind == "capacity":
                    c(v.tensor_scalar(tgt[:, :], pos[:, :], float(CAP), None, ALU.is_lt))
                    c(v.tensor_tensor(kept[:, :], kept[:, :], tgt[:, :], ALU.mult))
                c(v.tensor_tensor(k.coef[:, 0:N], k.coef[:, 0:N], kept[:, :], ALU.mult))
                c(v.tensor_tensor(pos[:, :], pos[:, :], base[:, :], ALU.add))
                c(v.tensor_tensor(tgt[:, :], pos[:, :], kept[:, :], ALU.mult))
                c(v.tensor_copy(k.back[:, 0:N], tgt[:, :]))
                c(v.tensor_tensor(pos[:, :], pos[:, :], trash[:, :], ALU.subtract))
                c(v.tensor_tensor(pos[:, :], pos[:, :], kept[:, :], ALU.mult))
                c(v.tensor_tensor(pos[:, :], pos[:, :], trash[:, :], ALU.add))
                c(v.tensor_copy(tgt_u[:, :], pos[:, :]))
                with v.Fori(0, NG) as i:
                    for j in range(G):
                        free[j].wait(v, i * 16 * C)
                        v.tensor_copy(rows[:, j, :], k.y[:, ds(i * G + j, 1), :].rearrange("p a d -> p (a d)")).then_inc(ready, 1)
                    for q in range(C):
                        ins = v.tensor_copy(ix[:, q, :], tgt_u[:, ds(i * G + q * NT, G)])
                        ins.then_inc(ready, 1)

            @b.scalar
            def _(a):
                a.wait_ge(a_in, 1)
                a.activation(lg[:, :, :], lg[:, :, :], ACT.Exp).then_inc(a_out, 1)
                if kind == "soft2":
                    a.wait_ge(a_in, 2)
                    a.activation(k.coef[:, NT:2 * NT], k.coef[:, NT:2 * NT], ACT.Exp).then_inc(a_out, 1)

            @b.tensor
            def _(pe):
                pe.wait_ge(cnt, 1)
                for q in range(C):
                    r = oh[:, q * NT:(q + 1) * NT, :].rearrange("p t e -> p (t e)")
                    pe.matmul(pp[:, 2 * q, 0:NT * EE], k.before[:, :], r, start=True, stop=True)
                    mm = pe.matmul(pp[:, 2 * q + 1, 0:NT * EE], k.ones[:, :], r, start=True, stop=True)
                mm.then_inc(off, 1)

            @b.sync
            def _(sp):
                sp.wait_ge(zeroed, 1)
                for r in range(0, nblocks * BLOCK, P * 8):
                    n = min(P * 8, nblocks * BLOCK - r) // P
                    sp.dma_start(xbuf[r:r + n * P, :].rearrange("(p t) d -> p (t d)", p=P), zero[:, 0:n * D]).then_inc(zfill, 16)

            @b.gpsimd
            def _(g):
                g.wait_ge(zfill, 16 * (-(-nblocks * BLOCK // (P * 8))))
                with g.Fori(0, NG) as i:
                    for j in range(G):
                        if j == 0:
                            g.wait_ge(ready, (G + C) * i + G + C)
                            g.sem_inc(passed, 1)
                        for q in range(C):
                            g.indirect_dma_start(xbuf, bass.IndirectOffsetOnAxis(ap=ix[:, q, j:j + 1], axis=0),
                                                 rows[:, j, :], None).then_inc(free[j].sem, 16)
                for s in free:
                    s.wait(g, 16 * C * NG)


def expert_blocks(nc, name, k, xbuf, ybuf, nblocks, hidden, last):
    dims = [(w.shape[1] // P, w.shape[2] // P) for w, _, _ in hidden]
    offs = [sum(f for _, f in dims[:q]) for q in range(len(dims))]
    NF = sum(f for _, f in dims)
    NB = 4
    assert NF % NB == 0
    wl, bl = last
    KL = wl.shape[1] // P
    per = [w for w, _, _ in hidden if w.shape[0] > 1]
    n_ld = 3 + 2 * len(per)
    common = [q for q, (w, _, _) in enumerate(hidden) if w.shape[0] == 1]
    with Phase(nc, name) as ph:
        loaded, once = ph.sems("loaded", 2, "hardware"), ph.sem("once", "hardware")
        xt_done, xt_copied = ph.sems("xt_done", 2), ph.sems("xt_copied", 2)
        hmul, hact, ymul, ydone = ph.sem("hmul"), ph.sem("hact"), ph.sem("ymul"), ph.sem("ydone")
        stored, passed = ph.row_dmas(2, 16 * (nblocks // 2)), ph.sem("passed")
        xb, xt = ph.sb("xb", [P, 2, 2, D]), ph.sb("xt", [P, KD, BLOCK])
        ws, bs = [], []
        for q, (w, _, _) in enumerate(hidden):
            n = 2 if w.shape[0] > 1 else 1
            ws.append(ph.sb(f"w{q}", [P, n, dims[q][0], w.shape[2]]))
            bs.append(ph.sb(f"b{q}", [P, n, dims[q][1]]))
        wls, bls = ph.sb("wl", [P, 2, KL, D]), ph.sb("bl", [P, 2, D])
        hs = [ph.sb(f"h{q}", [P, dims[q][1], BLOCK]) for q in range(len(hidden))]
        ys = ph.sb("ys", [P, 2, 2, D])
        pt, phid, py = ph.ps("pt", [P, 2, 512]), ph.ps("phid", [P, NB, 512]), ph.ps("py", [P, 2, 512])
        iters = nblocks // 2
        with nc.Block() as b:
            @b.sync
            def _(sp):
                for q in common:
                    sp.dma_start(ws[q][:, 0, :, :], hidden[q][0][0].rearrange("(k p) f -> p k f", p=P)).then_inc(once, 16)
                    sp.dma_start(bs[q][:, 0, :], hidden[q][1][0]).then_inc(once, 16)
                with sp.Fori(0, iters) as i:
                    for s in range(2):
                        B = i * 2 + s
                        e = sp.value_load(k.block_expert[0:1, ds(B, 1)], min_val=0, max_val=wl.shape[0] - 1)
                        sp.wait_ge(ydone, 2 * B)
                        for q, (w, bias, _) in enumerate(hidden):
                            if w.shape[0] > 1:
                                sp.dma_start(ws[q][:, s, :, :], w[ds(e, 1), :, :].rearrange("a (k p) f -> p (a k) f", p=P)).then_inc(loaded[s], 16)
                                sp.dma_start(bs[q][:, s, :], bias[ds(e, 1), :, :].rearrange("a p f -> p (a f)")).then_inc(loaded[s], 16)
                        sp.dma_start(xb[:, s, :, :], xbuf[ds(B * BLOCK, BLOCK), :].rearrange("(n p) d -> p n d", p=P)).then_inc(loaded[s], 16)
                        sp.dma_start(wls[:, s, :, :], wl[ds(e, 1), :, :].rearrange("a (k p) n -> p (a k) n", p=P)).then_inc(loaded[s], 16)
                        sp.dma_start(bls[:, s, :], bl[ds(e, 1), :].rearrange("a n -> (a n)").partition_broadcast(P)).then_inc(loaded[s], 16)

            @b.tensor
            def _(pe):
                if common:
                    pe.wait_ge(once, 32 * len(common))
                with pe.Fori(0, iters) as i:
                    for s in range(2):
                        B = i * 2 + s
                        pe.wait_ge(loaded[s], 16 * n_ld * i + 16 * n_ld)
                        pe.wait_ge(xt_copied[s], i)
                        for n in range(2):
                            for q in range(KD):
                                mm = pe.transpose(pt[:, s, q * BLOCK + n * P:q * BLOCK + (n + 1) * P],
                                                  xb[:, s, n, q * P:(q + 1) * P], k.ident[:, :])
                        mm.then_inc(xt_done[s], 1)
                        for l, (kt, ft) in enumerate(dims):
                            src = hs[l - 1] if l else xt
                            if l:
                                pe.wait_ge(hact, B * NF + offs[l] + NB)
                            else:
                                pe.wait_ge(xt_copied[s], i + 1)
                            sl = s if hidden[l][0].shape[0] > 1 else 0
                            for f in range(ft):
                                pe.wait_ge(hact, B * NF + offs[l] + f + 1)
                                for q in range(kt):
                                    mm = pe.matmul(phid[:, (offs[l] + f) % NB, 0:BLOCK], ws[l][:, sl, q, f * P:(f + 1) * P], src[:, q, :],
                                                   start=q == 0, stop=q == kt - 1)
                                mm.then_inc(hmul, 1)
                        for n in range(2):
                            pe.wait_ge(ydone, B * 2 + n + 1)
                            for q in range(KL):
                                if n == 0:
                                    pe.wait_ge(hact, B * NF + offs[-1] + q + 1 + NB)
                                mm = pe.matmul(py[:, n, 0:D], hs[-1][:, q, n * P:(n + 1) * P], wls[:, s, q, :],
                                               start=q == 0, stop=q == KL - 1)
                            mm.then_inc(ymul, 1)

            @b.scalar
            def _(a):
                a.sem_inc(hact, NB)
                if common:
                    a.wait_ge(once, 32 * len(common))
                with a.Fori(0, iters) as i:
                    for s in range(2):
                        B = i * 2 + s
                        a.wait_ge(xt_done[s], i + 1)
                        a.copy(xt[:, :, :], pt[:, s, :].rearrange("p (k n) -> p k n", k=KD)).then_inc(xt_copied[s], 1)
                        a.wait_ge(loaded[s], 16 * n_ld * i + 16 * n_ld)
                        for l, (kt, ft) in enumerate(dims):
                            sl = s if hidden[l][0].shape[0] > 1 else 0
                            for f in range(ft):
                                a.wait_ge(hmul, B * NF + offs[l] + f + 1)
                                a.activation(hs[l][:, f, :], phid[:, (offs[l] + f) % NB, 0:BLOCK], hidden[l][2],
                                             bias=bs[l][:, sl, f:f + 1]).then_inc(hact, 1)

            @b.vector
            def _(v):
                v.sem_inc(ydone, 2)
                with v.Fori(0, iters) as i:
                    for s in range(2):
                        stored[s].wait(v, 16 * i)
                        v.wait_ge(loaded[s], 16 * n_ld * i + 16 * n_ld)
                        for n in range(2):
                            v.wait_ge(ymul, (i * 2 + s) * 2 + n + 1)
                            v.tensor_tensor(ys[:, s, n, :], py[:, n, 0:D], bls[:, s, :], ALU.add).then_inc(ydone, 1)

            @b.gpsimd
            def _(g):
                with g.Fori(0, iters) as i:
                    for s in range(2):
                        B = i * 2 + s
                        g.wait_ge(ydone, B * 2 + 4)
                        g.sem_inc(passed, 1)
                        g.dma_start(ybuf[ds(B * BLOCK, BLOCK), :].rearrange("(n p) d -> p n d", p=P), ys[:, s, :, :]).then_inc(stored[s].sem, 16)
                for s in stored:
                    s.wait(g, 16 * iters)


def combine(nc, name, k, ybuf, C):
    with Phase(nc, name) as ph:
        staged, landed, added, passed = ph.sem("staged"), ph.row_dmas(G, 16 * C * NG), ph.sem("added"), ph.sem("passed")
        ix, rows = ph.sb("ix", [P, G], U32), ph.sb("rows", [P, G, D])
        with nc.Block() as b:
            @b.gpsimd
            def _(g):
                with g.Fori(0, C * NG) as i:
                    g.wait_ge(staged, i + 1)
                    g.sem_inc(passed, 1)
                    for j in range(G):
                        g.indirect_dma_start(rows[:, j, :], None, ybuf, bass.IndirectOffsetOnAxis(ap=ix[:, j:j + 1], axis=0)).then_inc(landed[j].sem, 16)

            @b.vector
            def _(v):
                for q in range(C):
                    with v.Fori(0, NG) as i:
                        v.tensor_copy(ix[:, :], k.back[:, ds(i * G + q * NT, G)]).then_inc(staged, 1)
                        for j in range(G):
                            xt = k.x[:, ds(i * G + j, 1), :].rearrange("p a d -> p (a d)")
                            landed[j].wait(v, 16 * i + 16 * q * NG + 16)
                            if q:
                                v.wait_ge(added, (q - 1) * NT + i * G + j + 1)
                            v.scalar_tensor_tensor(xt, rows[:, j, :], k.coef[:, ds(i * G + j + q * NT, 1)], xt, ALU.mult, ALU.add).then_inc(added, 1)


def degrees(nc, k):
    with Phase(nc, "deg") as ph:
        d, r = ph.sem("d"), ph.sem("r")
        with nc.Block() as b:
            @b.vector
            def _(v):
                v.tensor_scalar(k.dinv[:, :], k.deg_in[:, :], 1.0, None, ALU.add).then_inc(d, 1)
                v.wait_ge(r, 1)
                v.reciprocal(k.dinv[:, :], k.dinv[:, :]).then_inc(d, 1)

            @b.scalar
            def _(a):
                a.wait_ge(d, 1)
                a.activation(k.dinv[:, :], k.dinv[:, :], ACT.Sqrt).then_inc(r, 1)


def batch_norm(nc, k, gamma, beta, eps=1e-5):
    with Phase(nc, "bn") as ph:
        ld, dve, summed, centred, squared, root = ph.sem("ld", "hardware"), ph.sem("dve"), ph.sem("summed"), ph.sem("centred"), ph.sem("squared"), ph.sem("root")
        gm, bt, mean, var = (ph.sb(n, [P, D]) for n in ("gm", "bt", "mean", "var"))
        sq = ph.sb("sq", [P, G, D])
        tmp, zero, cleared = ph.sb("tmp", [P, G, D]), ph.sb("zero", [P, D]), ph.sem("cleared")
        pm = ph.ps("pm", [P, 2, 512])
        with nc.Block() as b:
            @b.sync
            def _(sp):
                sp.dma_start(gm[:, :], gamma.partition_broadcast(P)).then_inc(ld, 16)
                sp.dma_start(bt[:, :], beta.partition_broadcast(P)).then_inc(ld, 16)

            @b.tensor
            def _(pe):
                pe.matmul(pm[:, 0, 0:D], k.ones[:, :], k.y[:, 0, :], start=True, stop=False)
                with pe.Fori(1, NT - 1) as t:
                    pe.matmul(pm[:, 0, 0:D], k.ones[:, :], k.y[:, ds(t, 1), :].rearrange("p a d -> p (a d)"), start=False, stop=False)
                pe.matmul(pm[:, 0, 0:D], k.onesmask[:, :], k.y[:, NT - 1, :], start=False, stop=True).then_inc(summed, 1)
                pe.wait_ge(cleared, 1)
                pe.matmul(pm[:, 1, 0:D], k.ones[:, :], zero[:, :], start=True, stop=False, skip_group_check=True)
                with pe.Fori(0, NG - 1) as i:
                    for j in range(G):
                        pe.wait_ge(squared, i * G + j + 1)
                        mm = pe.matmul(pm[:, 1, 0:D], k.ones[:, :], sq[:, j, :], start=False, stop=False, skip_group_check=True)
                        mm.then_inc(summed, 1)
                for j in range(G):
                    pe.wait_ge(squared, NT - G + j + 1)
                    mm = pe.matmul(pm[:, 1, 0:D], k.ones[:, :] if j < G - 1 else k.onesmask[:, :], sq[:, j, :], start=False, stop=j == G - 1, skip_group_check=True)
                    mm.then_inc(summed, 1)

            @b.vector
            def _(v):
                c = Chain(v, dve)
                v.memset(zero[:, :], 0.0).then_inc(cleared, 1)
                v.wait_ge(summed, 1)
                c(v.tensor_scalar(mean[:, :], pm[:, 0, 0:D], 1.0 / N_NODES, None, ALU.mult))
                with v.Fori(0, NG) as i:
                    for j in range(G):
                        yt = k.y[:, ds(i * G + j, 1), :].rearrange("p a d -> p (a d)")
                        v.tensor_tensor(yt, yt, mean[:, :], ALU.subtract).then_inc(centred, 1)
                v.wait_ge(summed, 1 + NT)
                c(v.tensor_scalar(var[:, :], pm[:, 1, 0:D], 1.0 / N_NODES, eps, ALU.mult, ALU.add))
                v.wait_ge(root, 1)
                c(v.reciprocal(var[:, :], var[:, :]))
                v.wait_ge(ld, 32)
                c(v.tensor_tensor(var[:, :], var[:, :], gm[:, :], ALU.mult))
                n = c.n
                with v.Fori(0, NG) as i:
                    for j in range(G):
                        t = i * G + j
                        yt = k.y[:, ds(t, 1), :].rearrange("p a d -> p (a d)")
                        xt = k.x[:, ds(t, 1), :].rearrange("p a d -> p (a d)")
                        v.wait_ge(dve, n + i * G * 3 + j * 3)
                        v.tensor_tensor(tmp[:, j, :], yt, var[:, :], ALU.mult).then_inc(dve, 1)
                        v.wait_ge(dve, n + i * G * 3 + j * 3 + 1)
                        v.tensor_tensor(tmp[:, j, :], tmp[:, j, :], bt[:, :], ALU.add).then_inc(dve, 1)
                        v.wait_ge(dve, n + i * G * 3 + j * 3 + 2)
                        v.scalar_tensor_tensor(xt, tmp[:, j, :], 0.0, xt, ALU.max, ALU.add).then_inc(dve, 1)

            @b.scalar
            def _(a):
                with a.Fori(0, NG) as i:
                    for j in range(G):
                        a.wait_ge(centred, i * G + j + 1)
                        a.wait_ge(summed, i * G + 1)
                        a.activation(sq[:, j, :], k.y[:, ds(i * G + j, 1), :].rearrange("p a d -> p (a d)"), ACT.Square).then_inc(squared, 1)
                a.wait_ge(dve, 2)
                a.activation(var[:, :], var[:, :], ACT.Sqrt).then_inc(root, 1)


CH = 400
NCH = NP // CH
TC = 640
NTC = NP // TC


def affine_norm(nc, name, k, src, gain, bias, dest, add, eps=1e-5):
    with Phase(nc, name) as ph:
        ld, dve, root = ph.sem("ld", "hardware"), ph.sem("dve"), ph.sem("root")
        st = ph.sb("st", [P, NT, 6])
        mean, var, dif, rstd = (ph.sb(n, [P, NT]) for n in ("mean", "var", "dif", "rstd"))
        gb, bb, tmp = ph.sb("gb", [P, D]), ph.sb("bb", [P, D]), ph.sb("tmp", [P, G, D])
        with nc.Block() as b:
            @b.sync
            def _(sp):
                sp.dma_start(gb[:, :], gain.partition_broadcast(P)).then_inc(ld, 16)
                sp.dma_start(bb[:, :], bias.partition_broadcast(P)).then_inc(ld, 16)

            @b.vector
            def _(v):
                with v.Fori(0, NT) as t:
                    v.bn_stats(st[:, ds(t, 1), :], src[:, ds(t, 1), :]).then_inc(dve, 1)
                v.wait_ge(dve, NT)
                c = Chain(v, dve)
                c.n = NT
                c(v.tensor_tensor(mean[:, :], st[:, :, 1], st[:, :, 4], ALU.add))
                c(v.tensor_scalar(mean[:, :], mean[:, :], 0.5, None, ALU.mult))
                c(v.tensor_tensor(dif[:, :], st[:, :, 1], st[:, :, 4], ALU.subtract))
                c(v.tensor_tensor(dif[:, :], dif[:, :], dif[:, :], ALU.mult))
                c(v.tensor_scalar(dif[:, :], dif[:, :], 0.25, eps, ALU.mult, ALU.add))
                c(v.tensor_tensor(var[:, :], st[:, :, 2], st[:, :, 5], ALU.add))
                c(v.scalar_tensor_tensor(var[:, :], var[:, :], 1.0 / D, dif[:, :], ALU.mult, ALU.add))
                v.wait_ge(root, 1)
                c(v.reciprocal(rstd[:, :], rstd[:, :]))
                v.wait_ge(ld, 32)
                n, m = c.n, 4 if add else 3
                with v.Fori(0, NG) as i:
                    for j in range(G):
                        t = i * G + j
                        at = n + i * G * m + j * m
                        row = dest[:, ds(t, 1), :].rearrange("p a d -> p (a d)")
                        v.wait_ge(dve, at)
                        v.tensor_scalar(tmp[:, j, :], src[:, ds(t, 1), :].rearrange("p a d -> p (a d)"), mean[:, ds(t, 1)],
                                        rstd[:, ds(t, 1)], ALU.subtract, ALU.mult).then_inc(dve, 1)
                        v.wait_ge(dve, at + 1)
                        v.tensor_tensor(tmp[:, j, :], tmp[:, j, :], gb[:, :], ALU.mult).then_inc(dve, 1)
                        v.wait_ge(dve, at + 2)
                        if add:
                            v.tensor_tensor(tmp[:, j, :], tmp[:, j, :], bb[:, :], ALU.add).then_inc(dve, 1)
                            v.wait_ge(dve, at + 3)
                            v.tensor_tensor(row, tmp[:, j, :], row, ALU.add).then_inc(dve, 1)
                        else:
                            v.tensor_tensor(row, tmp[:, j, :], bb[:, :], ALU.add).then_inc(dve, 1)

            @b.scalar
            def _(a):
                a.wait_ge(dve, NT + 7)
                a.activation(rstd[:, :], var[:, :], ACT.Sqrt).then_inc(root, 1)


def turn(nc, name, k, dest, rows=None, table=None):
    with Phase(nc, name) as ph:
        staged, tdone, evac = ph.sem("staged"), ph.sems("tdone", G), ph.sems("evac", G)
        landed = ph.sems("landed", G, "hardware")
        stage = ph.sb("stage", [P, G, D])
        pt = ph.ps("pt", [P, G, 512])
        with nc.Block() as b:
            if table is not None:
                @b.sync
                def _(sp):
                    with sp.Fori(0, NG) as i:
                        for j in range(G):
                            sp.wait_ge(tdone[j], i)
                            sp.dma_start(stage[:, j, :], table[ds((i * G + j) * P, P), :]).then_inc(landed[j], 16)
            else:
                @b.vector
                def _(v):
                    with v.Fori(0, NG) as i:
                        for j in range(G):
                            v.wait_ge(tdone[j], i)
                            v.tensor_copy(stage[:, j, :], rows[:, ds(i * G + j, 1), :].rearrange("p a d -> p (a d)")).then_inc(staged, 1)

            @b.tensor
            def _(pe):
                with pe.Fori(0, NG) as i:
                    for j in range(G):
                        if table is not None:
                            pe.wait_ge(landed[j], 16 * i + 16)
                        else:
                            pe.wait_ge(staged, i * G + j + 1)
                        pe.wait_ge(evac[j], i)
                        for q in range(KD):
                            mm = pe.transpose(pt[:, j, q * P:(q + 1) * P], stage[:, j, q * P:(q + 1) * P], k.ident[:, :])
                        mm.then_inc(tdone[j], 1)

            @b.scalar
            def _(a):
                with a.Fori(0, NG) as i:
                    for j in range(G):
                        a.wait_ge(tdone[j], i + 1)
                        a.copy(dest[:, :, ds((i * G + j) * P, P)], pt[:, j, 0:D].rearrange("p (k n) -> p k n", k=KD)).then_inc(evac[j], 1)


def turn_back(nc, name, k, src, rows):
    with Phase(nc, name) as ph:
        staged, tdone, evac = ph.sem("staged"), ph.sems("tdone", G), ph.sems("evac", G)
        stage = ph.sb("stage", [P, G, KD, P])
        pt = ph.ps("pt", [P, G, 512])
        with nc.Block() as b:
            @b.scalar
            def _(a):
                with a.Fori(0, NG) as i:
                    for j in range(G):
                        a.wait_ge(tdone[j], i)
                        a.copy(stage[:, j, :, :], src[:, :, ds((i * G + j) * P, P)]).then_inc(staged, 1)

            @b.tensor
            def _(pe):
                with pe.Fori(0, NG) as i:
                    for j in range(G):
                        pe.wait_ge(staged, i * G + j + 1)
                        pe.wait_ge(evac[j], i)
                        for q in range(KD):
                            mm = pe.transpose(pt[:, j, q * P:(q + 1) * P], stage[:, j, q, :], k.ident[:, :])
                        mm.then_inc(tdone[j], 1)

            @b.vector
            def _(v):
                with v.Fori(0, NG) as i:
                    for j in range(G):
                        v.wait_ge(tdone[j], i + 1)
                        v.tensor_copy(rows[:, ds(i * G + j, 1), :].rearrange("p a d -> p (a d)"), pt[:, j, 0:D]).then_inc(evac[j], 1)


def order_nodes(nc, k, noise, vrow_dram, table):
    with Phase(nc, "ord") as ph:
        ld, vst, vld = ph.sem("ld", "hardware"), ph.sem("vst", "hardware"), ph.sem("vld", "hardware")
        dve, tr, nums, staged, passed = ph.sem("dve"), ph.sem("tr"), ph.sem("nums"), ph.sem("staged"), ph.sem("passed")
        out = ph.row_dmas(G, 16 * NG)
        val, ns, gone = ph.sb("val", [P, NT]), ph.sb("ns", [P, NT]), ph.sb("gone", [P, 1])
        number = ph.sb("number", [P, NT])
        vt, vrow = ph.sb("vt", [NT, P]), ph.sb("vrow", [P, NP])
        nrow_i, nrow = ph.sb("nrow_i", [P, NP], I32), ph.sb("nrow", [P, NP])
        less, first = ph.sb("less", [P, NP]), ph.sb("first", [P, NP])
        below, ties = ph.sb("below", [P, NT]), ph.sb("ties", [P, NT])
        rows, ix = ph.sb("rows", [P, G, D]), ph.sb("ix", [P, G], U32)
        pt = ph.ps("pt", [P, 512])
        with nc.Block() as b:
            @b.gpsimd
            def _(g):
                g.iota(nrow_i[:, :], pattern=[[1, NP]], base=0, channel_multiplier=0).then_inc(nums, 1)
                with g.Fori(0, NG) as i:
                    g.wait_ge(staged, i * (G + 1) + G + 1)
                    g.sem_inc(passed, 1)
                    for j in range(G):
                        g.indirect_dma_start(table, bass.IndirectOffsetOnAxis(ap=ix[:, j:j + 1], axis=0), rows[:, j, :], None).then_inc(out[j].sem, 16)
                for q in out:
                    q.wait(g, 16 * NG)

            @b.sync
            def _(sp):
                sp.dma_start(ns[:, :], noise).then_inc(ld, 16)
                sp.wait_ge(dve, 5)
                sp.dma_start(vrow_dram.rearrange("(t p) -> t p", p=P), vt[:, :]).then_inc(vst, 16)
                sp.wait_ge(vst, 16)
                sp.dma_start(vrow[:, :], vrow_dram.partition_broadcast(P)).then_inc(vld, 16)

            @b.tensor
            def _(pe):
                pe.wait_ge(dve, 4)
                pe.transpose(pt[0:NT, 0:P], val[:, :], k.ident[:, :]).then_inc(tr, 1)

            @b.vector
            def _(v):
                c = Chain(v, dve)
                v.wait_ge(ld, 16)
                c(v.tensor_tensor(val[:, :], k.deg_out[:, :], ns[:, :], ALU.add))
                c(v.tensor_scalar(gone[:, :], k.lastmask[:, :], -1e30, 1e30, ALU.mult, ALU.add))
                c(v.tensor_tensor(val[:, NT - 1:NT], val[:, NT - 1:NT], k.lastmask[:, :], ALU.mult))
                c(v.tensor_tensor(val[:, NT - 1:NT], val[:, NT - 1:NT], gone[:, :], ALU.add))
                v.wait_ge(tr, 1)
                c(v.tensor_copy(vt[:, :], pt[0:NT, 0:P]))
                c(v.tensor_scalar(number[:, :], k.iota[:, 0:NT], float(P), k.pnum[:, 0:1], ALU.mult, ALU.add))
                v.wait_ge(nums, 1)
                c(v.tensor_copy(nrow[:, :], nrow_i[:, :]))
                v.wait_ge(vld, 16)
                n = c.n
                with v.Fori(0, NT) as t:
                    v.wait_ge(dve, n + 3 * t)
                    v.tensor_scalar(less[:, :], vrow[:, :], val[:, ds(t, 1)], None, ALU.is_lt, ALU.add, accum_out=below[:, ds(t, 1)]).then_inc(dve, 1)
                    v.tensor_scalar(first[:, :], nrow[:, :], number[:, ds(t, 1)], None, ALU.is_lt).then_inc(dve, 1)
                    v.wait_ge(dve, n + 3 * t + 2)
                    v.scalar_tensor_tensor(less[:, :], vrow[:, :], val[:, ds(t, 1)], first[:, :], ALU.is_equal, ALU.mult,
                                           accum_out=ties[:, ds(t, 1)]).then_inc(dve, 1)
                c.n = n + 3 * NT
                v.wait_ge(dve, c.n)
                c(v.tensor_tensor(below[:, :], below[:, :], ties[:, :], ALU.add))
                c(v.tensor_copy(k.rank[:, :], below[:, :]))
                with v.Fori(0, NG) as i:
                    for j in range(G):
                        out[j].wait(v, 16 * i)
                        v.tensor_copy(rows[:, j, :], k.y[:, ds(i * G + j, 1), :].rearrange("p a d -> p (a d)")).then_inc(staged, 1)
                    v.tensor_copy(ix[:, :], k.rank[:, ds(i * G, G)]).then_inc(staged, 1)


def mamba_in(nc, k, w, xc, zs):
    with Phase(nc, "mi") as ph:
        ld, stored = ph.sem("ld", "hardware"), ph.sem("stored", "hardware")
        mul, evac = ph.sem("mul"), ph.sem("evac")
        wsb, zst = ph.sb("w", [P, KD, 2 * D]), ph.sb("zst", [P, KD, CH])
        pi = ph.ps("pi", [P, 4, 512])
        with nc.Block() as b:
            @b.sync
            def _(sp):
                sp.dma_start(wsb[:, :, :], w.rearrange("(k p) n -> p k n", p=P)).then_inc(ld, 16)
                with sp.Fori(0, NCH) as i:
                    sp.wait_ge(evac, 4 * i + 8)
                    sp.dma_start(zs[:, :, ds(i * CH, CH)], zst[:, :, :]).then_inc(stored, 16)
                sp.wait_ge(stored, 16 * NCH)

            @b.tensor
            def _(pe):
                pe.wait_ge(ld, 16)
                with pe.Fori(0, NCH) as i:
                    for o in range(4):
                        pe.wait_ge(evac, 4 * i + o + 1)
                        for q in range(KD):
                            mm = pe.matmul(pi[:, o, 0:CH], wsb[:, q, o * P:(o + 1) * P], k.t[:, q, ds(i * CH, CH)], start=q == 0, stop=q == KD - 1)
                        mm.then_inc(mul, 1)

            @b.scalar
            def _(a):
                a.sem_inc(evac, 4)
                with a.Fori(0, NCH) as i:
                    for o in range(2):
                        a.wait_ge(mul, 4 * i + o + 1)
                        a.copy(xc[:, o, ds(i * CH + TAPS - 1, CH)], pi[:, o, 0:CH]).then_inc(evac, 1)
                    a.wait_ge(stored, 16 * i)
                    for o in range(2):
                        a.wait_ge(mul, 4 * i + o + 3)
                        a.activation(zst[:, o, :], pi[:, 2 + o, 0:CH], ACT.Silu).then_inc(evac, 1)

            @b.vector
            def _(v):
                v.memset(xc[:, :, 0:TAPS - 1], 0.0)


def mamba_conv(nc, k, w, bias, xc, cv):
    with Phase(nc, "mc") as ph:
        ld, dve, act = ph.sem("ld", "hardware"), ph.sem("dve"), ph.sem("act")
        ws, bs = ph.sb("w", [P, KD, TAPS]), ph.sb("b", [P, KD])
        with nc.Block() as b:
            @b.sync
            def _(sp):
                sp.dma_start(ws[:, :, :], w.rearrange("(k p) n -> p k n", p=P)).then_inc(ld, 16)
                sp.dma_start(bs[:, :], bias).then_inc(ld, 16)

            @b.vector
            def _(v):
                c = Chain(v, dve)
                v.wait_ge(ld, 32)
                for o in range(KD):
                    c(v.tensor_scalar(cv[:, o, :], xc[:, o, 0:NP], ws[:, o, 0:1], None, ALU.mult))
                    for q in range(1, TAPS):
                        c(v.scalar_tensor_tensor(cv[:, o, :], xc[:, o, q:q + NP], ws[:, o, q:q + 1], cv[:, o, :], ALU.mult, ALU.add))

            @b.scalar
            def _(a):
                a.wait_ge(ld, 32)
                for o in range(KD):
                    a.wait_ge(dve, (o + 1) * TAPS)
                    a.activation(xc[:, o, 0:NP], cv[:, o, :], ACT.Silu, bias=bs[:, o:o + 1])


def mamba_steps(nc, k, wx, wdt, bdt, dpar, xc, dt, bc):
    H2 = NP // 2
    with Phase(nc, "ms") as ph:
        ld, stored = ph.sem("ld", "hardware"), ph.sem("stored", "hardware")
        mul, evac, mul2, evac2, dve, act, passed = (ph.sem(n) for n in ("mul", "evac", "mul2", "evac2", "dve", "act", "passed"))
        R = RANK + 2 * STATES
        wxs, wds, bds, dps = ph.sb("wx", [P, KD, R]), ph.sb("wdt", [RANK, D]), ph.sb("bdt", [P, KD]), ph.sb("dp", [P, KD])
        dbc = ph.sb("dbc", [R, NP])
        e, wv, lnw, z = (ph.sb(n, [P, H2]) for n in ("e", "wv", "lnw", "z"))
        pd, pdt = ph.ps("pd", [P, 512]), ph.ps("pdt", [P, 2, 512])
        with nc.Block() as b:
            @b.sync
            def _(sp):
                sp.dma_start(wxs[:, :, :], wx.rearrange("(k p) n -> p k n", p=P)).then_inc(ld, 16)
                sp.dma_start(wds[:, :], wdt).then_inc(ld, 16)
                sp.dma_start(bds[:, :], bdt).then_inc(ld, 16)
                sp.dma_start(dps[:, :], dpar).then_inc(ld, 16)
                sp.wait_ge(evac, NCH)
                sp.dma_start(bc, dbc[RANK:R, :]).then_inc(stored, 16)
                sp.wait_ge(stored, 16)

            @b.tensor
            def _(pe):
                pe.wait_ge(ld, 64)
                with pe.Fori(0, NCH) as i:
                    pe.wait_ge(evac, i)
                    pe.sem_inc(passed, 1)
                    for q in range(KD):
                        mm = pe.matmul(pd[0:R, 0:CH], wxs[:, q, :], xc[:, q, ds(i * CH, CH)], start=q == 0, stop=q == KD - 1)
                    mm.then_inc(mul, 1)
                    pe.wait_ge(evac2, 2 * i)
                    pe.wait_ge(evac, i + 1)
                    pe.sem_inc(passed, 1)
                    for o in range(KD):
                        pe.matmul(pdt[:, o, 0:CH], wds[:, o * P:(o + 1) * P], dbc[0:RANK, ds(i * CH, CH)], start=True, stop=True).then_inc(mul2, 1)

            @b.scalar
            def _(a):
                a.wait_ge(ld, 64)
                with a.Fori(0, NCH) as i:
                    a.wait_ge(mul, i + 1)
                    a.copy(dbc[:, ds(i * CH, CH)], pd[0:R, 0:CH]).then_inc(evac, 1)
                    for o in range(KD):
                        a.wait_ge(mul2, 2 * i + o + 1)
                        a.activation(dt[:, o, ds(i * CH, CH)], pdt[:, o, 0:CH], ACT.Identity, bias=bds[:, o:o + 1]).then_inc(evac2, 1)
                a.wait_ge(evac2, 2 * NCH)
                for h in range(4):
                    x = dt[:, h // 2, h % 2 * H2:(h % 2 + 1) * H2]
                    a.wait_ge(dve, 9 * h)
                    a.activation(e[:, :], x, ACT.Abs).then_inc(act, 1)
                    a.wait_ge(act, 3 * h + 1)
                    a.activation(e[:, :], e[:, :], ACT.Exp, scale=-1.0).then_inc(act, 1)
                    a.wait_ge(dve, 9 * h + 1)
                    a.activation(lnw[:, :], wv[:, :], ACT.Ln).then_inc(act, 1)

            @b.vector
            def _(v):
                c = Chain(v, dve)
                v.wait_ge(evac2, 2 * NCH)
                for h in range(4):
                    x = dt[:, h // 2, h % 2 * H2:(h % 2 + 1) * H2]
                    v.wait_ge(act, 3 * h + 2)
                    c(v.tensor_scalar(wv[:, :], e[:, :], 1.0, None, ALU.add))
                    v.wait_ge(act, 3 * h + 3)
                    c(v.tensor_scalar(wv[:, :], wv[:, :], -1.0, None, ALU.add))
                    c(v.tensor_scalar(z[:, :], wv[:, :], 0.0, None, ALU.is_equal))
                    c(v.tensor_tensor(wv[:, :], wv[:, :], z[:, :], ALU.add))
                    c(v.tensor_tensor(lnw[:, :], lnw[:, :], z[:, :], ALU.add))
                    c(v.reciprocal(wv[:, :], wv[:, :]))
                    c(v.tensor_tensor(lnw[:, :], lnw[:, :], wv[:, :], ALU.mult))
                    c(v.tensor_tensor(lnw[:, :], lnw[:, :], e[:, :], ALU.mult))
                    c(v.scalar_tensor_tensor(x, x, 0.0, lnw[:, :], ALU.max, ALU.add))
                v.wait_ge(ld, 64)
                for o in range(KD):
                    c(v.tensor_scalar(k.t[:, o, :], xc[:, o, 0:NP], dps[:, o:o + 1], None, ALU.mult))
                    c(v.tensor_tensor(xc[:, o, 0:NP], xc[:, o, 0:NP], dt[:, o, :], ALU.mult))


def mamba_scan(nc, k, a_log, xc, dt, bc):
    with Phase(nc, "scan") as ph:
        ld, landed = ph.sem("ld", "hardware"), ph.sems("landed", 2, "hardware")
        dve, neg, grown, prod, scanned, outed, added, carry, passed, asked = (ph.sem(n) for n in ("dve", "neg", "grown", "prod", "scanned", "outed", "added", "carry", "passed", "asked"))
        A = ph.sb("A", [P, KD, STATES])
        bb, cb = ph.sb("bb", [P, 2, TC]), ph.sb("cb", [P, 2, TC])
        da, dbx, h, hc = (ph.sb(n, [P, 2, KD, TC]) for n in ("da", "dbx", "h", "hc"))
        last = ph.sb("last", [P, KD, STATES])
        with nc.Block() as b:
            @b.sync
            def _(sp):
                sp.dma_start(A[:, :, :], a_log.rearrange("(k p) n -> p k n", p=P)).then_inc(ld, 16)
                with sp.Fori(0, NTC) as c:
                    with sp.Fori(0, STATES // 2) as n:
                        for s in range(2):
                            step = c * STATES + n * 2 + s
                            sp.wait_ge(outed, (step + 1) * KD)
                            sp.sem_inc(asked, 1)
                            sp.wait_ge(landed[s], 32 * (c * (STATES // 2) + n))
                            sp.sem_inc(asked, 1)
                            for q, dst in ((0, bb), (STATES, cb)):
                                row = bc[ds(n * 2 + (s + q), 1), ds(c * TC, TC)].rearrange("a t -> (a t)")
                                sp.dma_start(dst[:, s, :], row.partition_broadcast(P)).then_inc(landed[s], 16)

            @b.scalar
            def _(a):
                a.wait_ge(ld, 16)
                a.activation(A[:, :, :], A[:, :, :], ACT.Exp).then_inc(neg, 1)
                a.wait_ge(neg, 2)
                with a.Fori(0, NTC) as c:
                    with a.Fori(0, STATES // 2) as n:
                        for s in range(2):
                            for o in range(KD):
                                a.wait_ge(scanned, (c * STATES + n * 2 + s) * KD + o + 1)
                                a.activation(da[:, s, o, :], dt[:, o, ds(c * TC, TC)], ACT.Exp, scale=A[:, o, ds(n * 2 + s, 1)]).then_inc(grown, 1)

            @b.vector
            def _(v):
                v.sem_inc(scanned, 2 * KD)
                v.sem_inc(outed, 2 * KD)
                v.memset(last[:, :, :].rearrange("p k n -> p (k n)"), 0.0).then_inc(carry, 1)
                v.wait_ge(neg, 1)
                v.tensor_scalar(A[:, :, :], A[:, :, :], -1.0, None, ALU.mult).then_inc(neg, 1)
                with v.Fori(0, NTC) as c:
                    with v.Fori(0, STATES // 2) as n:
                        for s in range(2):
                            st = c * STATES + n * 2 + s
                            v.wait_ge(landed[s], 32 * (c * (STATES // 2) + n) + 32)
                            for o in range(KD):
                                v.tensor_tensor(dbx[:, s, o, :], xc[:, o, ds(c * TC, TC)], bb[:, s, :], ALU.mult).then_inc(prod, 1)
                            for o in range(KD):
                                g = st * KD + o
                                v.wait_ge(grown, g + 1)
                                v.wait_ge(prod, g + 1)
                                v.wait_ge(carry, st * KD + 1)
                                v.tensor_tensor_scan(h[:, s, o, :], da[:, s, o, :], dbx[:, s, o, :], last[:, o, ds(n * 2 + s, 1)], ALU.mult, ALU.add).then_inc(scanned, 1)
                            for o in range(KD):
                                g = st * KD + o
                                v.wait_ge(scanned, g + 1 + 2 * KD)
                                v.wait_ge(added, g + 1)
                                v.tensor_tensor(hc[:, s, o, :], h[:, s, o, :], cb[:, s, :], ALU.mult).then_inc(outed, 1)
                                v.tensor_copy(last[:, o, ds(n * 2 + s, 1)], h[:, s, o, TC - 1:TC]).then_inc(carry, 1)

            @b.gpsimd
            def _(g):
                g.sem_inc(added, 2 * KD)
                with g.Fori(0, NTC) as c:
                    with g.Fori(0, STATES // 2) as n:
                        for s in range(2):
                            for o in range(KD):
                                at = (c * STATES + n * 2 + s) * KD + o
                                g.wait_ge(outed, at + 1 + 2 * KD)
                                g.wait_ge(added, at + KD + 1)
                                g.sem_inc(passed, 1)
                                y = k.t[:, o, ds(c * TC, TC)]
                                g.tensor_tensor(y, y, hc[:, s, o, :], ALU.add).then_inc(added, 1)


def gate_rows(nc, k, zs):
    with Phase(nc, "gz") as ph:
        landed, used, asked = ph.sems("landed", 2, "hardware"), ph.sem("used"), ph.sem("asked")
        z = ph.sb("z", [P, 2, KD, CH])
        with nc.Block() as b:
            @b.sync
            def _(sp):
                with sp.Fori(0, NCH // 2) as i:
                    for s in range(2):
                        sp.wait_ge(used, 2 * i + s + 1)
                        sp.sem_inc(asked, 1)
                        sp.wait_ge(landed[s], 16 * i)
                        sp.dma_start(z[:, s, :, :], zs[:, :, ds((2 * i + s) * CH, CH)]).then_inc(landed[s], 16)

            @b.vector
            def _(v):
                v.sem_inc(used, 2)
                with v.Fori(0, NCH // 2) as i:
                    for s in range(2):
                        v.wait_ge(landed[s], 16 * i + 16)
                        t = k.t[:, :, ds((2 * i + s) * CH, CH)]
                        v.tensor_tensor(t, t, z[:, s, :, :], ALU.mult).then_inc(used, 1)


def fetch_rows(nc, k, table):
    with Phase(nc, "fr") as ph:
        landed = ph.row_dmas(G, 16 * NG)
        staged, passed, added = ph.sem("staged"), ph.sem("passed"), ph.sem("added")
        ix, rows = ph.sb("ix", [P, G], U32), ph.sb("rows", [P, G, D])
        with nc.Block() as b:
            @b.gpsimd
            def _(g):
                with g.Fori(0, NG) as i:
                    g.wait_ge(staged, i + 1)
                    g.sem_inc(passed, 1)
                    for j in range(G):
                        g.indirect_dma_start(rows[:, j, :], None, table, bass.IndirectOffsetOnAxis(ap=ix[:, j:j + 1], axis=0)).then_inc(landed[j].sem, 16)

            @b.vector
            def _(v):
                with v.Fori(0, NG) as i:
                    v.wait_ge(added, i * G)
                    v.tensor_copy(ix[:, :], k.rank[:, ds(i * G, G)]).then_inc(staged, 1)
                    for j in range(G):
                        landed[j].wait(v, 16 * i + 16)
                        v.tensor_tensor(k.rows[:, ds(i * G + j, 1), :], rows[:, j:j + 1, :], k.y[:, ds(i * G + j, 1), :], ALU.add).then_inc(added, 1)


def edge_scores(nc, k, lists, stable, ev):
    gi, kl, wl, own = lists
    iters = ST // RING
    with Phase(nc, "sc") as ph:
        landed = ph.row_dmas(RING, 16 * iters)
        sst = ph.sem("sst", "hardware")
        staged, passed, oh_ready, tr, tcopied, mul, added = (ph.sem(n) for n in ("staged", "passed", "oh", "tr", "tcopied", "mul", "added"))
        dve, act, gp = ph.sem("dve"), ph.sem("act"), ph.sem("gp")
        ix = ph.sb("ix", [P, RING], U32)
        src, oh = ph.sb("src", [P, RING, HEADS]), ph.sb("oh", [P, RING, P])
        tgt = ph.sb("tgt", [P, NT, HEADS])
        TB = 4
        oht = ph.sb("oht", [P, RING, P])
        valid, far = ph.sb("valid", [P, SP_]), ph.sb("far", [P, SP_])
        low = ph.sb("low", [P, SP_, HEADS])
        top, alltop = ph.sb("top", [P, 1]), ph.sb("alltop", [P, 1])
        pt, pe4 = ph.ps("pt", [P, TB, 512]), ph.ps("pe4", [P, 2, 512])
        with nc.Block() as b:
            @b.sync
            def _(sp):
                sp.dma_start(stable.rearrange("(t p) h -> p t h", p=P), k.score[:, :, 0, :]).then_inc(sst, 16)
                sp.wait_ge(sst, 16)

            @b.gpsimd
            def _(g):
                g.wait_ge(sst, 16)
                with g.Fori(0, iters) as i:
                    for j in range(RING):
                        if j % HALF == 0:
                            g.wait_ge(staged, 2 * i + j // HALF + 1)
                            g.sem_inc(passed, 1)
                        g.indirect_dma_start(src[:, j, :], None, stable, bass.IndirectOffsetOnAxis(ap=ix[:, j:j + 1], axis=0)).then_inc(landed[j].sem, 16)
                g.wait_ge(dve, 8)
                g.partition_all_reduce(alltop[:, :], top[:, :], P, RMAX).then_inc(gp, 1)

            def one_hots(v, first, h):
                for j in range(h * HALF, (h + 1) * HALF):
                    v.tensor_scalar(oh[:, j, :], k.iota[:, 0:P], kl[:, ds(first + j, 1)], None, ALU.is_equal).then_inc(oh_ready, 1)

            @b.vector
            def _(v):
                c = Chain(v, dve)
                v.sem_inc(added, 1)
                v.tensor_copy(ix[:, 0:HALF], gi[:, 0:HALF]).then_inc(staged, 1)
                v.tensor_copy(ix[:, HALF:RING], gi[:, HALF:RING]).then_inc(staged, 1)
                c(v.tensor_copy(tgt[:, :, :], k.score[:, :, 1, :]))
                c(v.memset(ev[:, ST:SP_, :].rearrange("p a h -> p (a h)"), 0.0))
                one_hots(v, 0, 0)
                with v.Fori(0, iters) as i:
                    for h in range(2):
                        one_hots(v, i * RING + (RING if h else 0), 1 - h)
                        for j in range(h * HALF, (h + 1) * HALF):
                            landed[j].wait(v, 16 * i + 16)
                        v.wait_ge(mul, 2 * i + h + 1)
                        v.tensor_tensor(ev[:, ds(i * RING + h * HALF, HALF), :], src[:, h * HALF:(h + 1) * HALF, :],
                                        pe4[:, h, 0:HALF * HEADS].rearrange("p (j h) -> p j h", h=HEADS), ALU.add).then_inc(added, 1)
                        v.wait_ge(added, 2 * i + h + 2)
                        v.tensor_copy(ix[:, h * HALF:(h + 1) * HALF], gi[:, ds(i * RING + RING + h * HALF, HALF)]).then_inc(staged, 1)
                v.wait_ge(added, 2 * iters + 1)
                c(v.tensor_scalar(valid[:, :], kl[:, :], 0.0, None, ALU.is_ge))
                c(v.tensor_scalar(far[:, :], valid[:, :], 1e30, -1e30, ALU.mult, ALU.add))
                c(v.tensor_tensor(ev[:, :, :], ev[:, :, :], spread(far[:, :], HEADS), ALU.add))
                c(v.tensor_scalar(low[:, :, :], ev[:, :, :], 0.2, None, ALU.mult))
                c(v.tensor_tensor(ev[:, :, :], ev[:, :, :], low[:, :, :], ALU.max))
                c(v.tensor_reduce(top[:, :], ev[:, :, :].rearrange("p a h -> p (a h)"), AX_X, ALU.max))
                v.wait_ge(gp, 1)
                c(v.tensor_scalar(top[:, :], alltop[:, :], -1.0, None, ALU.mult))

            @b.tensor
            def _(pe):
                pe.wait_ge(dve, 1)
                with pe.Fori(0, iters) as i:
                    for h in range(2):
                        slots = range(h * HALF, (h + 1) * HALF)
                        for j in slots:
                            pe.wait_ge(oh_ready, i * RING + j + 1)
                            pe.wait_ge(tcopied, i * RING + j + 1)
                            pe.transpose(pt[:, j % TB, 0:P], oh[:, j, :], k.ident[:, :]).then_inc(tr, 1)
                        pe.wait_ge(added, 2 * i + h)
                        for j in slots:
                            tile = pe.value_load(own[0:1, ds(i * RING + j, 1)], min_val=0, max_val=NT - 1)
                            pe.wait_ge(tcopied, i * RING + j + 1 + TB)
                            mm = pe.matmul(pe4[:, h, j % HALF * HEADS:(j % HALF + 1) * HEADS], oht[:, j, :],
                                           tgt[:, ds(tile, 1), :].rearrange("p a h -> p (a h)"), start=True, stop=True)
                        mm.then_inc(mul, 1)

            @b.scalar
            def _(a):
                a.sem_inc(tcopied, TB)
                with a.Fori(0, iters) as i:
                    for j in range(RING):
                        a.wait_ge(tr, i * RING + j + 1)
                        if j % HALF == 0:
                            a.wait_ge(mul, 2 * i)
                        a.copy(oht[:, j, :], pt[:, j % TB, 0:P]).then_inc(tcopied, 1)
                a.wait_ge(dve, 9)
                a.activation(ev[:, :, :], ev[:, :, :], ACT.Exp, bias=top[:, 0:1]).then_inc(act, 1)


def attend(nc, k, lists, table, ev, ag):
    gi, kl, _, own = lists
    iters = ST // RING
    with Phase(nc, "at") as ph:
        landed = ph.row_dmas(RING, 16 * iters)
        staged, passed, oh_ready, scaled, summed, added = (ph.sem(n) for n in ("staged", "passed", "oh", "scaled", "summed", "added"))
        ix = ph.sb("ix", [P, RING], U32)
        rows, oh = ph.sb("rows", [P, RING, D]), ph.sb("oh", [P, RING, P])
        NB = 4
        pa = ph.ps("pa", [P, NB, 512])
        with nc.Block() as b:
            @b.gpsimd
            def _(g):
                with g.Fori(0, iters) as i:
                    for j in range(RING):
                        if j % HALF == 0:
                            g.wait_ge(staged, 2 * i + j // HALF + 1)
                            g.sem_inc(passed, 1)
                        g.indirect_dma_start(rows[:, j, :], None, table, bass.IndirectOffsetOnAxis(ap=ix[:, j:j + 1], axis=0)).then_inc(landed[j].sem, 16)

            def one_hots(v, first, h):
                for j in range(h * HALF, (h + 1) * HALF):
                    v.tensor_scalar(oh[:, j, :], k.iota[:, 0:P], kl[:, ds(first + j, 1)], None, ALU.is_equal).then_inc(oh_ready, 1)

            @b.vector
            def _(v):
                v.memset(ag[:, :, :].rearrange("p t c -> p (t c)"), 0.0).then_inc(added, NB)
                v.tensor_copy(ix[:, 0:HALF], gi[:, 0:HALF]).then_inc(staged, 1)
                v.tensor_copy(ix[:, HALF:RING], gi[:, HALF:RING]).then_inc(staged, 1)
                one_hots(v, 0, 0)
                with v.Fori(0, iters) as i:
                    for h in range(2):
                        one_hots(v, i * RING + (RING if h else 0), 1 - h)

                        def scale(j):
                            landed[j].wait(v, 16 * i + 16)
                            heads = rows[:, j, :].rearrange("p (h f) -> p h f", h=HEADS)
                            v.tensor_tensor(heads, heads, spread(ev[:, ds(i * RING + j, 1), :].rearrange("p a h -> p (a h)"), D // HEADS), ALU.mult).then_inc(scaled, 1)

                        scale(h * HALF)
                        scale(h * HALF + 1)
                        for j in range(h * HALF, (h + 1) * HALF):
                            if j + 2 < (h + 1) * HALF:
                                scale(j + 2)
                            tile = v.value_load(own[0:1, ds(i * RING + j, 1)], min_val=0, max_val=NT - 1)
                            v.wait_ge(summed, i * RING + j + 1)
                            v.wait_ge(added, i * RING + j + NB)
                            sums = ag[:, ds(tile, 1), :].rearrange("p a c -> p (a c)")
                            v.tensor_tensor(sums, sums, pa[:, j % NB, 0:D + HEADS], ALU.add).then_inc(added, 1)
                        v.tensor_copy(ix[:, h * HALF:(h + 1) * HALF], gi[:, ds(i * RING + RING + h * HALF, HALF)]).then_inc(staged, 1)

            @b.tensor
            def _(pe):
                with pe.Fori(0, iters) as i:
                    for j in range(RING):
                        pe.wait_ge(oh_ready, i * RING + j + 1)
                        pe.wait_ge(scaled, i * RING + j + 1)
                        pe.wait_ge(added, i * RING + j + 1)
                        pe.matmul(pa[:, j % NB, 0:D], oh[:, j, :], rows[:, j, :], start=True, stop=True)
                        pe.matmul(pa[:, j % NB, D:D + HEADS], oh[:, j, :], ev[:, ds(i * RING + j, 1), :].rearrange("p a h -> p (a h)"), start=True, stop=True).then_inc(summed, 1)


def local_rows(nc, k, ag, bias):
    with Phase(nc, "lr") as ph:
        ld, dve, act = ph.sem("ld", "hardware"), ph.sem("dve"), ph.sem("act")
        bb, inv, low = ph.sb("bb", [P, D]), ph.sb("inv", [P, NT, HEADS]), ph.sb("low", [P, NT, D])
        F = D // HEADS
        with nc.Block() as b:
            @b.sync
            def _(sp):
                sp.dma_start(bb[:, :], bias.partition_broadcast(P)).then_inc(ld, 16)

            @b.vector
            def _(v):
                c = Chain(v, dve)
                c(v.tensor_scalar(inv[:, :, :], ag[:, :, D:D + HEADS], 1e-16, None, ALU.add))
                c(v.reciprocal(inv[:, :, :], inv[:, :, :]))
                for h in range(HEADS):
                    v.tensor_tensor(k.rows[:, :, h * F:(h + 1) * F], ag[:, :, h * F:(h + 1) * F], spread(inv[:, :, h], F), ALU.mult).then_inc(dve, 1)
                c.n += HEADS
                v.wait_ge(dve, c.n)
                c(v.tensor_tensor(k.rows[:, :, :], k.rows[:, :, :], k.y[:, :, :], ALU.add))
                v.wait_ge(ld, 16)
                c(v.tensor_tensor(k.rows[:, :, :], k.rows[:, :, :], bb[:, :].unsqueeze(1).broadcast_to([P, NT, D]), ALU.add))
                c(v.tensor_scalar(low[:, :, :], k.rows[:, :, :], 0.0, None, ALU.min))
                v.wait_ge(act, 1)
                c(v.scalar_tensor_tensor(k.rows[:, :, :], k.rows[:, :, :], 0.0, low[:, :, :], ALU.max, ALU.add))
                c(v.tensor_scalar(k.rows[:, :, :], k.rows[:, :, :], -1.0, None, ALU.add))

            @b.scalar
            def _(a):
                a.wait_ge(dve, 5 + HEADS)
                a.activation(low[:, :, :], low[:, :, :], ACT.Exp).then_inc(act, 1)


def gate_and_feed(nc, k, t2, wl, wg, w1, b1, w2, b2):
    KH = 2 * KD
    with Phase(nc, "gf") as ph:
        ld = ph.sem("ld", "hardware")
        gmul, gated, dve, mixed, hmul, hidden, omul, fin = (ph.sem(n) for n in ("gmul", "gated", "dve", "mixed", "hmul", "hidden", "omul", "fin"))
        wls, wgs = ph.sb("wl", [P, KD, D]), ph.sb("wg", [P, KD, D])
        w1s, w2s = ph.sb("w1", [P, KD, 2 * D]), ph.sb("w2", [P, KH, D])
        b1s, b2s = ph.sb("b1", [P, KH]), ph.sb("b2", [P, KD])
        gate, dif, hid = ph.sb("gate", [P, KD, CH]), ph.sb("dif", [P, KD, CH]), ph.sb("hid", [P, KH, CH])
        pg, phid, po = ph.ps("pg", [P, KD, 512]), ph.ps("ph", [P, KH, 512]), ph.ps("po", [P, KD, 512])
        with nc.Block() as b:
            @b.sync
            def _(sp):
                for dst, w in ((wls, wl), (wgs, wg), (w1s, w1), (w2s, w2)):
                    sp.dma_start(dst[:, :, :], w.rearrange("(k p) n -> p k n", p=P)).then_inc(ld, 16)
                sp.dma_start(b1s[:, :], b1).then_inc(ld, 16)
                sp.dma_start(b2s[:, :], b2).then_inc(ld, 16)

            @b.tensor
            def _(pe):
                pe.wait_ge(ld, 96)
                with pe.Fori(0, NCH) as i:
                    pe.wait_ge(gated, KD * i)
                    for o in range(KD):
                        for q in range(KD):
                            pe.matmul(pg[:, o, 0:CH], wls[:, q, o * P:(o + 1) * P], k.t[:, q, ds(i * CH, CH)], start=q == 0, stop=False)
                        for q in range(KD):
                            mm = pe.matmul(pg[:, o, 0:CH], wgs[:, q, o * P:(o + 1) * P], t2[:, q, ds(i * CH, CH)], start=False, stop=q == KD - 1)
                        mm.then_inc(gmul, 1)
                    pe.wait_ge(hidden, KH * i)
                    pe.wait_ge(mixed, i + 1)
                    for f in range(KH):
                        for q in range(KD):
                            mm = pe.matmul(phid[:, f, 0:CH], w1s[:, q, f * P:(f + 1) * P], k.t[:, q, ds(i * CH, CH)], start=q == 0, stop=q == KD - 1)
                        mm.then_inc(hmul, 1)
                    pe.wait_ge(fin, KD * i)
                    pe.wait_ge(hidden, KH * i + KH)
                    for o in range(KD):
                        for f in range(KH):
                            mm = pe.matmul(po[:, o, 0:CH], w2s[:, f, o * P:(o + 1) * P], hid[:, f, :], start=f == 0, stop=f == KH - 1)
                        mm.then_inc(omul, 1)

            @b.scalar
            def _(a):
                a.wait_ge(ld, 96)
                with a.Fori(0, NCH) as i:
                    a.wait_ge(mixed, i)
                    for o in range(KD):
                        a.wait_ge(gmul, KD * i + o + 1)
                        a.activation(gate[:, o, :], pg[:, o, 0:CH], ACT.Sigmoid).then_inc(gated, 1)
                    a.wait_ge(omul, KD * i)
                    for f in range(KH):
                        a.wait_ge(hmul, KH * i + f + 1)
                        a.activation(hid[:, f, :], phid[:, f, 0:CH], ACT.Relu, bias=b1s[:, f:f + 1]).then_inc(hidden, 1)

            @b.vector
            def _(v):
                v.wait_ge(ld, 96)
                with v.Fori(0, NCH) as i:
                    one, two = k.t[:, :, ds(i * CH, CH)], t2[:, :, ds(i * CH, CH)]
                    v.wait_ge(mixed, i)
                    v.tensor_tensor(dif[:, :, :], one, two, ALU.subtract).then_inc(dve, 1)
                    v.wait_ge(gated, KD * i + KD)
                    v.wait_ge(dve, 2 * i + 1)
                    v.tensor_tensor(dif[:, :, :], dif[:, :, :], gate[:, :, :], ALU.mult).then_inc(dve, 1)
                    v.wait_ge(dve, 2 * i + 2)
                    v.wait_ge(gmul, KD * i + KD)
                    v.tensor_tensor(one, two, dif[:, :, :], ALU.add).then_inc(mixed, 1)
                    v.wait_ge(mixed, i + 1)
                    v.wait_ge(hmul, KH * i + KH)
                    for o in range(KD):
                        v.wait_ge(omul, KD * i + o + 1)
                        t = k.t[:, o, ds(i * CH, CH)]
                        v.scalar_tensor_tensor(t, po[:, o, 0:CH], b2s[:, o:o + 1], t, ALU.add, ALU.add).then_inc(fin, 1)


def attention_layer(nc, k, a, by_dst, drams):
    xs, ys, zs, bc, vrow, table, stable = drams

    def w(name):
        return a["L3_gnn_" + name]

    with ExitStack() as ctx:
        def sb(name, shape, dt=F32):
            return ctx.enter_context(nc.sbuf_tensor(name, shape, dt))

        k.rank, k.score = sb("rank", [P, NT], U32), sb("score", [P, NT, 2, HEADS])
        normalise(nc, "n6", k, keep=True)
        order_nodes(nc, k, a["node_vec"], vrow, xs)
        turn(nc, "tx", k, k.t, table=xs)
        with nc.sbuf_tensor("xc", [P, KD, NP + TAPS - 1], F32) as xc, nc.sbuf_tensor("dt", [P, KD, NP], F32) as dt:
            mamba_in(nc, k, w("in_proj_w"), xc, zs)
            mamba_conv(nc, k, w("conv_w"), w("conv_b"), xc, dt)
            mamba_steps(nc, k, w("x_proj_w"), w("dt_proj_w"), w("dt_proj_b"), w("D_param"), xc, dt, bc)
            mamba_scan(nc, k, w("A_log"), xc, dt, bc)
        gate_rows(nc, k, zs)
        transform(nc, "tm", k, k.t, w("out_proj_w"), "rows", table=ys)
        turn(nc, "ty", k, k.t, rows=k.y)
        transform(nc, "tg", k, k.t, w("gat_w"), "gat", table=table, heads=(w("gat_a_src"), w("gat_a_tgt")))
        k.rows = sb("rows", [P, NT, D])
        with nc.sbuf_tensor("ev", [P, SP_, HEADS], F32) as ev, nc.sbuf_tensor("ag", [P, NT, D + HEADS], F32) as ag:
            edge_scores(nc, k, by_dst, stable, ev)
            attend(nc, k, by_dst, table, ev, ag)
            local_rows(nc, k, ag, w("gat_b"))
        affine_norm(nc, "nl", k, k.rows, w("ln_local_g"), w("ln_local_b"), k.rows, False)
        turn(nc, "tl", k, k.t, rows=k.rows)
        fetch_rows(nc, k, ys)
        affine_norm(nc, "ng", k, k.rows, w("ln_global_g"), w("ln_global_b"), k.rows, False)
        with nc.sbuf_tensor("t2", [P, KD, NP], F32) as t2:
            turn(nc, "tt", k, t2, rows=k.rows)
            gate_and_feed(nc, k, t2, w("wl"), w("wg"), w("ff1_w"), w("ff1_b"), w("ff2_w"), w("ff2_b"))
        turn_back(nc, "tb", k, k.t, k.y)
        affine_norm(nc, "n2g", k, k.y, w("ln2_g"), w("ln2_b"), k.x, True)


class Keep:
    pass


def program(nc, a, out, upto=99, start=0):
    k = Keep()
    with ExitStack() as ctx:
        def sb(name, shape, dt=F32):
            return ctx.enter_context(nc.sbuf_tensor(name, shape, dt))

        def dram(name, shape, dt=F32):
            return nc.dram_tensor(name, shape, dt).ap()

        k.x, k.y, k.t = sb("x_sb", [P, NT, D]), sb("y_sb", [P, NT, D]), sb("t_sb", [P, KD, NP])
        k.ident, k.before, k.ones, k.onesmask = (sb(n, [P, P]) for n in ("ident", "before", "ones", "onesmask"))
        k.iota, k.onerow = sb("iota", [P, SP_]), sb("onerow", [P, EC])
        k.pnum, k.pnum_i, k.lastmask = sb("pnum", [P, 1]), sb("pnum_i", [P, 1], I32), sb("lastmask", [P, 1])
        k.dinv, k.deg_in, k.deg_out = sb("dinv", [P, NT]), sb("deg_in", [P, NT]), sb("deg_out", [P, NT])
        by_src = (sb("s_gi", [P, SP_], U32), sb("s_kl", [P, SP_]), sb("s_wl", [P, SP_]), sb("s_own", [1, SP_], I32))
        by_dst = (sb("d_gi", [P, SP_], U32), sb("d_kl", [P, SP_]), None, sb("d_own", [1, SP_], I32))
        k.lg, k.expert, k.small = sb("lg", [P, NT, 8]), sb("expert", [P, NT, 9]), sb("small", [P, NT])
        k.coef, k.back = sb("coef", [P, 3 * NT]), sb("back", [P, 3 * NT], U32)
        k.block_expert = sb("block_expert", [1, MAX_BLOCKS], I32)
        xbuf, ybuf = dram("xbuf", (MAX_BLOCKS * BLOCK + 3 * NP, D)), dram("ybuf", (MAX_BLOCKS * BLOCK, D))
        RowDma.values.clear()
        nc.row_dma = [ctx.enter_context(nc.semaphore(f"row_dma{j}", n)) for j, n in enumerate(ROW_DMAS)]
        table = dram("table", (NP, D))
        rec_s, rec_d = dram("rec_s", (P * ST, REC), I32), dram("rec_d", (P * ST, REC), I32)

        xs, ys, stable = dram("xs", (NP, D)), dram("ys", (NP, D)), dram("stable", (NP, HEADS))
        zs, bc, vrow = dram("zs", (P, KD, NP)), dram("bc", (2 * STATES, NP)), dram("vrow", (NP,))

        def edges(v):
            return v.rearrange("(p c) -> p c", c=EC)

        load_constants(nc, k, a["x"])
        sort_edges(nc, "es", k, edges(a["src"]), edges(a["dst"]), edges(a["edge_weight"]), rec_s, by_src, k.deg_out)
        if start < 1:
            normalise(nc, "n0", k, table=table)
            aggregate(nc, "a0", k, by_src, table, k.t, True)
            transform(nc, "t0", k, k.t, a["L0_gnn_WT"], "add")
        if upto <= 1:
            return store(nc, k, out)
        if start < 2:
            normalise(nc, "n1", k, keep=True, dest=k.t)
            logits(nc, "g1", k, D, a["L0_ffn_gate_w"], a["L0_ffn_gate_b"], 8, k.lg[:, :, 0:8])
            route(nc, "r1", k, k.lg[:, :, 0:8], 8, "capacity", xbuf, 16)
            expert_blocks(nc, "e1", k, xbuf, ybuf, 16, [(a["L0_ffn_w1"], a["L0_ffn_b1"], ACT.Relu)], (a["L0_ffn_w2"], a["L0_ffn_b2"]))
            combine(nc, "c1", k, ybuf[0:16 * BLOCK, :], 1)
        if upto <= 2:
            return store(nc, k, out)
        sort_edges(nc, "ed", k, edges(a["dst"]), edges(a["src"]), edges(a["edge_weight"]), rec_d, by_dst, k.deg_in)
        degrees(nc, k)
        if start < 3:
            normalise(nc, "n2", k, scale=k.dinv, table=table, dest=k.t)
            for l in range(3):
                aggregate(nc, f"a2{l}", k, by_dst, table, k.t, False)
                transform(nc, f"t2{l}", k, k.t, a["L1_gnn_W"][l], "next" if l < 2 else "last", a["L1_gnn_b"][l], table)
        if upto <= 3:
            return store(nc, k, out)
        if start < 4:
            normalise(nc, "n3", k, keep=True, dest=k.t)
            logits(nc, "g3", k, D, a["L1_ffn_Wr"], None, 8, k.lg[:, :, 0:8])
            nb = block_count(3 * N_NODES, 9)
            route(nc, "r3", k, k.lg[:, :, 0:8], 8, "shared", xbuf, nb)
            expert_blocks(nc, "e3", k, xbuf, ybuf, nb, [(a["L1_ffn_W1"], a["L1_ffn_b1"], ACT.Gelu)], (a["L1_ffn_W2"], a["L1_ffn_b2"]))
            combine(nc, "c3", k, ybuf[0:nb * BLOCK, :], 3)
        if upto <= 4:
            return store(nc, k, out)
        if start < 5:
            normalise(nc, "n4", k, scale=k.dinv, table=table, dest=k.t)
            aggregate(nc, "a4", k, by_dst, table, k.t, False)
            transform(nc, "t4", k, k.t, a["L2_gnn_WT"], "keep", a["L2_gnn_b"])
            batch_norm(nc, k, a["L2_gnn_gamma"], a["L2_gnn_beta"])
        if upto <= 5:
            return store(nc, k, out)
        if start < 6:
            normalise(nc, "n5", k, keep=True, dest=k.t)
            logits(nc, "g5", k, P, a["L2_ffn_router_w2"], a["L2_ffn_router_b2"], 6, k.lg[:, :, 0:6], ACT.Relu, a["L2_ffn_router_w1"], a["L2_ffn_router_b1"])
            nb = block_count(2 * N_NODES, 6)
            route(nc, "r5", k, k.lg[:, :, 0:6], 6, "soft2", xbuf, nb)
            expert_blocks(nc, "e5", k, xbuf, ybuf, nb, [(a["L2_ffn_expert_w1"], a["L2_ffn_expert_b1"], ACT.Relu), (a["L2_ffn_expert_w2"], a["L2_ffn_expert_b2"], ACT.Relu)],
                          (a["L2_ffn_expert_w3"], a["L2_ffn_expert_b3"]))
            combine(nc, "c5", k, ybuf[0:nb * BLOCK, :], 2)
        if upto <= 6:
            return store(nc, k, out)
        if start < 7:
            attention_layer(nc, k, a, by_dst, (xs, ys, zs, bc, vrow, table, stable))
        if upto <= 7:
            return store(nc, k, out)
        normalise(nc, "n7", k, keep=True, dest=k.t)
        logits(nc, "g7", k, 1024, a["L3_ffn_Wg"], a["L3_ffn_bg"], 8, k.lg[:, :, 0:8], ACT.Gelu, a["L3_ffn_W1"], a["L3_ffn_b1"])
        nb = block_count(N_NODES, 8)
        route(nc, "r7", k, k.lg[:, :, 0:8], 8, "top1", xbuf, nb)
        expert_blocks(nc, "e7", k, xbuf, ybuf, nb, [(a["L3_ffn_W1"].unsqueeze(0), a["L3_ffn_b1"].unsqueeze(0), ACT.Gelu)], (a["L3_ffn_Wd"], a["L3_ffn_bd"]))
        combine(nc, "c7", k, ybuf[0:nb * BLOCK, :], 1)
        store(nc, k, out)


def store(nc, k, out):
    with Phase(nc, "out") as ph:
        done = ph.sems("done", 2, "hardware")
        with nc.Block() as b:
            @b.sync
            def _(sp):
                sp.dma_start(out[0:(NT - 1) * P, :].rearrange("(t p) d -> p t d", p=P), k.x[:, 0:NT - 1, :]).then_inc(done[0], 16)
                sp.dma_start(out[(NT - 1) * P:N_NODES, :], k.x[0:LAST, NT - 1, :]).then_inc(done[1], 16)
                sp.wait_ge(done[0], 16)
                sp.wait_ge(done[1], 16)


_TRANSPOSED = ("L0_gnn_W", "L2_gnn_W")
_L3_TRANSPOSED = ("gat_w", "in_proj_w", "x_proj_w", "dt_proj_w", "out_proj_w", "wl", "wg", "ff1_w", "ff2_w")
_L3_BY_PARTITION = ("conv_b", "dt_proj_b", "D_param", "ff1_b", "ff2_b")


def host_layout(inputs):
    import numpy as np
    arrays = {}
    for name, v in inputs.items():
        v = np.asarray(v)
        if name in _TRANSPOSED:
            name, v = name + "T", v.T
        arrays[name] = np.ascontiguousarray(v)
    for n in ("L0_ffn_b1", "L1_ffn_b1s", "L1_ffn_b1p", "L2_ffn_expert_b1", "L2_ffn_expert_b2", "L2_ffn_router_b1", "L3_ffn_b1"):
        v = arrays[n]
        arrays[n] = np.ascontiguousarray(np.swapaxes(v.reshape(v.shape[:-1] + (-1, P)), -1, -2))
    for n in _L3_TRANSPOSED:
        arrays["L3_gnn_" + n] = np.ascontiguousarray(arrays["L3_gnn_" + n].T)
    for n in _L3_BY_PARTITION:
        arrays["L3_gnn_" + n] = np.ascontiguousarray(arrays["L3_gnn_" + n].reshape(-1, P).T)
    noise = np.zeros(NP, arrays["node_vec"].dtype)
    noise[:N_NODES] = arrays["node_vec"]
    arrays["node_vec"] = np.ascontiguousarray(noise.reshape(NT, P).T)
    for n in ("W1", "b1", "W2", "b2"):
        shared, private = arrays.pop(f"L1_ffn_{n}s"), arrays.pop(f"L1_ffn_{n}p")
        arrays[f"L1_ffn_{n}"] = np.concatenate([private, shared[None]], axis=0)
    return arrays


def kernel(**inputs):
    import numpy as np
    import concourse.bacc as bacc
    from concourse.bass_utils import run_bass_kernel_spmd

    nc = bacc.Bacc("TRN2", target_bir_lowering=False, num_devices=1)
    arrays, args = {}, {}
    for name, v in host_layout(inputs).items():
        arrays[f"in_{name}"] = v
        args[name] = nc.dram_tensor(f"in_{name}", v.shape, mybir.dt.from_np(v.dtype), kind="ExternalInput").ap()
    out = nc.dram_tensor("out_x", (N_NODES, D), F32, kind="ExternalOutput").ap()
    program(nc, args, out)
    r = run_bass_kernel_spmd(nc, [arrays], core_ids=[0])
    return r.results[0]["out_x"]
```

```python
from contextlib import ExitStack

import concourse.bass as bass
from concourse import mybir

ALU = mybir.AluOpType
ACT = mybir.ActivationFunctionType
F32 = mybir.dt.float32
BF16 = mybir.dt.bfloat16
I32 = mybir.dt.int32
U32 = mybir.dt.uint32
AX_X = mybir.AxisListType.X
RMAX = bass.bass_isa.ReduceOp.max

P = 128
N_NODES = 3125
D = 256
KD = D // P
NT = (N_NODES + P - 1) // P
NP = NT * P
LAST = N_NODES - (NT - 1) * P
G = 5
NG = NT // G
N_EDGES = 50000
EP, EC = 125, 400
SLOT_TILES = (N_EDGES + NT * (P - 1)) // P
RING = 16
HALF = RING // 2
ST = (SLOT_TILES + RING - 1) // RING * RING
SP_ = ST + RING
REC = 4
CAP = 489
CAP_ROWS = 512
MAX_BLOCKS = 48
HEADS, STATES, TAPS, RANK = 4, 16, 4, 16
ds, ts = bass.ds, bass.ts

SEMAPHORES = {"hardware": range(124, 150), "engine": range(150, 250)}
ROW_DMAS = range(100, 100 + RING + 2)


class Phase:

    def __init__(self, nc, name):
        self.nc, self.name, self.ctx, self.nums = nc, name, ExitStack(), []
        self.free = {kind: iter(numbers) for kind, numbers in SEMAPHORES.items()}

    def __enter__(self):
        return self

    def sem(self, name, kind="engine"):
        s = self.ctx.enter_context(self.nc.semaphore(f"{self.name}_{name}", next(self.free[kind])))
        self.nums.append(s.num)
        return s

    def sems(self, name, n, kind="engine"):
        return [self.sem(f"{name}{i}", kind) for i in range(n)]

    def row_dmas(self, n, each):
        return [RowDma(self.nc, j, each) for j in range(n)]

    def sb(self, name, shape, dt=F32):
        return self.ctx.enter_context(self.nc.sbuf_tensor(f"{self.name}_{name}", shape, dt))

    def ps(self, name, shape, dt=F32):
        return self.ctx.enter_context(self.nc.psum_tensor(f"{self.name}_{name}", shape, dt))

    def __exit__(self, kind, value, tb):
        if kind is None:
            lo, hi = min(self.nums), max(self.nums)
            self.nc.all_engine_barrier(sems_to_clear=range(lo, hi + 1))
            self.ctx.close()
        return False


class RowDma:

    values = {}

    def __init__(self, nc, j, each):
        self.sem = nc.row_dma[j]
        self.start = self.values.get(j, 0)
        self.values[j] = self.start + each

    def wait(self, eng, count):
        eng.wait_ge(self.sem, self.start + count)


class Chain:

    def __init__(self, eng, sem):
        self.eng, self.sem, self.n = eng, sem, 0

    def __call__(self, ins):
        self.n += 1
        ins.then_inc(self.sem, 1)
        self.eng.wait_ge(self.sem, self.n)


def load_constants(nc, k, x):
    with Phase(nc, "init") as ph:
        ld, dv, gp = ph.sems("ld", 2, "hardware"), ph.sem("dv"), ph.sem("gp")
        ii = ph.sb("ii", [P, SP_], I32)
        ei = ph.sb("ei", [P, NT, 9], I32)
        with nc.Block() as b:
            @b.sync
            def _(sp):
                sp.dma_start(k.x[:, 0:NT - 1, :], x[0:(NT - 1) * P, :].rearrange("(t p) d -> p t d", p=P)).then_inc(ld[0], 16)
                sp.wait_ge(dv, 1)
                sp.dma_start(k.x[0:LAST, NT - 1, :], x[(NT - 1) * P:N_NODES, :]).then_inc(ld[1], 16)
                sp.wait_ge(ld[0], 16)
                sp.wait_ge(ld[1], 16)

            @b.vector
            def _(v):
                v.memset(k.x[:, NT - 1, :], 0.0).then_inc(dv, 1)
                v.memset(k.ones[:, :], 1.0)
                v.memset(k.back[:, :], 0)
                v.memset(k.onerow[:, :], 1.0).then_inc(dv, 1)
                v.wait_ge(gp, 5)
                v.tensor_copy(k.iota[:, :], ii[:, 0:SP_]).then_inc(dv, 1)
                v.wait_ge(gp, 7)
                v.tensor_copy(k.expert[:, :, :], ei[:, :, :])
                v.tensor_copy(k.pnum[:, :], k.pnum_i[:, :]).then_inc(dv, 1)
                v.wait_ge(dv, 4)
                v.tensor_scalar(k.lastmask[:, :], k.pnum[:, :], float(LAST), None, ALU.is_lt).then_inc(dv, 1)
                v.wait_ge(dv, 5)
                v.tensor_scalar(k.onesmask[:, :], k.ones[:, :], k.lastmask[:, 0:1], None, ALU.mult).then_inc(dv, 1)

            @b.gpsimd
            def _(g):
                g.memset(k.ident[:, :], 0.0).then_inc(gp, 1)
                g.memset(k.before[:, :], 0.0).then_inc(gp, 1)
                g.wait_ge(gp, 2)
                g.affine_select(out=k.ident[:, :], in_=k.ident[:, :], compare_op=ALU.not_equal, fill=1.0,
                                base=0, pattern=[[-1, P]], channel_multiplier=1).then_inc(gp, 1)
                g.affine_select(out=k.before[:, :], in_=k.before[:, :], compare_op=ALU.is_ge, fill=1.0,
                                base=0, pattern=[[-1, P]], channel_multiplier=1).then_inc(gp, 1)
                g.iota(ii[:, :], pattern=[[1, SP_]], base=0, channel_multiplier=0).then_inc(gp, 1)
                g.wait_ge(gp, 5)
                g.iota(ei[:, :, :], pattern=[[0, NT], [1, 9]], base=0, channel_multiplier=0).then_inc(gp, 1)
                g.iota(k.pnum_i[:, :], pattern=[[0, 1]], base=0, channel_multiplier=1).then_inc(gp, 1)


class SlotScatter:

    STEPS = EC // RING

    def __init__(self, nc, name, memory, rec, lists, degree):
        def sb(n, shape, dt):
            return memory.enter_context(nc.sbuf_tensor(f"{name}_{n}", shape, dt))

        self.nc, self.name, self.rec, self.lists, self.degree = nc, name, rec, lists, degree
        self.recs, self.tgt = sb("recs", [EP, EC, REC], I32), sb("tgt", [EP, EC], U32)
        self.tstage, self.rstage = sb("tstage", [EP, RING], U32), sb("rstage", [EP, RING, REC], I32)
        self.done = 0

    def take(self, ph, steps):
        self.first, self.done = self.done, self.done + steps
        self.placed = [RowDma(self.nc, RING + h, 16 * HALF * steps) for h in range(2)]
        self.staged, self.passed = ph.sem(self.name + "_staged"), ph.sem(self.name + "_passed")

    def step(self, g, i):
        for h in range(2):
            self.placed[h].wait(g, 16 * HALF * i)
            g.sem_inc(self.passed, 1)
            col = (self.first + i) * RING + h * HALF
            g.tensor_copy(self.tstage[:, h * HALF:(h + 1) * HALF], self.tgt[:, ds(col, HALF)]).then_inc(self.staged, 1)
            g.tensor_copy(self.rstage[:, h * HALF:(h + 1) * HALF, :], self.recs[:, ds(col, HALF), :]).then_inc(self.staged, 1)
            g.wait_ge(self.staged, 4 * i + 2 * h + 2)
            g.sem_inc(self.passed, 1)
            for j in range(h * HALF, (h + 1) * HALF):
                g.indirect_dma_start(self.rec, bass.IndirectOffsetOnAxis(ap=self.tstage[:, j:j + 1], axis=0),
                                     self.rstage[:, j, :], None).then_inc(self.placed[h].sem, 16)

    def steps(self, g, n):
        with g.Fori(0, n) as i:
            self.step(g, i)

    def read_back(self, sp, buf, sem, steps):
        for q in self.placed:
            q.wait(sp, 16 * HALF * steps)
        sp.dma_start(buf[:, :, :].rearrange("p t w -> p (t w)"), self.rec.rearrange("(p t) w -> p (t w)", p=P)).then_inc(sem, 16)
        sp.wait_ge(sem, 16)

    def unpack(self, v, c, buf):
        gi, kl, wl, _ = self.lists
        c(v.memset(gi[:, ST:SP_], 0))
        c(v.memset(kl[:, ST:SP_], -1.0))
        c(v.tensor_copy(gi[:, 0:ST], buf[:, :, 0]))
        c(v.tensor_copy(kl[:, 0:ST], buf[:, :, 1].bitcast(F32)))
        if wl is not None:
            c(v.memset(wl[:, ST:SP_], 0.0))
            c(v.tensor_copy(wl[:, 0:ST], buf[:, :, 2].bitcast(F32)))


ZERO_ROWS = 8


def sort_edges(nc, k, src, dst, weight, by_src, by_dst, xbuf):
    with Phase(nc, "es") as ph:
        sorts = ((by_src, 0, 1), (by_dst, 1, 0))
        by_src.take(ph, by_src.STEPS)
        ld, fill, back = ph.sems("ld", 3, "hardware"), ph.sem("fill", "hardware"), ph.sem("back", "hardware")
        cleared = ph.sem("cleared", "hardware")
        zeros = ph.sb("zeros", [P, ZERO_ROWS * D])
        dve, slots = ph.sem("dve"), ph.sem("slots")
        cnt_ready, off_ready, dege, counted = (ph.sems(n, 2) for n in ("cnt", "off", "dege", "counted"))
        keys = [ph.sb(n, [EP, EC], I32) for n in ("src", "dst")]
        wt = ph.sb("wt", [EP, EC])
        hi_i, hi, lo = ph.sb("hi_i", [EP, EC], I32), ph.sb("hi", [EP, EC]), ph.sb("lo", [EP, EC])
        oh, sc, pos = ph.sb("oh", [EP, G, EC]), ph.sb("sc", [EP, G, EC]), ph.sb("pos", [EP, EC])
        pos_i = ph.sb("pos_i", [EP, EC], I32)
        cnt = ph.sb("cnt", [EP, NT])
        offb, nt_i, nt, endt, start = ph.sb("offb", [P, NT]), ph.sb("nt_i", [P, NT], I32), ph.sb("nt", [P, NT]), ph.sb("endt", [P, NT]), ph.sb("start", [P, NT])
        ow = ph.sb("ow", [1, SP_])
        empty = ph.sb("empty", [P, ST, REC], I32)
        ohlo, ohhi, zero = ph.sb("ohlo", [EP, RING, P], BF16), ph.sb("ohhi", [EP, RING, NT], BF16), ph.sb("zero", [EP, P], BF16)
        pt = ph.ps("pt", [P, 2, 512])
        pdeg = ph.ps("pdeg", [P, 512])
        iters = EC // RING
        with nc.Block() as b:
            @b.sync
            def _(sp):
                for buf, v, s in ((keys[0], src, ld[0]), (keys[1], dst, ld[1]), (wt, weight, ld[2])):
                    sp.dma_start(buf[:, :], v).then_inc(s, 16)
                sp.wait_ge(dve, 3)
                for sort in (by_src, by_dst):
                    sp.dma_start(sort.rec.rearrange("(p t) w -> p (t w)", p=P), empty[:, :, :].rearrange("p t w -> p (t w)")).then_inc(fill, 16)
                for r in range(0, xbuf.shape[0], P * ZERO_ROWS):
                    n = min(P * ZERO_ROWS, xbuf.shape[0] - r) // P
                    sp.dma_start(xbuf[r:r + n * P, :].rearrange("(p t) d -> p (t d)", p=P), zeros[:, 0:n * D]).then_inc(cleared, 16)
                sp.wait_ge(cleared, 16 * -(-xbuf.shape[0] // (P * ZERO_ROWS)))
                sp.wait_ge(fill, 32)
                by_src.read_back(sp, empty, back, by_src.STEPS)

            @b.vector
            def _(v):
                c = Chain(v, dve)
                c(v.memset(empty[:, :, :].rearrange("p t w -> p (t w)"), 0))
                c(v.memset(empty[:, :, 1].bitcast(F32), -1.0))
                c(v.memset(zeros[:, :], 0.0))
                c(v.memset(zero[:, :], 0.0))
                for s in ld:
                    v.wait_ge(s, 16)
                for q, (sort, key, val) in enumerate(sorts):
                    c(v.tensor_scalar(hi_i[:, :], keys[key][:, :], 7, None, ALU.arith_shift_right))
                    c(v.tensor_copy(hi[:, :], hi_i[:, :]))
                    c(v.tensor_scalar(hi_i[:, :], keys[key][:, :], P - 1, None, ALU.bitwise_and))
                    c(v.tensor_copy(lo[:, :], hi_i[:, :]))
                    c(v.memset(pos[:, :], 0.0))
                    c(v.memset(sort.recs[:, :, 3], 0))
                    c(v.tensor_copy(sort.recs[:, :, 0], keys[val][:, :]))
                    c(v.tensor_copy(sort.recs[:, :, 1].bitcast(F32), lo[:, :]))
                    c(v.tensor_copy(sort.recs[:, :, 2].bitcast(F32), wt[:, :]))
                    with v.Fori(0, NG) as i:
                        v.wait_ge(cnt_ready[q], i * G)
                        for j in range(G):
                            v.tensor_scalar(oh[:, j, :], hi[:, :], k.iota[0:EP, ds(i * G + j, 1)], None, ALU.is_equal, ALU.add,
                                            accum_out=cnt[:, ds(i * G + j, 1)]).then_inc(cnt_ready[q], 1)
                    v.wait_ge(off_ready[q], 1)
                    c(v.tensor_copy(nt[:, :], pt[:, 1, 0:NT]))
                    c(v.tensor_scalar(nt[:, :], nt[:, :], float(P - 1), None, ALU.add))
                    c(v.tensor_copy(nt_i[:, :], nt[:, :]))
                    c(v.tensor_scalar(nt_i[:, :], nt_i[:, :], 7, None, ALU.arith_shift_right))
                    c(v.tensor_copy(nt[:, :], nt_i[:, :]))
                    c(v.tensor_tensor_scan(endt[:, :], k.ones[:, 0:NT], nt[:, :], 0.0, ALU.mult, ALU.add))
                    c(v.tensor_tensor(start[:, :], endt[:, :], nt[:, :], ALU.subtract))
                    c(v.tensor_scalar(offb[:, :], start[:, :], float(P), -1.0, ALU.mult, ALU.add))
                    c(v.tensor_tensor(offb[:, :], offb[:, :], pt[:, 0, 0:NT], ALU.add))
                    n = c.n
                    with v.Fori(0, NG) as i:
                        at = n + i * 4 * G
                        v.wait_ge(dve, at)
                        for j in range(G):
                            v.tensor_scalar(oh[:, j, :], hi[:, :], k.iota[0:EP, ds(i * G + j, 1)], None, ALU.is_equal).then_inc(dve, 1)
                        for j in range(G):
                            v.wait_ge(dve, at + j + 1)
                            v.tensor_tensor_scan(sc[:, j, :], k.onerow[0:EP, 0:EC], oh[:, j, :], 0.0, ALU.mult, ALU.add).then_inc(dve, 1)
                        for j in range(G):
                            v.wait_ge(dve, at + G + j + 1)
                            v.scalar_tensor_tensor(sc[:, j, :], sc[:, j, :], offb[0:EP, ds(i * G + j, 1)], oh[:, j, :], ALU.add, ALU.mult).then_inc(dve, 1)
                        for j in range(G):
                            v.wait_ge(dve, at + 3 * G + j)
                            v.tensor_tensor(pos[:, :], pos[:, :], sc[:, j, :], ALU.add).then_inc(dve, 1)
                    c.n = n + 4 * NT
                    v.wait_ge(dve, c.n)
                    c(v.tensor_copy(pos_i[:, :], pos[:, :]))
                    c(v.tensor_scalar(hi_i[:, :], pos_i[:, :], P - 1, None, ALU.bitwise_and))
                    c(v.tensor_scalar(pos_i[:, :], pos_i[:, :], 7, None, ALU.arith_shift_right))
                    c(v.tensor_copy(sc[:, 0, :], hi_i[:, :]))
                    c(v.tensor_copy(sc[:, 1, :], pos_i[:, :]))
                    c(v.scalar_tensor_tensor(pos[:, :], sc[:, 0, :], float(ST), sc[:, 1, :], ALU.mult, ALU.add))
                    c(v.tensor_copy(sort.tgt[:, :], pos[:, :]))
                    v.sem_inc(slots, 1)
                    c(v.memset(ow[:, :], -1.0))
                    n = c.n
                    with v.Fori(0, NG) as i:
                        for j in range(G):
                            v.wait_ge(dve, n + i * G + j)
                            v.scalar_tensor_tensor(ow[:, :], k.iota[0:1, :], start[0:1, ds(i * G + j, 1)], ow[:, :], ALU.is_ge, ALU.add).then_inc(dve, 1)
                    c.n = n + NT
                    v.wait_ge(dve, c.n)
                    c(v.tensor_copy(sort.lists[3][:, :], ow[:, :]))
                    with v.Fori(0, iters) as i:
                        v.wait_ge(counted[q], i)
                        for j in range(RING):
                            v.tensor_scalar(ohlo[:, j, :], k.iota[0:EP, 0:P], lo[:, ds(i * RING + j, 1)], None, ALU.is_equal)
                            v.tensor_scalar(ohhi[:, j, :], k.iota[0:EP, 0:NT], hi[:, ds(i * RING + j, 1)], None, ALU.is_equal).then_inc(dege[q], 1)
                    v.wait_ge(counted[q], iters + 1)
                    c(v.tensor_copy(sort.degree[:, :], pdeg[:, 0:NT]))
                v.wait_ge(back, 16)
                by_src.unpack(v, c, empty)

            @b.tensor
            def _(pe):
                for q in range(2):
                    pe.wait_ge(cnt_ready[q], NT)
                    pe.matmul(pt[0:P, 0, 0:NT], k.before[0:EP, :], cnt[:, :], start=True, stop=True)
                    pe.matmul(pt[0:P, 1, 0:NT], k.ones[0:EP, :], cnt[:, :], start=True, stop=True).then_inc(off_ready[q], 1)
                    pe.matmul(pdeg[:, 0:NT], zero[:, :], zero[:, 0:NT], start=True, stop=False)
                    with pe.Fori(0, iters) as i:
                        for j in range(RING):
                            pe.wait_ge(dege[q], i * RING + j + 1)
                            mm = pe.matmul(pdeg[:, 0:NT], ohlo[:, j, :], ohhi[:, j, :], start=False, stop=False)
                        mm.then_inc(counted[q], 1)
                    pe.matmul(pdeg[:, 0:NT], zero[:, :], zero[:, 0:NT], start=False, stop=True).then_inc(counted[q], 1)

            @b.gpsimd
            def _(g):
                g.wait_ge(fill, 32)
                g.wait_ge(slots, 1)
                by_src.steps(g, by_src.STEPS)


def finish_sort(nc, sort, k):
    with Phase(nc, "ed") as ph:
        steps = sort.STEPS - sort.done
        sort.take(ph, steps)
        back, dve = ph.sem("back", "hardware"), ph.sem("dve")
        buf = ph.sb("buf", [P, ST, REC], I32)
        with nc.Block() as b:
            @b.gpsimd
            def _(g):
                sort.steps(g, steps)

            @b.sync
            def _(sp):
                sort.read_back(sp, buf, back, steps)

            @b.vector
            def _(v):
                v.wait_ge(back, 16)
                sort.unpack(v, Chain(v, dve), buf)


def normalise(nc, name, k, scale=None, table=None, keep=False, dest=None, eps=1e-5, beside=None, steps=0):
    with Phase(nc, name) as ph:
        dve, root, ready = ph.sem("dve"), ph.sem("root"), ph.sem("ready")
        tdone, evac, stored = ph.sems("tdone", G), ph.sems("evac", G), ph.sems("stored", G, "hardware")
        st = ph.sb("st", [P, NT, 6])
        mean, var, dif, rstd = (ph.sb(n, [P, NT]) for n in ("mean", "var", "dif", "rstd"))
        stage = ph.sb("stage", [P, G, D])
        pt = ph.ps("pt", [P, G, 512])
        if beside:
            beside.take(ph, steps)
        with nc.Block() as b:
            if beside:
                @b.gpsimd
                def _(g):
                    beside.steps(g, steps)

            @b.vector
            def _(v):
                with v.Fori(0, NG) as i:
                    for j in range(G):
                        v.bn_stats(st[:, ds(i * G + j, 1), :], k.x[:, ds(i * G + j, 1), :]).then_inc(dve, 1)
                v.wait_ge(dve, NT)
                c = Chain(v, dve)
                c.n = NT
                c(v.tensor_tensor(mean[:, :], st[:, :, 1], st[:, :, 4], ALU.add))
                c(v.tensor_scalar(mean[:, :], mean[:, :], 0.5, None, ALU.mult))
                c(v.tensor_tensor(dif[:, :], st[:, :, 1], st[:, :, 4], ALU.subtract))
                c(v.tensor_tensor(dif[:, :], dif[:, :], dif[:, :], ALU.mult))
                c(v.tensor_scalar(dif[:, :], dif[:, :], 0.25, eps, ALU.mult, ALU.add))
                c(v.tensor_tensor(var[:, :], st[:, :, 2], st[:, :, 5], ALU.add))
                c(v.scalar_tensor_tensor(var[:, :], var[:, :], 1.0 / D, dif[:, :], ALU.mult, ALU.add))
                v.wait_ge(root, 1)
                c(v.reciprocal(rstd[:, :], rstd[:, :]))
                if scale is not None:
                    c(v.tensor_tensor(rstd[:, :], rstd[:, :], scale[:, :], ALU.mult))
                with v.Fori(0, NG) as i:
                    for j in range(G):
                        t = i * G + j
                        if dest is not None:
                            v.wait_ge(tdone[j], i)
                        if table is not None:
                            v.wait_ge(stored[j], 16 * i)
                        if dest is not None or table is not None:
                            v.tensor_scalar(stage[:, j, :], k.x[:, ds(t, 1), :].rearrange("p a d -> p (a d)"), mean[:, ds(t, 1)], rstd[:, ds(t, 1)],
                                            ALU.subtract, ALU.mult).then_inc(ready, 1)
                        if keep:
                            v.tensor_scalar(k.y[:, ds(t, 1), :].rearrange("p a d -> p (a d)"), k.x[:, ds(t, 1), :].rearrange("p a d -> p (a d)"), mean[:, ds(t, 1)], rstd[:, ds(t, 1)],
                                            ALU.subtract, ALU.mult)

            @b.scalar
            def _(a):
                a.wait_ge(dve, NT + 7)
                a.activation(rstd[:, :], var[:, :], ACT.Sqrt).then_inc(root, 1)
                if dest is not None:
                    with a.Fori(0, NG) as i:
                        for j in range(G):
                            a.wait_ge(tdone[j], i + 1)
                            a.copy(dest[:, :, ds((i * G + j) * P, P)], pt[:, j, 0:D].rearrange("p (k n) -> p k n", k=KD)).then_inc(evac[j], 1)

            if dest is not None:
                @b.tensor
                def _(pe):
                    with pe.Fori(0, NG) as i:
                        for j in range(G):
                            pe.wait_ge(ready, i * G + j + 1)
                            pe.wait_ge(evac[j], i)
                            for q in range(KD):
                                mm = pe.transpose(pt[:, j, q * P:(q + 1) * P], stage[:, j, q * P:(q + 1) * P], k.ident[:, :])
                            mm.then_inc(tdone[j], 1)

            if table is not None:
                @b.sync
                def _(sp):
                    with sp.Fori(0, NG) as i:
                        for j in range(G):
                            sp.wait_ge(ready, i * G + j + 1)
                            sp.dma_start(table[ds((i * G + j) * P, P), 0:D], stage[:, j, :]).then_inc(stored[j], 16)
                    for s in stored:
                        sp.wait_ge(s, 16 * NG)


def load_tiles(eng, registers, own, first):
    eng.load(registers, own[0:1, ds(first, len(registers))])
    return [eng.snap(r, min_val=0, max_val=NT - 1) for r in registers]


def aggregate(nc, name, k, lists, table, acc, clear):
    gi, kl, wl, own = lists
    iters = ST // RING
    with Phase(nc, name) as ph:
        staged, landed, passed = ph.sem("staged"), ph.row_dmas(RING, 16 * iters), ph.sem("passed")
        oh_ready, summed, added = ph.sem("oh"), ph.sem("summed"), ph.sem("added")
        ix = ph.sb("ix", [P, RING], U32)
        rows, oh = ph.sb("rows", [P, RING, D]), ph.sb("oh", [P, RING, P])
        NB = 4
        pa = ph.ps("pa", [P, NB, 512])
        with nc.Block() as b:
            @b.gpsimd
            def _(g):
                with g.Fori(0, iters) as i:
                    for j in range(RING):
                        if j % HALF == 0:
                            g.wait_ge(staged, 2 * i + j // HALF + 1)
                            g.sem_inc(passed, 1)
                        g.indirect_dma_start(rows[:, j, :], None, table,
                                             bass.IndirectOffsetOnAxis(ap=ix[:, j:j + 1], axis=0)).then_inc(landed[j].sem, 16)

            def one_hots(v, first, h):
                for j in range(h * HALF, (h + 1) * HALF):
                    col = first + j
                    if wl is None:
                        ins = v.tensor_scalar(oh[:, j, :], k.iota[:, 0:P], kl[:, ds(col, 1)], None, ALU.is_equal)
                    else:
                        ins = v.tensor_scalar(oh[:, j, :], k.iota[:, 0:P], kl[:, ds(col, 1)], wl[:, ds(col, 1)],
                                              ALU.is_equal, ALU.mult)
                    ins.then_inc(oh_ready, 1)

            @b.vector
            def _(v):
                number = [v.alloc_register(f"{name}_tile{j}") for j in range(HALF)]
                if clear:
                    v.memset(acc[:, :, :].rearrange("p k n -> p (k n)"), 0.0).then_inc(added, NB)
                else:
                    v.sem_inc(added, NB)
                v.tensor_copy(ix[:, 0:HALF], gi[:, 0:HALF]).then_inc(staged, 1)
                v.tensor_copy(ix[:, HALF:RING], gi[:, HALF:RING]).then_inc(staged, 1)
                one_hots(v, 0, 0)
                with v.Fori(0, iters) as i:
                    for h in range(2):
                        tiles = load_tiles(v, number, own, i * RING + h * HALF)
                        one_hots(v, i * RING + (RING if h else 0), 1 - h)
                        for j in range(h * HALF, (h + 1) * HALF):
                            tile = tiles[j % HALF]
                            v.wait_ge(summed, i * RING + j + 1)
                            v.wait_ge(added, i * RING + j + NB)
                            v.tensor_tensor(acc[:, :, ts(tile, P)], acc[:, :, ts(tile, P)],
                                            pa[:, j % NB, 0:D].rearrange("p (k n) -> p k n", k=KD), ALU.add).then_inc(added, 1)
                        v.tensor_copy(ix[:, h * HALF:(h + 1) * HALF], gi[:, ds(i * RING + RING + h * HALF, HALF)]).then_inc(staged, 1)

            @b.tensor
            def _(pe):
                with pe.Fori(0, iters) as i:
                    for j in range(RING):
                        landed[j].wait(pe, 16 * i + 16)
                        pe.wait_ge(oh_ready, i * RING + j + 1)
                        pe.wait_ge(added, i * RING + j + 1)
                        for q in range(KD):
                            mm = pe.matmul(pa[:, j % NB, q * P:(q + 1) * P], rows[:, j, q * P:(q + 1) * P], oh[:, j, :],
                                           start=True, stop=True)
                        mm.then_inc(summed, 1)


def transform(nc, name, k, acc, w, mode, bias=None, table=None, heads=None, scores=None, beside=None, steps=0):
    with Phase(nc, name) as ph:
        ld, inn, mul, fin, passed = ph.sems("ld", 2, "hardware"), ph.sems("inn", G), ph.sems("mul", G), ph.sem("fin"), ph.sem("passed")
        free, ready = ph.sems("free", G), ph.sem("ready")
        tdone, evac, stored = ph.sems("tdone", G), ph.sem("evac"), ph.sems("stored", G, "hardware")
        wsb = ph.sb("w", [P, KD, D])
        ast = ph.sb("ast", [P, G, KD, P])
        tmp, out = ph.sb("tmp", [P, G, D]), ph.sb("out", [P, G, D])
        bb = ph.sb("bb", [P, D])
        if mode == "gat":
            head, both = ph.sb("head", [P, 2, D]), ph.sb("both", [P, 2, G, D])
        pz = ph.ps("pz", [P, G, 512])

        def slot(j):
            return pz[:, j, D:2 * D]

        def row(buf, t):
            return buf[:, ds(t, 1), :].rearrange("p a d -> p (a d)")

        if beside:
            beside.take(ph, steps)
        with nc.Block() as b:
            if beside:
                @b.gpsimd
                def _(g):
                    beside.steps(g, steps)

            @b.sync
            def _(sp):
                sp.dma_start(wsb[:, :, :], w.rearrange("(k p) n -> p k n", p=P)).then_inc(ld[0], 16)
                if bias is not None:
                    sp.dma_start(bb[:, :], bias.partition_broadcast(P)).then_inc(ld[1], 16)
                if mode == "gat":
                    for q in range(2):
                        sp.dma_start(head[:, q, :], heads[q].rearrange("h f -> (h f)").partition_broadcast(P)).then_inc(ld[1], 16)
                if mode in ("next", "rows", "gat"):
                    with sp.Fori(0, NG) as i:
                        for j in range(G):
                            sp.wait_ge(ready, i * G + j + 1)
                            sp.dma_start(table[ds((i * G + j) * P, P), :], out[:, j, :]).then_inc(stored[j], 16)
                    for s in stored:
                        sp.wait_ge(s, 16 * NG)
                if mode == "gat":
                    sp.wait_ge(fin, 4 * NT)
                    sp.dma_start(scores.rearrange("(t p) h -> p t h", p=P), k.score[:, :, 0, :]).then_inc(ld[1], 16)
                    sp.wait_ge(ld[1], 48)

            @b.scalar
            def _(a):
                with a.Fori(0, NG) as i:
                    for j in range(G):
                        a.wait_ge(mul[j], i)
                        a.copy(ast[:, j, :, :], acc[:, :, ds((i * G + j) * P, P)]).then_inc(inn[j], 1)
                    if mode == "next":
                        for j in range(G):
                            a.wait_ge(tdone[j], i + 1)
                            a.sem_inc(passed, 1)
                            a.copy(acc[:, :, ds((i * G + j) * P, P)], slot(j).rearrange("p (k n) -> p k n", k=KD)).then_inc(evac, 1)

            @b.tensor
            def _(pe):
                pe.wait_ge(ld[0], 16)
                with pe.Fori(0, NG) as i:
                    if mode == "next":
                        pe.wait_ge(evac, i * G)
                    for j in range(G):
                        pe.wait_ge(inn[j], i + 1)
                        pe.wait_ge(free[j], i)
                        for q in range(KD):
                            mm = pe.matmul(pz[:, j, 0:D], ast[:, j, q, :], wsb[:, q, :], start=q == 0, stop=q == KD - 1)
                        mm.then_inc(mul[j], 1)
                    if mode == "next":
                        for j in range(G):
                            pe.wait_ge(ready, i * G + j + 1)
                            for q in range(KD):
                                mm = pe.transpose(slot(j)[:, q * P:(q + 1) * P], out[:, j, q * P:(q + 1) * P], k.ident[:, :])
                            mm.then_inc(tdone[j], 1)

            @b.vector
            def _(v):
                if bias is not None:
                    v.wait_ge(ld[1], 16)
                if mode == "gat":
                    v.wait_ge(ld[1], 32)
                if mode == "gat":
                    with v.Fori(0, NG) as i:
                        at = i * G * 4
                        for j in range(G):
                            v.wait_ge(mul[j], i + 1)
                            v.wait_ge(stored[j], 16 * i)
                            v.tensor_copy(out[:, j, :], pz[:, j, 0:D]).then_inc(ready, 1)
                            for q in range(2):
                                v.tensor_tensor(both[:, q, j, :], pz[:, j, 0:D], head[:, q, :], ALU.mult).then_inc(fin, 1)
                        for j in range(G):
                            for q in range(2):
                                v.wait_ge(fin, at + 2 * j + q + 1)
                                v.tensor_reduce(k.score[:, ds(i * G + j, 1), q, :].rearrange("p a h -> p (a h)"),
                                                both[:, q, j, :].rearrange("p (h f) -> p h f", h=HEADS), AX_X, ALU.add).then_inc(fin, 1)
                            v.sem_inc(free[j], 1)
                        v.wait_ge(fin, at + 4 * G)
                    return
                with v.Fori(0, NG) as i:
                    if mode in ("next", "last"):
                        v.wait_ge(ready, i * G)
                    for j in range(G):
                        t = i * G + j
                        v.wait_ge(mul[j], i + 1)
                        if mode == "add":
                            v.tensor_tensor(row(k.x, t), row(k.x, t), pz[:, j, 0:D], ALU.add).then_inc(free[j], 1)
                            continue
                        if mode == "rows":
                            v.wait_ge(stored[j], 16 * i)
                            v.tensor_copy(out[:, j, :], pz[:, j, 0:D]).then_inc(ready, 1)
                            v.wait_ge(ready, t + 1)
                            v.sem_inc(free[j], 1)
                            continue
                        if mode == "keep":
                            v.scalar_tensor_tensor(row(k.y, t), pz[:, j, 0:D], k.dinv[:, ds(t, 1)], bb[:, :],
                                                   ALU.mult, ALU.add).then_inc(free[j], 1)
                            continue
                        v.scalar_tensor_tensor(tmp[:, j, :], pz[:, j, 0:D], k.dinv[:, ds(t, 1)], bb[:, :],
                                               ALU.mult, ALU.add).then_inc(free[j], 1)
                        for done in [j] if mode == "next" else ([j - 1] if j else []) + ([j] if j == G - 1 else []):
                            u = i * G + done
                            v.wait_ge(free[done], i + 1)
                            if mode == "next":
                                v.wait_ge(tdone[done], i)
                                v.wait_ge(stored[done], 16 * i)
                                v.tensor_scalar(out[:, done, :], tmp[:, done, :], 0.0, k.dinv[:, ds(u, 1)], ALU.max, ALU.mult).then_inc(ready, 1)
                            else:
                                v.scalar_tensor_tensor(row(k.x, u), tmp[:, done, :], 0.0, row(k.x, u), ALU.max, ALU.add).then_inc(ready, 1)


BLOCK = 2 * P
SHARED_BLOCKS = (NP + BLOCK - 1) // BLOCK


def spread(ap, n):
    return ap.unsqueeze(2).broadcast_to([ap.shape[0], ap.shape[1], n])


def block_count(pairs, experts):
    n = (pairs + experts * (BLOCK - 1)) // BLOCK
    return n + n % 2


def logits(nc, name, k, hidden, w, bias, E, lg, act=None, w_in=None, b_in=None, beside=None, steps=0):
    C = NP // NG
    H = C // 2
    FT = hidden // P
    MB = min(4, 2 * FT)
    with Phase(nc, name) as ph:
        ld = ph.sem("ld", "hardware")
        mid, mid_act = ph.sem("mid"), ph.sem("mid_act")
        passed = ph.sem("passed")
        mul, evac, tr, put = ph.sem("mul"), ph.sem("evac"), ph.sem("tr"), ph.sem("put")
        wsb, bsb = ph.sb("w", [P, FT, E]), ph.sb("b", [E, 1])
        lst = ph.sb("lst", [E, C])
        pl, pt = ph.ps("pl", [P, 2, 512]), ph.ps("pt", [P, 512])
        if w_in is not None:
            win, bin_ = ph.sb("win", [P, KD, hidden]), ph.sb("bin", [P, FT])
            hs = ph.sb("hs", [P, 2, FT, H])
            pm = ph.ps("pm", [P, 4, 512])
        n_ld = 1 + (bias is not None) + 2 * (w_in is not None)
        if beside:
            beside.take(ph, steps)
        with nc.Block() as b:
            if beside:
                @b.gpsimd
                def _(g):
                    beside.steps(g, steps)

            @b.sync
            def _(sp):
                sp.dma_start(wsb[:, :, :], w.rearrange("(f p) e -> p f e", p=P)).then_inc(ld, 16)
                if bias is not None:
                    sp.dma_start(bsb[:, :], bias.rearrange("(e a) -> e a", a=1)).then_inc(ld, 16)
                if w_in is not None:
                    sp.dma_start(win[:, :, :], w_in.rearrange("(k p) f -> p k f", p=P)).then_inc(ld, 16)
                    sp.dma_start(bin_[:, :], b_in).then_inc(ld, 16)

            @b.tensor
            def _(pe):
                pe.wait_ge(ld, 16 * n_ld)
                with pe.Fori(0, NG) as i:
                    for h in range(2):
                        if w_in is not None:
                            for f in range(FT):
                                pe.wait_ge(mid_act, (2 * i + h) * FT + f + 1)
                                for q in range(KD):
                                    mm = pe.matmul(pm[:, (h * FT + f) % MB, 0:H], win[:, q, f * P:(f + 1) * P], k.t[:, q, ds(i * C + h * H, H)],
                                                   start=q == 0, stop=q == KD - 1)
                                mm.then_inc(mid, 1)
                    pe.wait_ge(put, i)
                    for h in range(2):
                        if w_in is not None:
                            pe.wait_ge(mid_act, (2 * i + h + 1) * FT + MB)
                        for f in range(FT):
                            src = k.t[:, f, ds(i * C + h * H, H)] if w_in is None else hs[:, h, f, :]
                            mm = pe.matmul(pl[0:E, h, 0:H], wsb[:, f, :], src, start=f == 0, stop=f == FT - 1)
                    mm.then_inc(mul, 1)
                    pe.wait_ge(evac, i + 1)
                    pe.sem_inc(passed, 1)
                    for j in range(G):
                        mm = pe.transpose(pt[:, j * E:(j + 1) * E], lst[:, j * P:(j + 1) * P], k.ident[0:E, 0:E])
                    mm.then_inc(tr, 1)

            @b.scalar
            def _(a):
                a.sem_inc(mid_act, MB)
                a.wait_ge(ld, 16 * n_ld)
                with a.Fori(0, NG) as i:
                    if w_in is not None:
                        for h in range(2):
                            for f in range(FT):
                                a.wait_ge(mid, (2 * i + h) * FT + f + 1)
                                a.activation(hs[:, h, f, :], pm[:, (h * FT + f) % MB, 0:H], act, bias=bin_[:, f:f + 1]).then_inc(mid_act, 1)
                    a.wait_ge(mul, i + 1)
                    dst = lst[:, :].rearrange("e (h n) -> e h n", h=2)
                    if bias is not None:
                        a.activation(dst, pl[0:E, :, 0:H], ACT.Identity, bias=bsb[:, 0:1]).then_inc(evac, 1)
                    else:
                        a.copy(dst, pl[0:E, :, 0:H]).then_inc(evac, 1)

            @b.vector
            def _(v):
                with v.Fori(0, NG) as i:
                    v.wait_ge(tr, i + 1)
                    v.tensor_copy(lg[:, ds(i * G, G), :], pt[:, 0:G * E].rearrange("p (t e) -> p t e", e=E)).then_inc(put, 1)


def softmax_steps(c, v, k, lg, E, mx, sm, act_in, act_out):
    c(v.tensor_reduce(mx[:, :], lg[:, :, :], AX_X, ALU.max))
    c(v.tensor_tensor(lg[:, :, :], lg[:, :, :], spread(mx[:, :], E), ALU.subtract))
    v.sem_inc(act_in, 1)
    v.wait_ge(act_out, 1)
    c(v.tensor_reduce(sm[:, :], lg[:, :, :], AX_X, ALU.add))
    c(v.reciprocal(sm[:, :], sm[:, :]))
    c(v.tensor_tensor(lg[:, :, :], lg[:, :, :], spread(sm[:, :], E), ALU.mult))


def pick(c, v, k, pr, E, mx, cand, oh):
    c(v.tensor_reduce(mx[:, :], pr[:, :, :], AX_X, ALU.max))
    c(v.tensor_tensor(cand[:, :, :], pr[:, :, :], spread(mx[:, :], E), ALU.is_equal))
    c(v.scalar_tensor_tensor(cand[:, :, :], cand[:, :, :], -1000.0, k.expert[:, :, 0:E], ALU.mult, ALU.add))
    c(v.tensor_reduce(k.small[:, :], cand[:, :, :], AX_X, ALU.min))
    c(v.tensor_tensor(oh, cand[:, :, :], spread(k.small[:, :], E), ALU.is_equal))


def route(nc, name, k, lg, E, kind, xbuf, nblocks, beside=None, steps=0):
    C = {"capacity": 1, "top1": 1, "shared": 2, "soft2": 2}[kind]
    EE = E
    N = C * NT
    top = EE * CAP_ROWS if kind == "capacity" else nblocks * BLOCK
    with Phase(nc, name) as ph:
        dve, a_in, a_out, cnt, off = ph.sem("dve"), ph.sem("a_in"), ph.sem("a_out"), ph.sem("cnt"), ph.sem("off")
        ready, free, whole, passed = ph.sem("ready"), ph.row_dmas(G, 16 * C * NG), ph.sem("whole", "hardware"), ph.sem("passed")
        mx, sm, m2 = ph.sb("mx", [P, NT]), ph.sb("sm", [P, NT]), ph.sb("m2", [P, NT])
        cand = ph.sb("cand", [P, NT, E])
        oh = ph.sb("oh", [P, N, EE])
        before, tot, incl = (ph.sb(n, [P, N, EE]) for n in ("before", "tot", "incl"))
        nb_i, nb, endb, startb = ph.sb("nb_i", [P, EE], I32), ph.sb("nb", [P, EE]), ph.sb("endb", [P, EE]), ph.sb("startb", [P, EE])
        pos, base, kept, tgt = ph.sb("pos", [P, N]), ph.sb("base", [P, N]), ph.sb("kept", [P, N]), ph.sb("tgt", [P, N])
        tgt_u = ph.sb("tgt_u", [P, N], U32)
        trash = ph.sb("trash", [P, N])
        ow = ph.sb("ow", [1, MAX_BLOCKS])
        rows, ix = ph.sb("rows", [P, G, D]), ph.sb("ix", [P, C, G], U32)
        pp = ph.ps("pp", [P, 2 * C, 512])
        probs = lg
        if beside:
            beside.take(ph, steps)
        with nc.Block() as b:
            @b.vector
            def _(v):
                c = Chain(v, dve)
                softmax_steps(c, v, k, lg, E, mx, sm, a_in, a_out)
                v1 = oh[:, 0:NT, 0:E]
                pick(c, v, k, probs, E, mx, cand, v1)
                if kind in ("capacity", "top1"):
                    c(v.tensor_copy(k.coef[:, 0:NT], mx[:, :]))
                else:
                    v2 = oh[:, NT:2 * NT, 0:E]
                    c(v.scalar_tensor_tensor(probs[:, :, :], v1, -4.0, probs[:, :, :], ALU.mult, ALU.add))
                    pick(c, v, k, probs, E, m2, cand, v2)
                    if kind == "shared":
                        c(v.tensor_tensor(sm[:, :], mx[:, :], m2[:, :], ALU.add))
                        c(v.reciprocal(sm[:, :], sm[:, :]))
                        c(v.tensor_tensor(k.coef[:, 0:NT], mx[:, :], sm[:, :], ALU.mult))
                        c(v.tensor_tensor(k.coef[:, NT:2 * NT], m2[:, :], sm[:, :], ALU.mult))
                    else:
                        c(v.tensor_tensor(k.coef[:, NT:2 * NT], m2[:, :], mx[:, :], ALU.subtract))
                        v.sem_inc(a_in, 1)
                        v.wait_ge(a_out, 2)
                        c(v.tensor_scalar(sm[:, :], k.coef[:, NT:2 * NT], 1.0, None, ALU.add))
                        c(v.reciprocal(sm[:, :], sm[:, :]))
                        c(v.tensor_copy(k.coef[:, 0:NT], sm[:, :]))
                        c(v.tensor_tensor(k.coef[:, NT:2 * NT], k.coef[:, NT:2 * NT], sm[:, :], ALU.mult))
                for q in range(C):
                    last = oh[:, (q + 1) * NT - 1, :]
                    c(v.tensor_scalar(last, last, k.lastmask[:, 0:1], None, ALU.mult))
                v.sem_inc(cnt, 1)
                v.wait_ge(off, 1)
                for q in range(C):
                    s = slice(q * NT, (q + 1) * NT)
                    c(v.tensor_copy(before[:, s, :], pp[:, 2 * q, 0:NT * EE].rearrange("p (t e) -> p t e", e=EE)))
                    c(v.tensor_copy(tot[:, s, :], pp[:, 2 * q + 1, 0:NT * EE].rearrange("p (t e) -> p t e", e=EE)))
                for e in range(EE):
                    c(v.tensor_tensor_scan(incl[:, :, e], k.onerow[:, 0:N], tot[:, :, e], 0.0, ALU.mult, ALU.add))
                if kind == "capacity":
                    c(v.tensor_scalar(startb[:, :], k.expert[:, 0, 0:EE], float(CAP_ROWS), None, ALU.mult))
                    c(v.memset(ow[:, :], 0.0))
                    for e in range(EE):
                        c(v.memset(ow[:, e * (CAP_ROWS // BLOCK):(e + 1) * (CAP_ROWS // BLOCK)], float(e)))
                else:
                    c(v.tensor_scalar(nb[:, :], incl[:, N - 1, :], float(BLOCK - 1), None, ALU.add))
                    c(v.tensor_copy(nb_i[:, :], nb[:, :]))
                    c(v.tensor_scalar(nb_i[:, :], nb_i[:, :], 8, None, ALU.arith_shift_right))
                    c(v.tensor_copy(nb[:, :], nb_i[:, :]))
                    c(v.tensor_tensor_scan(endb[:, :], k.ones[:, 0:EE], nb[:, :], 0.0, ALU.mult, ALU.add))
                    c(v.tensor_tensor(startb[:, :], endb[:, :], nb[:, :], ALU.subtract))
                    if kind == "shared":
                        c(v.tensor_scalar(startb[:, :], startb[:, :], float(SHARED_BLOCKS), None, ALU.add))
                    c(v.memset(ow[:, :], -1.0))
                    for e in range(EE):
                        c(v.scalar_tensor_tensor(ow[:, :], k.iota[0:1, 0:MAX_BLOCKS], startb[0:1, e:e + 1], ow[:, :], ALU.is_ge, ALU.add))
                    if kind == "shared":
                        c(v.memset(ow[:, 0:SHARED_BLOCKS], float(E)))
                    c(v.tensor_scalar(startb[:, :], startb[:, :], float(BLOCK), None, ALU.mult))
                c(v.tensor_copy(k.block_expert[:, :], ow[:, 0:MAX_BLOCKS]))
                c(v.tensor_tensor(before[:, :, :], before[:, :, :], incl[:, :, :], ALU.add))
                c(v.tensor_tensor(before[:, :, :], before[:, :, :], tot[:, :, :], ALU.subtract))
                c(v.tensor_tensor(before[:, :, :], before[:, :, :], oh[:, :, :], ALU.mult))
                c(v.tensor_reduce(pos[:, :], before[:, :, :], AX_X, ALU.add))
                for e in range(EE):
                    c(v.tensor_scalar(incl[:, :, e], oh[:, :, e], startb[:, e:e + 1], None, ALU.mult))
                c(v.tensor_reduce(base[:, :], incl[:, :, :], AX_X, ALU.add))
                c(v.tensor_reduce(kept[:, :], oh[:, :, :], AX_X, ALU.add))
                c(v.tensor_scalar(trash[:, :], k.iota[:, 0:N], float(P), k.pnum[:, 0:1], ALU.mult, ALU.add))
                c(v.tensor_scalar(trash[:, :], trash[:, :], float(top), None, ALU.add))
                if kind == "capacity":
                    c(v.tensor_scalar(tgt[:, :], pos[:, :], float(CAP), None, ALU.is_lt))
                    c(v.tensor_tensor(kept[:, :], kept[:, :], tgt[:, :], ALU.mult))
                c(v.tensor_tensor(k.coef[:, 0:N], k.coef[:, 0:N], kept[:, :], ALU.mult))
                c(v.tensor_tensor(pos[:, :], pos[:, :], base[:, :], ALU.add))
                c(v.tensor_tensor(tgt[:, :], pos[:, :], kept[:, :], ALU.mult))
                c(v.tensor_copy(k.back[:, 0:N], tgt[:, :]))
                c(v.tensor_tensor(pos[:, :], pos[:, :], trash[:, :], ALU.subtract))
                c(v.tensor_tensor(pos[:, :], pos[:, :], kept[:, :], ALU.mult))
                c(v.tensor_tensor(pos[:, :], pos[:, :], trash[:, :], ALU.add))
                c(v.tensor_copy(tgt_u[:, :], pos[:, :]))
                with v.Fori(0, NG) as i:
                    for j in range(G):
                        free[j].wait(v, i * 16 * C)
                        v.tensor_copy(rows[:, j, :], k.y[:, ds(i * G + j, 1), :].rearrange("p a d -> p (a d)")).then_inc(ready, 1)
                        v.tensor_copy(ix[:, :, j:j + 1], tgt_u[:, :].rearrange("p (c t) -> p c t", c=C)[:, :, ds(i * G + j, 1)]).then_inc(ready, 1)

            @b.scalar
            def _(a):
                a.wait_ge(a_in, 1)
                a.activation(lg[:, :, :], lg[:, :, :], ACT.Exp).then_inc(a_out, 1)
                if kind == "soft2":
                    a.wait_ge(a_in, 2)
                    a.activation(k.coef[:, NT:2 * NT], k.coef[:, NT:2 * NT], ACT.Exp).then_inc(a_out, 1)

            @b.tensor
            def _(pe):
                pe.wait_ge(cnt, 1)
                for q in range(C):
                    r = oh[:, q * NT:(q + 1) * NT, :].rearrange("p t e -> p (t e)")
                    pe.matmul(pp[:, 2 * q, 0:NT * EE], k.before[:, :], r, start=True, stop=True)
                    mm = pe.matmul(pp[:, 2 * q + 1, 0:NT * EE], k.ones[:, :], r, start=True, stop=True)
                mm.then_inc(off, 1)

            if kind == "shared":
                @b.sync
                def _(sp):
                    sp.dma_start(xbuf[0:NP, :].rearrange("(t p) d -> p t d", p=P), k.y[:, :, :]).then_inc(whole, 16)
                    sp.wait_ge(whole, 16)

            @b.gpsimd
            def _(g):
                if beside:
                    beside.steps(g, steps)
                with g.Fori(0, NG) as i:
                    for j in range(G):
                        g.wait_ge(ready, 2 * (i * G + j) + 2)
                        g.sem_inc(passed, 1)
                        for q in range(C):
                            g.indirect_dma_start(xbuf, bass.IndirectOffsetOnAxis(ap=ix[:, q, j:j + 1], axis=0),
                                                 rows[:, j, :], None).then_inc(free[j].sem, 16)
                for s in free:
                    s.wait(g, 16 * C * NG)


def expert_blocks(nc, name, k, xbuf, ybuf, nblocks, hidden, last, beside=None):
    dims = [(w.shape[1] // P, w.shape[2] // P) for w, _, _ in hidden]
    offs = [sum(f for _, f in dims[:q]) for q in range(len(dims))]
    NF = sum(f for _, f in dims)
    NB = 4
    assert NF % NB == 0
    wl, bl = last
    KL = wl.shape[1] // P
    per = [w for w, _, _ in hidden if w.shape[0] > 1]
    n_ld = 2 + 2 * len(per)
    common = [q for q, (w, _, _) in enumerate(hidden) if w.shape[0] == 1]
    with Phase(nc, name) as ph:
        loaded, once, xloaded = ph.sems("loaded", 2, "hardware"), ph.sem("once", "hardware"), ph.sems("xloaded", 2, "hardware")
        xt_done, xt_copied = ph.sems("xt_done", 2), ph.sems("xt_copied", 2)
        hmul, hact, ymul, ydone = ph.sem("hmul"), ph.sem("hact"), ph.sem("ymul"), ph.sem("ydone")
        stored, passed = ph.row_dmas(2, 16 * (nblocks // 2)), ph.sem("passed")
        xb, xt = ph.sb("xb", [P, 2, 2, D]), ph.sb("xt", [P, 2, KD, BLOCK])
        ws, bs = [], []
        for q, (w, _, _) in enumerate(hidden):
            n = 2 if w.shape[0] > 1 else 1
            ws.append(ph.sb(f"w{q}", [P, n, dims[q][0], w.shape[2]]))
            bs.append(ph.sb(f"b{q}", [P, n, dims[q][1]]))
        wls, bls = ph.sb("wl", [P, 2, KL, D]), ph.sb("bl", [P, 2, D])
        hs = [ph.sb(f"h{q}", [P, dims[q][1], BLOCK]) for q in range(len(hidden))]
        ys = ph.sb("ys", [P, 2, 2, D])
        pt, phid, py = ph.ps("pt", [P, 2, 512]), ph.ps("phid", [P, NB, 512]), ph.ps("py", [P, 2, 512])
        iters = nblocks // 2
        if beside:
            beside.take(ph, nblocks)
        with nc.Block() as b:
            @b.sync
            def _(sp):
                for q in common:
                    sp.dma_start(ws[q][:, 0, :, :], hidden[q][0][0].rearrange("(k p) f -> p k f", p=P)).then_inc(once, 16)
                    sp.dma_start(bs[q][:, 0, :], hidden[q][1][0]).then_inc(once, 16)
                with sp.Fori(0, iters) as i:
                    for s in range(2):
                        B = i * 2 + s
                        e = sp.value_load(k.block_expert[0:1, ds(B, 1)], min_val=0, max_val=wl.shape[0] - 1)
                        sp.wait_ge(ydone, 2 * B)
                        sp.dma_start(xb[:, s, :, :], xbuf[ds(B * BLOCK, BLOCK), :].rearrange("(n p) d -> p n d", p=P)).then_inc(xloaded[s], 16)
                        for q, (w, bias, _) in enumerate(hidden):
                            if w.shape[0] > 1:
                                sp.dma_start(ws[q][:, s, :, :], w[ds(e, 1), :, :].rearrange("a (k p) f -> p (a k) f", p=P)).then_inc(loaded[s], 16)
                                sp.dma_start(bs[q][:, s, :], bias[ds(e, 1), :, :].rearrange("a p f -> p (a f)")).then_inc(loaded[s], 16)
                        sp.dma_start(wls[:, s, :, :], wl[ds(e, 1), :, :].rearrange("a (k p) n -> p (a k) n", p=P)).then_inc(loaded[s], 16)
                        sp.dma_start(bls[:, s, :], bl[ds(e, 1), :].rearrange("a n -> (a n)").partition_broadcast(P)).then_inc(loaded[s], 16)

            @b.tensor
            def _(pe):
                if common:
                    pe.wait_ge(once, 32 * len(common))
                def turn_rows(i, s):
                    pe.wait_ge(xloaded[s], 16 * i + 16)
                    pe.wait_ge(xt_copied[s], i)
                    for n in range(2):
                        for q in range(KD):
                            mm = pe.transpose(pt[:, s, q * BLOCK + n * P:q * BLOCK + (n + 1) * P],
                                              xb[:, s, n, q * P:(q + 1) * P], k.ident[:, :])
                    mm.then_inc(xt_done[s], 1)

                def block(i, s, more):
                    B = i * 2 + s
                    pe.wait_ge(loaded[s], 16 * n_ld * i + 16 * n_ld)
                    pe.wait_ge(xt_copied[s], i + 1)
                    for l, (kt, ft) in enumerate(dims):
                        sl = s if hidden[l][0].shape[0] > 1 else 0
                        for f in range(ft):
                            pe.wait_ge(hact, B * NF + offs[l] + f + 1)
                            for q in range(kt):
                                if l and f == 0:
                                    pe.wait_ge(hact, B * NF + offs[l - 1] + q + 1 + NB)
                                src = hs[l - 1][:, q, :] if l else xt[:, s, q, :]
                                mm = pe.matmul(phid[:, (offs[l] + f) % NB, 0:BLOCK], ws[l][:, sl, q, f * P:(f + 1) * P], src,
                                               start=q == 0, stop=q == kt - 1)
                            mm.then_inc(hmul, 1)
                    if more:
                        turn_rows(i + s, 1 - s)
                    for n in range(2):
                        pe.wait_ge(ydone, B * 2 + n + 1)
                        for q in range(KL):
                            if n == 0:
                                pe.wait_ge(hact, B * NF + offs[-1] + q + 1 + NB)
                            mm = pe.matmul(py[:, n, 0:D], hs[-1][:, q, n * P:(n + 1) * P], wls[:, s, q, :],
                                           start=q == 0, stop=q == KL - 1)
                        mm.then_inc(ymul, 1)

                turn_rows(0, 0)
                with pe.Fori(0, iters - 1) as i:
                    block(i, 0, True)
                    block(i, 1, True)
                block(iters - 1, 0, True)
                block(iters - 1, 1, False)

            @b.scalar
            def _(a):
                a.sem_inc(hact, NB)
                if common:
                    a.wait_ge(once, 32 * len(common))
                def copy_rows(i, s):
                    a.wait_ge(xt_done[s], i + 1)
                    a.copy(xt[:, s, :, :], pt[:, s, :].rearrange("p (k n) -> p k n", k=KD)).then_inc(xt_copied[s], 1)

                def block(i, s, more):
                    B = i * 2 + s
                    a.wait_ge(loaded[s], 16 * n_ld * i + 16 * n_ld)
                    for l, (kt, ft) in enumerate(dims):
                        sl = s if hidden[l][0].shape[0] > 1 else 0
                        for f in range(ft):
                            a.wait_ge(hmul, B * NF + offs[l] + f + 1)
                            a.activation(hs[l][:, f, :], phid[:, (offs[l] + f) % NB, 0:BLOCK], hidden[l][2],
                                         bias=bs[l][:, sl, f:f + 1]).then_inc(hact, 1)
                    if more:
                        copy_rows(i + s, 1 - s)

                copy_rows(0, 0)
                with a.Fori(0, iters - 1) as i:
                    block(i, 0, True)
                    block(i, 1, True)
                block(iters - 1, 0, True)
                block(iters - 1, 1, False)

            @b.vector
            def _(v):
                v.sem_inc(ydone, 2)
                with v.Fori(0, iters) as i:
                    for s in range(2):
                        stored[s].wait(v, 16 * i)
                        v.wait_ge(loaded[s], 16 * n_ld * i + 16 * n_ld)
                        for n in range(2):
                            v.wait_ge(ymul, (i * 2 + s) * 2 + n + 1)
                            v.tensor_tensor(ys[:, s, n, :], py[:, n, 0:D], bls[:, s, :], ALU.add).then_inc(ydone, 1)

            @b.gpsimd
            def _(g):
                with g.Fori(0, iters) as i:
                    for s in range(2):
                        B = i * 2 + s
                        g.wait_ge(ydone, B * 2 + 4)
                        g.sem_inc(passed, 1)
                        g.dma_start(ybuf[ds(B * BLOCK, BLOCK), :].rearrange("(n p) d -> p n d", p=P), ys[:, s, :, :]).then_inc(stored[s].sem, 16)
                        if beside:
                            beside.step(g, B)
                for s in stored:
                    s.wait(g, 16 * iters)


def combine(nc, name, k, ybuf, C, shared=False):
    with Phase(nc, name) as ph:
        staged, landed, added, passed = ph.sem("staged"), ph.row_dmas(G, 16 * C * NG), ph.sem("added"), ph.sem("passed")
        first = [0, NT * (1 + shared)]
        ix, rows = ph.sb("ix", [P, G], U32), ph.sb("rows", [P, G, D])
        if shared:
            all_landed, all_rows = ph.sems("all_landed", G, "hardware"), ph.sb("all_rows", [P, G, D])
        with nc.Block() as b:
            if shared:
                @b.sync
                def _(sp):
                    with sp.Fori(0, NG) as i:
                        for j in range(G):
                            sp.wait_ge(added, 2 * i * G)
                            sp.dma_start(all_rows[:, j, :], ybuf[ds((i * G + j) * P, P), :]).then_inc(all_landed[j], 16)

            @b.gpsimd
            def _(g):
                with g.Fori(0, C * NG) as i:
                    for j in range(G):
                        g.wait_ge(staged, i * G + j + 1)
                        g.sem_inc(passed, 1)
                        g.indirect_dma_start(rows[:, j, :], None, ybuf, bass.IndirectOffsetOnAxis(ap=ix[:, j:j + 1], axis=0)).then_inc(landed[j].sem, 16)

            @b.vector
            def _(v):
                for j in range(G):
                    v.tensor_copy(ix[:, j:j + 1], k.back[:, j:j + 1]).then_inc(staged, 1)
                for q in range(C):
                    with v.Fori(0, NG) as i:
                        for j in range(G):
                            xt = k.x[:, ds(i * G + j, 1), :].rearrange("p a d -> p (a d)")
                            n = first[q] + (i * G + j) * (1 + (shared and q == 0))
                            if shared and q == 0:
                                v.wait_ge(all_landed[j], 16 * i + 16)
                                v.tensor_tensor(xt, xt, all_rows[:, j, :], ALU.add).then_inc(added, 1)
                                n = n + 1
                            landed[j].wait(v, 16 * i + 16 * q * NG + 16)
                            v.wait_ge(added, n)
                            v.scalar_tensor_tensor(xt, rows[:, j, :], k.coef[:, ds(i * G + j + q * NT, 1)], xt, ALU.mult, ALU.add).then_inc(added, 1)
                            v.wait_ge(added, n + 1)
                            v.tensor_copy(ix[:, j:j + 1], k.back[:, ds(i * G + j + q * NT + G, 1)]).then_inc(staged, 1)


def degrees(nc, k):
    with Phase(nc, "deg") as ph:
        d, r = ph.sem("d"), ph.sem("r")
        with nc.Block() as b:
            @b.vector
            def _(v):
                v.tensor_scalar(k.dinv[:, :], k.deg_in[:, :], 1.0, None, ALU.add).then_inc(d, 1)
                v.wait_ge(r, 1)
                v.reciprocal(k.dinv[:, :], k.dinv[:, :]).then_inc(d, 1)

            @b.scalar
            def _(a):
                a.wait_ge(d, 1)
                a.activation(k.dinv[:, :], k.dinv[:, :], ACT.Sqrt).then_inc(r, 1)


def batch_norm(nc, k, gamma, beta, eps=1e-5):
    with Phase(nc, "bn") as ph:
        ld, dve, summed, centred, squared, root = ph.sem("ld", "hardware"), ph.sem("dve"), ph.sem("summed"), ph.sem("centred"), ph.sem("squared"), ph.sem("root")
        gm, bt, mean, var = (ph.sb(n, [P, D]) for n in ("gm", "bt", "mean", "var"))
        sq = ph.sb("sq", [P, G, D])
        tmp, zero, cleared = ph.sb("tmp", [P, G, D]), ph.sb("zero", [P, D]), ph.sem("cleared")
        pm = ph.ps("pm", [P, 2, 512])
        with nc.Block() as b:
            @b.sync
            def _(sp):
                sp.dma_start(gm[:, :], gamma.partition_broadcast(P)).then_inc(ld, 16)
                sp.dma_start(bt[:, :], beta.partition_broadcast(P)).then_inc(ld, 16)

            @b.tensor
            def _(pe):
                pe.matmul(pm[:, 0, 0:D], k.ones[:, :], k.y[:, 0, :], start=True, stop=False)
                with pe.Fori(0, NG - 1) as i:
                    for j in range(G):
                        pe.matmul(pm[:, 0, 0:D], k.ones[:, :], k.y[:, ds(i * G + j + 1, 1), :].rearrange("p a d -> p (a d)"), start=False, stop=False)
                for t in range(NT - G + 1, NT - 1):
                    pe.matmul(pm[:, 0, 0:D], k.ones[:, :], k.y[:, t, :], start=False, stop=False)
                pe.matmul(pm[:, 0, 0:D], k.onesmask[:, :], k.y[:, NT - 1, :], start=False, stop=True).then_inc(summed, 1)
                pe.wait_ge(cleared, 1)
                pe.matmul(pm[:, 1, 0:D], k.ones[:, :], zero[:, :], start=True, stop=False, skip_group_check=True)
                with pe.Fori(0, NG - 1) as i:
                    for j in range(G):
                        pe.wait_ge(squared, i * G + j + 1)
                        mm = pe.matmul(pm[:, 1, 0:D], k.ones[:, :], sq[:, j, :], start=False, stop=False, skip_group_check=True)
                        mm.then_inc(summed, 1)
                for j in range(G):
                    pe.wait_ge(squared, NT - G + j + 1)
                    mm = pe.matmul(pm[:, 1, 0:D], k.ones[:, :] if j < G - 1 else k.onesmask[:, :], sq[:, j, :], start=False, stop=j == G - 1, skip_group_check=True)
                    mm.then_inc(summed, 1)

            @b.vector
            def _(v):
                c = Chain(v, dve)
                v.memset(zero[:, :], 0.0).then_inc(cleared, 1)
                v.wait_ge(summed, 1)
                c(v.tensor_scalar(mean[:, :], pm[:, 0, 0:D], 1.0 / N_NODES, None, ALU.mult))
                with v.Fori(0, NG) as i:
                    for j in range(G):
                        yt = k.y[:, ds(i * G + j, 1), :].rearrange("p a d -> p (a d)")
                        v.tensor_tensor(yt, yt, mean[:, :], ALU.subtract).then_inc(centred, 1)
                v.wait_ge(summed, 1 + NT)
                c(v.tensor_scalar(var[:, :], pm[:, 1, 0:D], 1.0 / N_NODES, eps, ALU.mult, ALU.add))
                v.wait_ge(root, 1)
                c(v.reciprocal(var[:, :], var[:, :]))
                v.wait_ge(ld, 32)
                c(v.tensor_tensor(var[:, :], var[:, :], gm[:, :], ALU.mult))
                n = c.n
                with v.Fori(0, NG) as i:
                    at = n + i * G * 3
                    v.wait_ge(dve, at)
                    for j in range(G):
                        v.tensor_tensor(tmp[:, j, :], k.y[:, ds(i * G + j, 1), :].rearrange("p a d -> p (a d)"), var[:, :], ALU.mult).then_inc(dve, 1)
                    for j in range(G):
                        v.wait_ge(dve, at + j + 1)
                        v.tensor_tensor(tmp[:, j, :], tmp[:, j, :], bt[:, :], ALU.add).then_inc(dve, 1)
                    for j in range(G):
                        xt = k.x[:, ds(i * G + j, 1), :].rearrange("p a d -> p (a d)")
                        v.wait_ge(dve, at + G + j + 1)
                        v.scalar_tensor_tensor(xt, tmp[:, j, :], 0.0, xt, ALU.max, ALU.add).then_inc(dve, 1)

            @b.scalar
            def _(a):
                with a.Fori(0, NG) as i:
                    for j in range(G):
                        a.wait_ge(centred, i * G + j + 1)
                        a.wait_ge(summed, i * G + 1)
                        a.activation(sq[:, j, :], k.y[:, ds(i * G + j, 1), :].rearrange("p a d -> p (a d)"), ACT.Square).then_inc(squared, 1)
                a.wait_ge(dve, 2)
                a.activation(var[:, :], var[:, :], ACT.Sqrt).then_inc(root, 1)


CH = 400
NCH = NP // CH
TC = 640
NTC = NP // TC


class ScoreGather:

    def __init__(self, nc, memory, table, index, scores):
        def sb(n, shape, dt=F32):
            return memory.enter_context(nc.sbuf_tensor(f"gather_{n}", shape, dt))

        self.nc, self.table, self.index, self.scores = nc, table, index, scores
        self.ix, self.ring = sb("ix", [P, RING], U32), sb("ring", [P, RING, HEADS])
        self.done = 0

    def left(self):
        return (ST - self.done) // RING

    def take(self, ph, steps, width=RING):
        self.first, self.width = self.done, width
        self.done += steps * width
        self.landed = RowDma(self.nc, RING, 16 * width * steps)
        self.staged, self.passed, self.kept = (ph.sem(f"gather_{n}") for n in ("staged", "passed", "kept"))

    def ask(self, g, i):
        g.tensor_copy(self.ix[:, 0:self.width], self.index[:, ds(self.first + i * self.width, self.width)]).then_inc(self.staged, 1)
        g.wait_ge(self.staged, i + 1)
        g.sem_inc(self.passed, 1)
        for j in range(self.width):
            g.indirect_dma_start(self.ring[:, j, :], None, self.table,
                                 bass.IndirectOffsetOnAxis(ap=self.ix[:, j:j + 1], axis=0)).then_inc(self.landed.sem, 16)

    def keep(self, g, i):
        self.landed.wait(g, 16 * self.width * (i + 1))
        g.sem_inc(self.passed, 1)
        g.tensor_copy(self.scores[:, ds(self.first + i * self.width, self.width), :], self.ring[:, 0:self.width, :]).then_inc(self.kept, 1)
        g.wait_ge(self.kept, i + 1)
        g.sem_inc(self.passed, 1)

    def steps(self, g, n):
        with g.Fori(0, n) as i:
            self.ask(g, i)
            self.keep(g, i)


def affine_norm(nc, name, k, src, gain, bias, dest, add, eps=1e-5):
    with Phase(nc, name) as ph:
        ld, dve, root = ph.sem("ld", "hardware"), ph.sem("dve"), ph.sem("root")
        st = ph.sb("st", [P, NT, 6])
        mean, var, dif, rstd = (ph.sb(n, [P, NT]) for n in ("mean", "var", "dif", "rstd"))
        gb, bb, tmp = ph.sb("gb", [P, D]), ph.sb("bb", [P, D]), ph.sb("tmp", [P, G, D])
        with nc.Block() as b:
            @b.sync
            def _(sp):
                sp.dma_start(gb[:, :], gain.partition_broadcast(P)).then_inc(ld, 16)
                sp.dma_start(bb[:, :], bias.partition_broadcast(P)).then_inc(ld, 16)

            @b.vector
            def _(v):
                with v.Fori(0, NG) as i:
                    for j in range(G):
                        v.bn_stats(st[:, ds(i * G + j, 1), :], src[:, ds(i * G + j, 1), :]).then_inc(dve, 1)
                v.wait_ge(dve, NT)
                c = Chain(v, dve)
                c.n = NT
                c(v.tensor_tensor(mean[:, :], st[:, :, 1], st[:, :, 4], ALU.add))
                c(v.tensor_scalar(mean[:, :], mean[:, :], 0.5, None, ALU.mult))
                c(v.tensor_tensor(dif[:, :], st[:, :, 1], st[:, :, 4], ALU.subtract))
                c(v.tensor_tensor(dif[:, :], dif[:, :], dif[:, :], ALU.mult))
                c(v.tensor_scalar(dif[:, :], dif[:, :], 0.25, eps, ALU.mult, ALU.add))
                c(v.tensor_tensor(var[:, :], st[:, :, 2], st[:, :, 5], ALU.add))
                c(v.scalar_tensor_tensor(var[:, :], var[:, :], 1.0 / D, dif[:, :], ALU.mult, ALU.add))
                v.wait_ge(root, 1)
                c(v.reciprocal(rstd[:, :], rstd[:, :]))
                v.wait_ge(ld, 32)
                n, m = c.n, 4 if add else 3
                with v.Fori(0, NG) as i:
                    rows = [dest[:, ds(i * G + j, 1), :].rearrange("p a d -> p (a d)") for j in range(G)]
                    at = n + i * G * m
                    for j in range(G):
                        v.wait_ge(dve, at)
                        v.tensor_scalar(tmp[:, j, :], src[:, ds(i * G + j, 1), :].rearrange("p a d -> p (a d)"), mean[:, ds(i * G + j, 1)],
                                        rstd[:, ds(i * G + j, 1)], ALU.subtract, ALU.mult).then_inc(dve, 1)
                    for j in range(G):
                        v.wait_ge(dve, at + j + 1)
                        v.tensor_tensor(tmp[:, j, :], tmp[:, j, :], gb[:, :], ALU.mult).then_inc(dve, 1)
                    if add:
                        for j in range(G):
                            v.wait_ge(dve, at + G + j + 1)
                            v.tensor_tensor(tmp[:, j, :], tmp[:, j, :], bb[:, :], ALU.add).then_inc(dve, 1)
                    for j in range(G):
                        v.wait_ge(dve, at + (m - 2) * G + j + 1)
                        v.tensor_tensor(rows[j], tmp[:, j, :], rows[j] if add else bb[:, :], ALU.add).then_inc(dve, 1)

            @b.scalar
            def _(a):
                a.wait_ge(dve, NT + 7)
                a.activation(rstd[:, :], var[:, :], ACT.Sqrt).then_inc(root, 1)


def turn(nc, name, k, dest, rows=None, table=None, beside=None, steps=0):
    with Phase(nc, name) as ph:
        staged, tdone, evac = ph.sem("staged"), ph.sems("tdone", G), ph.sems("evac", G)
        landed = ph.sems("landed", G, "hardware")
        stage = ph.sb("stage", [P, G, D])
        pt = ph.ps("pt", [P, G, 512])
        if beside:
            beside.take(ph, steps)
        with nc.Block() as b:
            if beside:
                @b.gpsimd
                def _(g):
                    beside.steps(g, steps)

            if table is not None:
                @b.sync
                def _(sp):
                    with sp.Fori(0, NG) as i:
                        for j in range(G):
                            sp.wait_ge(tdone[j], i)
                            sp.dma_start(stage[:, j, :], table[ds((i * G + j) * P, P), :]).then_inc(landed[j], 16)
            else:
                @b.vector
                def _(v):
                    with v.Fori(0, NG) as i:
                        for j in range(G):
                            v.wait_ge(tdone[j], i)
                            v.tensor_copy(stage[:, j, :], rows[:, ds(i * G + j, 1), :].rearrange("p a d -> p (a d)")).then_inc(staged, 1)

            @b.tensor
            def _(pe):
                with pe.Fori(0, NG) as i:
                    for j in range(G):
                        if table is not None:
                            pe.wait_ge(landed[j], 16 * i + 16)
                        else:
                            pe.wait_ge(staged, i * G + j + 1)
                        pe.wait_ge(evac[j], i)
                        for q in range(KD):
                            mm = pe.transpose(pt[:, j, q * P:(q + 1) * P], stage[:, j, q * P:(q + 1) * P], k.ident[:, :])
                        mm.then_inc(tdone[j], 1)

            @b.scalar
            def _(a):
                with a.Fori(0, NG) as i:
                    for j in range(G):
                        a.wait_ge(tdone[j], i + 1)
                        a.copy(dest[:, :, ds((i * G + j) * P, P)], pt[:, j, 0:D].rearrange("p (k n) -> p k n", k=KD)).then_inc(evac[j], 1)


def turn_back(nc, name, k, src, rows):
    with Phase(nc, name) as ph:
        staged, tdone, evac = ph.sem("staged"), ph.sems("tdone", G), ph.sems("evac", G)
        stage = ph.sb("stage", [P, G, KD, P])
        pt = ph.ps("pt", [P, G, 512])
        with nc.Block() as b:
            @b.scalar
            def _(a):
                with a.Fori(0, NG) as i:
                    for j in range(G):
                        a.wait_ge(tdone[j], i)
                        a.copy(stage[:, j, :, :], src[:, :, ds((i * G + j) * P, P)]).then_inc(staged, 1)

            @b.tensor
            def _(pe):
                with pe.Fori(0, NG) as i:
                    for j in range(G):
                        pe.wait_ge(staged, i * G + j + 1)
                        pe.wait_ge(evac[j], i)
                        for q in range(KD):
                            mm = pe.transpose(pt[:, j, q * P:(q + 1) * P], stage[:, j, q, :], k.ident[:, :])
                        mm.then_inc(tdone[j], 1)

            @b.vector
            def _(v):
                with v.Fori(0, NG) as i:
                    for j in range(G):
                        v.wait_ge(tdone[j], i + 1)
                        v.tensor_copy(rows[:, ds(i * G + j, 1), :].rearrange("p a d -> p (a d)"), pt[:, j, 0:D]).then_inc(evac[j], 1)


def order_nodes(nc, k, noise, vrow_dram, table, beside=None, steps=0):
    with Phase(nc, "ord") as ph:
        ld, vst, vld = ph.sem("ld", "hardware"), ph.sem("vst", "hardware"), ph.sem("vld", "hardware")
        dve, tr, staged, passed = ph.sem("dve"), ph.sem("tr"), ph.sem("staged"), ph.sem("passed")
        out = ph.row_dmas(G, 16 * NG)
        val, ns, gone = ph.sb("val", [P, NT]), ph.sb("ns", [P, NT]), ph.sb("gone", [P, 1])
        vt, vrow = ph.sb("vt", [NT, P]), ph.sb("vrow", [P, NP])
        less, earlier, tied = ph.sb("less", [P, NP]), ph.sb("earlier", [P, P]), ph.sb("tied", [P, P])
        below, upto, ties = (ph.sb(n, [P, NT]) for n in ("below", "upto", "ties"))
        rows, ix = ph.sb("rows", [P, G, D]), ph.sb("ix", [P, G], U32)
        pt = ph.ps("pt", [P, 512])
        if beside:
            beside.take(ph, steps)
        with nc.Block() as b:
            @b.gpsimd
            def _(g):
                if beside:
                    beside.steps(g, steps)
                with g.Fori(0, NG) as i:
                    g.wait_ge(staged, i * (G + 1) + G + 1)
                    g.sem_inc(passed, 1)
                    for j in range(G):
                        g.indirect_dma_start(table, bass.IndirectOffsetOnAxis(ap=ix[:, j:j + 1], axis=0), rows[:, j, :], None).then_inc(out[j].sem, 16)
                for q in out:
                    q.wait(g, 16 * NG)

            @b.sync
            def _(sp):
                sp.dma_start(ns[:, :], noise).then_inc(ld, 16)
                sp.wait_ge(dve, 5)
                sp.dma_start(vrow_dram.rearrange("(t p) -> t p", p=P), vt[:, :]).then_inc(vst, 16)
                sp.wait_ge(vst, 16)
                sp.dma_start(vrow[:, :], vrow_dram.partition_broadcast(P)).then_inc(vld, 16)

            @b.tensor
            def _(pe):
                pe.wait_ge(dve, 4)
                pe.transpose(pt[0:NT, 0:P], val[:, :], k.ident[:, :]).then_inc(tr, 1)

            @b.vector
            def _(v):
                c = Chain(v, dve)
                v.wait_ge(ld, 16)
                c(v.tensor_tensor(val[:, :], k.deg_out[:, :], ns[:, :], ALU.add))
                c(v.tensor_scalar(gone[:, :], k.lastmask[:, :], -1e30, 1e30, ALU.mult, ALU.add))
                c(v.tensor_tensor(val[:, NT - 1:NT], val[:, NT - 1:NT], k.lastmask[:, :], ALU.mult))
                c(v.tensor_tensor(val[:, NT - 1:NT], val[:, NT - 1:NT], gone[:, :], ALU.add))
                v.wait_ge(tr, 1)
                c(v.tensor_copy(vt[:, :], pt[0:NT, 0:P]))
                c(v.tensor_tensor(earlier[:, :], k.ones[:, :], k.before[:, :], ALU.subtract))
                c(v.tensor_tensor(earlier[:, :], earlier[:, :], k.ident[:, :], ALU.subtract))
                c(v.memset(upto[:, 0:1], 0.0))
                v.wait_ge(vld, 16)
                for t in range(NT):
                    v.tensor_scalar(less[:, t * P:NP], vrow[:, t * P:NP], val[:, t:t + 1], None, ALU.is_lt, ALU.add, accum_out=below[:, t:t + 1])
                    if t:
                        v.tensor_scalar(less[:, 0:t * P], vrow[:, 0:t * P], val[:, t:t + 1], None, ALU.is_le, ALU.add, accum_out=upto[:, t:t + 1])
                    v.scalar_tensor_tensor(tied[:, :], vrow[:, ts(t, P)], val[:, t:t + 1], earlier[:, :], ALU.is_equal, ALU.mult,
                                           accum_out=ties[:, t:t + 1]).then_inc(dve, 1)
                    c.n += 1
                    v.wait_ge(dve, c.n)
                c(v.tensor_tensor(below[:, :], below[:, :], ties[:, :], ALU.add))
                c(v.tensor_tensor(below[:, :], below[:, :], upto[:, :], ALU.add))
                c(v.memset(k.rank[:, NT:NT + G], 0))
                c(v.tensor_copy(k.rank[:, 0:NT], below[:, :]))
                with v.Fori(0, NG) as i:
                    for j in range(G):
                        out[j].wait(v, 16 * i)
                        v.tensor_copy(rows[:, j, :], k.y[:, ds(i * G + j, 1), :].rearrange("p a d -> p (a d)")).then_inc(staged, 1)
                    v.tensor_copy(ix[:, :], k.rank[:, ds(i * G, G)]).then_inc(staged, 1)


def mamba_in(nc, k, w, xc, zs, beside=None, steps=0):
    with Phase(nc, "mi") as ph:
        ld, stored = ph.sem("ld", "hardware"), ph.sem("stored", "hardware")
        mul, evac = ph.sem("mul"), ph.sem("evac")
        wsb, zst = ph.sb("w", [P, KD, 2 * D]), ph.sb("zst", [P, KD, CH])
        pi = ph.ps("pi", [P, 4, 512])
        if beside:
            beside.take(ph, steps)
        with nc.Block() as b:
            if beside:
                @b.gpsimd
                def _(g):
                    beside.steps(g, steps)

            @b.sync
            def _(sp):
                sp.dma_start(wsb[:, :, :], w.rearrange("(k p) n -> p k n", p=P)).then_inc(ld, 16)
                with sp.Fori(0, NCH) as i:
                    sp.wait_ge(evac, 4 * i + 8)
                    sp.dma_start(zs[:, :, ds(i * CH, CH)], zst[:, :, :]).then_inc(stored, 16)
                sp.wait_ge(stored, 16 * NCH)

            @b.tensor
            def _(pe):
                pe.wait_ge(ld, 16)
                with pe.Fori(0, NCH) as i:
                    for o in range(4):
                        pe.wait_ge(evac, 4 * i + o + 1)
                        for q in range(KD):
                            mm = pe.matmul(pi[:, o, 0:CH], wsb[:, q, o * P:(o + 1) * P], k.t[:, q, ds(i * CH, CH)], start=q == 0, stop=q == KD - 1)
                        mm.then_inc(mul, 1)

            @b.scalar
            def _(a):
                a.sem_inc(evac, 4)
                with a.Fori(0, NCH) as i:
                    for o in range(2):
                        a.wait_ge(mul, 4 * i + o + 1)
                        a.copy(xc[:, o, ds(i * CH + TAPS - 1, CH)], pi[:, o, 0:CH]).then_inc(evac, 1)
                    a.wait_ge(stored, 16 * i)
                    for o in range(2):
                        a.wait_ge(mul, 4 * i + o + 3)
                        a.activation(zst[:, o, :], pi[:, 2 + o, 0:CH], ACT.Silu).then_inc(evac, 1)

            @b.vector
            def _(v):
                v.memset(xc[:, :, 0:TAPS - 1], 0.0)


def mamba_conv(nc, k, w, bias, xc, cv, beside=None, steps=0):
    with Phase(nc, "mc") as ph:
        ld, dve = ph.sem("ld", "hardware"), ph.sem("dve")
        ws, bs = ph.sb("w", [P, KD, TAPS]), ph.sb("b", [P, KD])
        if beside:
            beside.take(ph, steps)
        with nc.Block() as b:
            if beside:
                @b.gpsimd
                def _(g):
                    beside.steps(g, steps)

            @b.sync
            def _(sp):
                sp.dma_start(ws[:, :, :], w.rearrange("(k p) n -> p k n", p=P)).then_inc(ld, 16)
                sp.dma_start(bs[:, :], bias).then_inc(ld, 16)

            @b.vector
            def _(v):
                c = Chain(v, dve)
                v.wait_ge(ld, 32)
                for o in range(KD):
                    c(v.tensor_scalar(cv[:, o, :], xc[:, o, 0:NP], ws[:, o, 0:1], None, ALU.mult))
                    for q in range(1, TAPS):
                        c(v.scalar_tensor_tensor(cv[:, o, :], xc[:, o, q:q + NP], ws[:, o, q:q + 1], cv[:, o, :], ALU.mult, ALU.add))

            @b.scalar
            def _(a):
                a.wait_ge(ld, 32)
                for o in range(KD):
                    a.wait_ge(dve, (o + 1) * TAPS)
                    a.activation(xc[:, o, 0:NP], cv[:, o, :], ACT.Silu, bias=bs[:, o:o + 1])


def mamba_steps(nc, k, wx, wdt, bdt, dpar, xc, dt, bc, beside=None, steps=0):
    H2 = NP // 2
    with Phase(nc, "ms") as ph:
        ld, stored = ph.sem("ld", "hardware"), ph.sem("stored", "hardware")
        mul, evac, mul2, evac2, dve, act, passed = (ph.sem(n) for n in ("mul", "evac", "mul2", "evac2", "dve", "act", "passed"))
        R = RANK + 2 * STATES
        wxs, wds, bds, dps = ph.sb("wx", [P, KD, R]), ph.sb("wdt", [RANK, D]), ph.sb("bdt", [P, KD]), ph.sb("dp", [P, KD])
        dbc = ph.sb("dbc", [R, NP])
        e, wv, lnw, z = (ph.sb(n, [P, H2]) for n in ("e", "wv", "lnw", "z"))
        pd, pdt = ph.ps("pd", [P, 512]), ph.ps("pdt", [P, 2, 512])
        if beside:
            beside.take(ph, steps)
        with nc.Block() as b:
            if beside:
                @b.gpsimd
                def _(g):
                    beside.steps(g, steps)

            @b.sync
            def _(sp):
                sp.dma_start(wxs[:, :, :], wx.rearrange("(k p) n -> p k n", p=P)).then_inc(ld, 16)
                sp.dma_start(wds[:, :], wdt).then_inc(ld, 16)
                sp.dma_start(bds[:, :], bdt).then_inc(ld, 16)
                sp.dma_start(dps[:, :], dpar).then_inc(ld, 16)
                sp.wait_ge(evac, NCH)
                sp.dma_start(bc, dbc[RANK:R, :]).then_inc(stored, 16)
                sp.wait_ge(stored, 16)

            @b.tensor
            def _(pe):
                pe.wait_ge(ld, 64)
                with pe.Fori(0, NCH) as i:
                    pe.wait_ge(evac, i)
                    pe.sem_inc(passed, 1)
                    for q in range(KD):
                        mm = pe.matmul(pd[0:R, 0:CH], wxs[:, q, :], xc[:, q, ds(i * CH, CH)], start=q == 0, stop=q == KD - 1)
                    mm.then_inc(mul, 1)
                    pe.wait_ge(evac2, 2 * i)
                    pe.wait_ge(evac, i + 1)
                    pe.sem_inc(passed, 1)
                    for o in range(KD):
                        pe.matmul(pdt[:, o, 0:CH], wds[:, o * P:(o + 1) * P], dbc[0:RANK, ds(i * CH, CH)], start=True, stop=True).then_inc(mul2, 1)

            @b.scalar
            def _(a):
                a.wait_ge(ld, 64)
                with a.Fori(0, NCH) as i:
                    a.wait_ge(mul, i + 1)
                    a.copy(dbc[:, ds(i * CH, CH)], pd[0:R, 0:CH]).then_inc(evac, 1)
                    for o in range(KD):
                        a.wait_ge(mul2, 2 * i + o + 1)
                        a.activation(dt[:, o, ds(i * CH, CH)], pdt[:, o, 0:CH], ACT.Identity, bias=bds[:, o:o + 1]).then_inc(evac2, 1)
                a.wait_ge(evac2, 2 * NCH)
                for h in range(4):
                    x = dt[:, h // 2, h % 2 * H2:(h % 2 + 1) * H2]
                    a.wait_ge(dve, 9 * h)
                    a.activation(e[:, :], x, ACT.Abs).then_inc(act, 1)
                    a.wait_ge(act, 3 * h + 1)
                    a.activation(e[:, :], e[:, :], ACT.Exp, scale=-1.0).then_inc(act, 1)
                    a.wait_ge(dve, 9 * h + 1)
                    a.activation(lnw[:, :], wv[:, :], ACT.Ln).then_inc(act, 1)

            @b.vector
            def _(v):
                c = Chain(v, dve)
                v.wait_ge(evac2, 2 * NCH)
                for h in range(4):
                    x = dt[:, h // 2, h % 2 * H2:(h % 2 + 1) * H2]
                    v.wait_ge(act, 3 * h + 2)
                    c(v.tensor_scalar(wv[:, :], e[:, :], 1.0, None, ALU.add))
                    v.wait_ge(act, 3 * h + 3)
                    c(v.tensor_scalar(wv[:, :], wv[:, :], -1.0, None, ALU.add))
                    c(v.tensor_scalar(z[:, :], wv[:, :], 0.0, None, ALU.is_equal))
                    c(v.tensor_tensor(wv[:, :], wv[:, :], z[:, :], ALU.add))
                    c(v.tensor_tensor(lnw[:, :], lnw[:, :], z[:, :], ALU.add))
                    c(v.reciprocal(wv[:, :], wv[:, :]))
                    c(v.tensor_tensor(lnw[:, :], lnw[:, :], wv[:, :], ALU.mult))
                    c(v.tensor_tensor(lnw[:, :], lnw[:, :], e[:, :], ALU.mult))
                    c(v.scalar_tensor_tensor(x, x, 0.0, lnw[:, :], ALU.max, ALU.add))
                v.wait_ge(ld, 64)
                for o in range(KD):
                    c(v.tensor_scalar(k.t[:, o, :], xc[:, o, 0:NP], dps[:, o:o + 1], None, ALU.mult))
                    c(v.tensor_tensor(xc[:, o, 0:NP], xc[:, o, 0:NP], dt[:, o, :], ALU.mult))


def mamba_scan(nc, k, a_log, xc, dt, bc, beside=None):
    with Phase(nc, "scan") as ph:
        ld, b_landed, c_landed = ph.sem("ld", "hardware"), ph.sems("b_landed", 2, "hardware"), ph.sems("c_landed", 2, "hardware")
        neg, grown, scanned, outed, summed, carry, passed, asked, flushed = (ph.sem(n) for n in ("neg", "grown", "scanned", "outed", "summed", "carry", "passed", "asked", "flushed"))
        passed_pe, closed = ph.sem("passed_pe"), ph.sem("closed")
        prod = ph.sems("prod", 2)
        A = ph.sb("A", [P, KD, STATES])
        bb, cb = ph.sb("bb", [P, 2, TC]), ph.sb("cb", [P, 2, TC])
        da, dbx, h, hc = (ph.sb(n, [P, 2, KD, TC]) for n in ("da", "dbx", "h", "hc"))
        last, zero = ph.sb("last", [P, KD, STATES]), ph.sb("zero", [P, TC // 2], BF16)
        py = ph.ps("py", [P, KD, 2, 512])
        H2 = TC // 2
        places = [(s, o) for s in range(2) for o in range(KD)]
        mine = places[:-1]
        if beside:
            beside.take(ph, NTC * STATES // 2, width=2)
        with nc.Block() as b:
            @b.sync
            def _(sp):
                sp.dma_start(A[:, :, :], a_log.rearrange("(k p) n -> p k n", p=P)).then_inc(ld, 16)
                with sp.Fori(0, NTC) as c:
                    with sp.Fori(0, STATES // 2) as n:
                        pair = c * (STATES // 2) + n
                        for s in range(2):
                            sp.wait_ge(prod[0], pair * len(mine) + (KD if s == 0 else len(mine)))
                            sp.sem_inc(asked, 1)
                            sp.wait_ge(prod[1], pair + s)
                            sp.sem_inc(asked, 1)
                            sp.wait_ge(b_landed[s], 16 * pair)
                            sp.sem_inc(asked, 1)
                            row = bc[ds(n * 2 + s, 1), ds(c * TC, TC)].rearrange("a t -> (a t)")
                            sp.dma_start(bb[:, s, :], row.partition_broadcast(P)).then_inc(b_landed[s], 16)
                        for s in range(2):
                            sp.wait_ge(outed, (pair * 2 + s + 1) * KD)
                            sp.sem_inc(asked, 1)
                            sp.wait_ge(c_landed[s], 16 * pair)
                            sp.sem_inc(asked, 1)
                            row = bc[ds(n * 2 + (s + STATES), 1), ds(c * TC, TC)].rearrange("a t -> (a t)")
                            sp.dma_start(cb[:, s, :], row.partition_broadcast(P)).then_inc(c_landed[s], 16)

            @b.scalar
            def _(a):
                a.wait_ge(ld, 16)
                a.activation(A[:, :, :], A[:, :, :], ACT.Exp).then_inc(neg, 1)
                a.wait_ge(neg, 2)
                with a.Fori(0, NTC) as c:
                    with a.Fori(0, STATES // 2) as n:
                        for s, o in places:
                            a.wait_ge(scanned, (c * STATES + n * 2 + s) * KD + o + 1)
                            a.activation(da[:, s, o, :], dt[:, o, ds(c * TC, TC)], ACT.Exp, scale=A[:, o, ds(n * 2 + s, 1)]).then_inc(grown, 1)

            @b.vector
            def _(v):
                v.sem_inc(scanned, 2 * KD)
                v.sem_inc(outed, 2 * KD)
                v.sem_inc(prod[1], 1)
                v.memset(zero[:, :], 0.0).then_inc(carry, 1)
                v.memset(last[:, :, :].rearrange("p k n -> p (k n)"), 0.0).then_inc(carry, 1)
                v.wait_ge(neg, 1)
                v.tensor_scalar(A[:, :, :], A[:, :, :], -1.0, None, ALU.mult).then_inc(neg, 1)
                with v.Fori(0, NTC) as c:
                    with v.Fori(0, STATES // 2) as n:
                        pair = c * (STATES // 2) + n
                        for s in range(2):
                            for o in range(KD):
                                if (s, o) not in mine:
                                    v.wait_ge(b_landed[s], 16 * pair + 16)
                                    v.tensor_tensor(dbx[:, s, o, :], xc[:, o, ds(c * TC, TC)], bb[:, s, :], ALU.mult).then_inc(prod[1], 1)
                            for o in range(KD):
                                v.wait_ge(grown, pair * 4 + s * KD + o + 1)
                                if (s, o) in mine:
                                    v.wait_ge(prod[0], pair * len(mine) + s * KD + o + 1 + len(mine))
                                else:
                                    v.wait_ge(prod[1], pair + 2)
                                v.wait_ge(carry, (pair * 2 + s) * KD + 2)
                                v.tensor_tensor_scan(h[:, s, o, :], da[:, s, o, :], dbx[:, s, o, :], last[:, o, ds(n * 2 + s, 1)], ALU.mult, ALU.add).then_inc(scanned, 1)
                            for o in range(KD):
                                g = pair * 4 + s * KD + o
                                v.wait_ge(scanned, g + 1 + 2 * KD)
                                v.wait_ge(c_landed[s], 16 * pair + 16)
                                v.wait_ge(summed, g + 1)
                                v.tensor_tensor(hc[:, s, o, :], h[:, s, o, :], cb[:, s, :], ALU.mult).then_inc(outed, 1)
                                v.tensor_copy(last[:, o, ds(n * 2 + s, 1)], h[:, s, o, TC - 1:TC]).then_inc(carry, 1)
                    v.wait_ge(closed, 2 * KD * c + 2 * KD)
                    for o in range(KD):
                        y = k.t[:, o, ds(c * TC, TC)].rearrange("p (a n) -> p a n", a=2)
                        v.tensor_tensor(y, y, py[:, o, :, 0:H2], ALU.add).then_inc(flushed, 1)

            @b.gpsimd
            def _(g):
                g.sem_inc(prod[0], len(mine))
                with g.Fori(0, NTC) as c:
                    with g.Fori(0, STATES // 2) as n:
                        pair = c * (STATES // 2) + n
                        if beside:
                            beside.ask(g, pair)
                        for s, o in mine:
                            g.wait_ge(b_landed[s], 16 * pair + 16)
                            g.sem_inc(passed, 1)
                            g.wait_ge(scanned, pair * 4 + s * KD + o + 1)
                            g.sem_inc(passed, 1)
                            g.tensor_tensor(dbx[:, s, o, :], xc[:, o, ds(c * TC, TC)], bb[:, s, :], ALU.mult).then_inc(prod[0], 1)
                        if beside:
                            beside.keep(g, pair)

            @b.tensor
            def _(pe):
                pe.sem_inc(summed, 2 * KD)
                pe.wait_ge(carry, 1)
                with pe.Fori(0, NTC) as c:
                    pe.wait_ge(flushed, KD * c)
                    pe.sem_inc(passed_pe, 1)
                    for o in range(KD):
                        for q in range(2):
                            pe.matmul(py[:, o, q, 0:H2], zero[:, 0:P], zero[:, :], start=True, stop=False)
                    with pe.Fori(0, STATES // 2) as n:
                        for s, o in places:
                            at = (c * (STATES // 2) + n) * 4 + s * KD + o
                            pe.wait_ge(outed, at + 1 + 2 * KD)
                            for q in range(2):
                                mm = pe.matmul(py[:, o, q, 0:H2], k.ident[:, :], hc[:, s, o, q * H2:(q + 1) * H2], start=False, stop=False)
                            mm.then_inc(summed, 1)
                    for o in range(KD):
                        for q in range(2):
                            pe.matmul(py[:, o, q, 0:H2], zero[:, 0:P], zero[:, :], start=False, stop=True).then_inc(closed, 1)


def gate_rows(nc, k, zs):
    with Phase(nc, "gz") as ph:
        landed, used, asked = ph.sems("landed", 2, "hardware"), ph.sem("used"), ph.sem("asked")
        z = ph.sb("z", [P, 2, KD, CH])
        with nc.Block() as b:
            @b.sync
            def _(sp):
                with sp.Fori(0, NCH // 2) as i:
                    for s in range(2):
                        sp.wait_ge(used, 2 * i + s + 1)
                        sp.sem_inc(asked, 1)
                        sp.wait_ge(landed[s], 16 * i)
                        sp.dma_start(z[:, s, :, :], zs[:, :, ds((2 * i + s) * CH, CH)]).then_inc(landed[s], 16)

            @b.vector
            def _(v):
                v.sem_inc(used, 2)
                with v.Fori(0, NCH // 2) as i:
                    for s in range(2):
                        v.wait_ge(landed[s], 16 * i + 16)
                        t = k.t[:, :, ds((2 * i + s) * CH, CH)]
                        v.tensor_tensor(t, t, z[:, s, :, :], ALU.mult).then_inc(used, 1)


def fetch_rows(nc, k, table):
    with Phase(nc, "fr") as ph:
        landed = ph.row_dmas(G, 16 * NG)
        staged, passed, added = ph.sem("staged"), ph.sem("passed"), ph.sem("added")
        ix, rows = ph.sb("ix", [P, G], U32), ph.sb("rows", [P, G, D])
        with nc.Block() as b:
            @b.gpsimd
            def _(g):
                with g.Fori(0, NG) as i:
                    for j in range(G):
                        g.wait_ge(staged, i * G + j + 1)
                        g.sem_inc(passed, 1)
                        g.indirect_dma_start(rows[:, j, :], None, table, bass.IndirectOffsetOnAxis(ap=ix[:, j:j + 1], axis=0)).then_inc(landed[j].sem, 16)

            @b.vector
            def _(v):
                for j in range(G):
                    v.tensor_copy(ix[:, j:j + 1], k.rank[:, j:j + 1]).then_inc(staged, 1)
                with v.Fori(0, NG) as i:
                    for j in range(G):
                        landed[j].wait(v, 16 * i + 16)
                        v.tensor_tensor(k.rows[:, ds(i * G + j, 1), :], rows[:, j:j + 1, :], k.y[:, ds(i * G + j, 1), :], ALU.add).then_inc(added, 1)
                        v.wait_ge(added, i * G + j + 1)
                        v.tensor_copy(ix[:, j:j + 1], k.rank[:, ds(i * G + j + G, 1)]).then_inc(staged, 1)


def edge_scores(nc, k, lists, ev):
    gi, kl, wl, own = lists
    iters = ST // RING
    with Phase(nc, "sc") as ph:
        oh_ready, tr, tcopied, mul, joined, added = (ph.sem(n) for n in ("oh", "tr", "tcopied", "mul", "joined", "added"))
        dve, act, gp = ph.sem("dve"), ph.sem("act"), ph.sem("gp")
        PARTS = 3
        oh, ident = ph.sb("oh", [P, RING, P], BF16), ph.sb("ident", [P, P], BF16)
        tgt, rest = ph.sb("tgt", [P, NT, PARTS, HEADS], BF16), ph.sb("rest", [P, NT, HEADS])
        got = ph.sb("got", [P, 2, HALF, HEADS])
        Q = 4
        oht = ph.sb("oht", [P, RING, P], BF16)
        valid, far = ph.sb("valid", [P, SP_]), ph.sb("far", [P, SP_])
        low = ph.sb("low", [P, SP_, HEADS])
        top, alltop = ph.sb("top", [P, 1]), ph.sb("alltop", [P, 1])
        pt, pe4 = ph.ps("pt", [P, RING // Q, 1024], BF16), ph.ps("pe4", [P, 2, 512])
        with nc.Block() as b:
            @b.gpsimd
            def _(g):
                g.wait_ge(dve, 9 + 2 * PARTS)
                g.partition_all_reduce(alltop[:, :], top[:, :], P, RMAX).then_inc(gp, 1)

            def one_hots(v, first, h):
                for j in range(h * HALF, (h + 1) * HALF):
                    v.tensor_scalar(oh[:, j, :], k.iota[:, 0:P], kl[:, ds(first + j, 1)], None, ALU.is_equal).then_inc(oh_ready, 1)

            @b.vector
            def _(v):
                c = Chain(v, dve)
                v.sem_inc(added, 1)
                c(v.tensor_copy(rest[:, :, :], k.score[:, :, 1, :]))
                for q in range(PARTS):
                    c(v.tensor_copy(tgt[:, :, q, :], rest[:, :, :]))
                    c(v.tensor_tensor(rest[:, :, :], rest[:, :, :], tgt[:, :, q, :], ALU.subtract))
                c(v.tensor_copy(ident[:, :], k.ident[:, :]))
                c(v.memset(ev[:, ST:SP_, :].rearrange("p a h -> p (a h)"), 0.0))
                one_hots(v, 0, 0)
                with v.Fori(0, iters) as i:
                    for h in range(2):
                        one_hots(v, i * RING + (RING if h else 0), 1 - h)
                        v.wait_ge(mul, 2 * i + h + 1)
                        v.tensor_reduce(got[:, h, :, :], pe4[:, h, 0:HALF * PARTS * HEADS].rearrange("p (j q h) -> p j h q", q=PARTS, h=HEADS),
                                        AX_X, ALU.add).then_inc(joined, 1)
                        v.wait_ge(joined, 2 * i + h + 1)
                        slots = ev[:, ds(i * RING + h * HALF, HALF), :]
                        v.tensor_tensor(slots, slots, got[:, h, :, :], ALU.add).then_inc(added, 1)
                v.wait_ge(added, 2 * iters + 1)
                c(v.tensor_scalar(valid[:, :], kl[:, :], 0.0, None, ALU.is_ge))
                c(v.tensor_scalar(far[:, :], valid[:, :], 1e30, -1e30, ALU.mult, ALU.add))
                c(v.tensor_tensor(ev[:, :, :], ev[:, :, :], spread(far[:, :], HEADS), ALU.add))
                c(v.tensor_scalar(low[:, :, :], ev[:, :, :], 0.2, None, ALU.mult))
                c(v.tensor_tensor(ev[:, :, :], ev[:, :, :], low[:, :, :], ALU.max))
                c(v.tensor_reduce(top[:, :], ev[:, :, :].rearrange("p a h -> p (a h)"), AX_X, ALU.max))
                v.wait_ge(gp, 1)
                c(v.tensor_scalar(top[:, :], alltop[:, :], -1.0, None, ALU.mult))

            @b.tensor
            def _(pe):
                number = [pe.alloc_register(f"sc_tile{j}") for j in range(RING)]
                pe.wait_ge(dve, 2 + 2 * PARTS)
                with pe.Fori(0, iters) as i:
                    def turn_over(q):
                        for j in range(q * Q, (q + 1) * Q):
                            pe.wait_ge(oh_ready, i * RING + j + 1)
                            if j % Q == 0:
                                pe.wait_ge(tcopied, i * (RING // Q) + q + 1)
                            mm = pe.transpose(pt[:, q, j % Q * P:(j % Q + 1) * P], oh[:, j, :], ident[:, :])
                        mm.then_inc(tr, 1)

                    def look_up(q):
                        h = q * Q // HALF
                        if q * Q % HALF == 0:
                            pe.wait_ge(added, 2 * i + h)
                        pe.wait_ge(tcopied, i * (RING // Q) + q + 1 + RING // Q)
                        for j in range(q * Q, (q + 1) * Q):
                            mm = pe.matmul(pe4[:, h, j % HALF * PARTS * HEADS:(j % HALF + 1) * PARTS * HEADS], oht[:, j, :],
                                           tgt[:, ds(tiles[j], 1), :, :].rearrange("p a q h -> p (a q h)"), start=True, stop=True)
                        if (q + 1) * Q % HALF == 0:
                            mm.then_inc(mul, 1)

                    turn_over(0)
                    tiles = load_tiles(pe, number, own, i * RING)
                    for q in range(1, RING // Q):
                        turn_over(q)
                        look_up(q - 1)
                    look_up(RING // Q - 1)

            @b.scalar
            def _(a):
                a.sem_inc(tcopied, RING // Q)
                with a.Fori(0, iters) as i:
                    for q in range(RING // Q):
                        a.wait_ge(tr, i * (RING // Q) + q + 1)
                        a.wait_ge(mul, 2 * i)
                        a.copy(oht[:, q * Q:(q + 1) * Q, :].rearrange("p j n -> p (j n)"), pt[:, q, 0:Q * P]).then_inc(tcopied, 1)
                a.wait_ge(dve, 10 + 2 * PARTS)
                a.activation(ev[:, :, :], ev[:, :, :], ACT.Exp, bias=top[:, 0:1]).then_inc(act, 1)


def attend(nc, k, lists, table, ev, ag):
    gi, kl, _, own = lists
    iters = ST // RING
    with Phase(nc, "at") as ph:
        landed = ph.row_dmas(RING, 16 * iters)
        staged, passed, oh_ready, behind, scaled, summed, added = (ph.sem(n) for n in ("staged", "passed", "oh", "behind", "scaled", "summed", "added"))
        ix = ph.sb("ix", [P, RING], U32)
        rows, oh = ph.sb("rows", [P, RING, D + HEADS]), ph.sb("oh", [P, RING, P])
        dist = ph.sb("dist", [P, RING, P])
        far, asked = ph.sem("far"), ph.sem("asked")
        NB = 4
        pa = ph.ps("pa", [P, NB, 512])
        with nc.Block() as b:
            @b.gpsimd
            def _(g):
                with g.Fori(0, iters) as i:
                    for j in range(RING):
                        if j % HALF == 0:
                            g.wait_ge(staged, 2 * i + j // HALF + 1)
                            g.sem_inc(passed, 1)
                        g.indirect_dma_start(rows[:, j, 0:D], None, table, bass.IndirectOffsetOnAxis(ap=ix[:, j:j + 1], axis=0)).then_inc(landed[j].sem, 16)

            @b.scalar
            def _(a):
                with a.Fori(0, iters) as i:
                    for h in range(2):
                        a.wait_ge(added, i * RING + h * NB)
                        a.sem_inc(asked, 1)
                        half = range(h * HALF, (h + 1) * HALF)
                        for j in half:
                            a.activation(dist[:, j, :], k.iota[:, 0:P], ACT.Abs, bias=kl[:, ds(i * RING + j, 1)], scale=-1.0).then_inc(far, 1)
                        for j in half:
                            a.wait_ge(far, i * RING + j + 1)
                            a.activation(oh[:, j, :], dist[:, j, :], ACT.Relu, bias=k.ones[:, 0:1], scale=-1.0).then_inc(oh_ready, 1)

            @b.vector
            def _(v):
                number = [v.alloc_register(f"at_tile{j}") for j in range(HALF)]
                v.memset(ag[:, :, :].rearrange("p t c -> p (t c)"), 0.0).then_inc(added, NB)
                v.tensor_copy(ix[:, 0:HALF], gi[:, 0:HALF]).then_inc(staged, 1)
                v.tensor_copy(ix[:, HALF:RING], gi[:, HALF:RING]).then_inc(staged, 1)
                with v.Fori(0, iters) as i:
                    for h in range(2):
                        tiles = load_tiles(v, number, own, i * RING + h * HALF)

                        v.tensor_copy(rows[:, h * HALF:(h + 1) * HALF, D:D + HEADS], ev[:, ds(i * RING + h * HALF, HALF), :]).then_inc(behind, 1)

                        def scale(j):
                            landed[j].wait(v, 16 * i + 16)
                            heads = rows[:, j, 0:D].rearrange("p (h f) -> p h f", h=HEADS)
                            v.tensor_tensor(heads, heads, spread(ev[:, ds(i * RING + j, 1), :].rearrange("p a h -> p (a h)"), D // HEADS), ALU.mult).then_inc(scaled, 1)

                        scale(h * HALF)
                        scale(h * HALF + 1)
                        for j in range(h * HALF, (h + 1) * HALF):
                            if j + 2 < (h + 1) * HALF:
                                scale(j + 2)
                            tile = tiles[j % HALF]
                            v.wait_ge(summed, i * RING + j + 1)
                            v.wait_ge(added, i * RING + j + NB)
                            sums = ag[:, ds(tile, 1), :].rearrange("p a c -> p (a c)")
                            v.tensor_tensor(sums, sums, pa[:, j % NB, 0:D + HEADS], ALU.add).then_inc(added, 1)
                        v.tensor_copy(ix[:, h * HALF:(h + 1) * HALF], gi[:, ds(i * RING + RING + h * HALF, HALF)]).then_inc(staged, 1)

            @b.tensor
            def _(pe):
                with pe.Fori(0, iters) as i:
                    for j in range(RING):
                        pe.wait_ge(oh_ready, i * RING + j + 1)
                        pe.wait_ge(scaled, i * RING + j + 1)
                        pe.wait_ge(added, i * RING + j + 1)
                        pe.wait_ge(behind, 2 * i + j // HALF + 1)
                        pe.matmul(pa[:, j % NB, 0:D + HEADS], oh[:, j, :], rows[:, j, :], start=True, stop=True).then_inc(summed, 1)


def local_rows(nc, k, ag, bias):
    with Phase(nc, "lr") as ph:
        ld, dve, act = ph.sem("ld", "hardware"), ph.sem("dve"), ph.sem("act")
        bb, inv, low = ph.sb("bb", [P, D]), ph.sb("inv", [P, NT, HEADS]), ph.sb("low", [P, NT, D])
        F = D // HEADS
        with nc.Block() as b:
            @b.sync
            def _(sp):
                sp.dma_start(bb[:, :], bias.partition_broadcast(P)).then_inc(ld, 16)

            @b.vector
            def _(v):
                c = Chain(v, dve)
                c(v.tensor_scalar(inv[:, :, :], ag[:, :, D:D + HEADS], 1e-16, None, ALU.add))
                c(v.reciprocal(inv[:, :, :], inv[:, :, :]))
                for h in range(HEADS):
                    v.tensor_tensor(k.rows[:, :, h * F:(h + 1) * F], ag[:, :, h * F:(h + 1) * F], spread(inv[:, :, h], F), ALU.mult).then_inc(dve, 1)
                c.n += HEADS
                v.wait_ge(dve, c.n)
                c(v.tensor_tensor(k.rows[:, :, :], k.rows[:, :, :], k.y[:, :, :], ALU.add))
                v.wait_ge(ld, 16)
                c(v.tensor_tensor(k.rows[:, :, :], k.rows[:, :, :], bb[:, :].unsqueeze(1).broadcast_to([P, NT, D]), ALU.add))
                c(v.tensor_scalar(low[:, :, :], k.rows[:, :, :], 0.0, None, ALU.min))
                v.wait_ge(act, 1)
                c(v.scalar_tensor_tensor(k.rows[:, :, :], k.rows[:, :, :], 0.0, low[:, :, :], ALU.max, ALU.add))
                c(v.tensor_scalar(k.rows[:, :, :], k.rows[:, :, :], -1.0, None, ALU.add))

            @b.scalar
            def _(a):
                a.wait_ge(dve, 5 + HEADS)
                a.activation(low[:, :, :], low[:, :, :], ACT.Exp).then_inc(act, 1)


def gate_and_feed(nc, k, t2, wl, wg, w1, b1, w2, b2):
    KH = 2 * KD
    with Phase(nc, "gf") as ph:
        ld = ph.sem("ld", "hardware")
        gmul, gated, dve, mixed, hmul, hidden, omul, fin = (ph.sem(n) for n in ("gmul", "gated", "dve", "mixed", "hmul", "hidden", "omul", "fin"))
        wls, wgs = ph.sb("wl", [P, KD, D]), ph.sb("wg", [P, KD, D])
        w1s, w2s = ph.sb("w1", [P, KD, 2 * D]), ph.sb("w2", [P, KH, D])
        b1s, b2s = ph.sb("b1", [P, KH]), ph.sb("b2", [P, KD])
        gate, dif, hid = ph.sb("gate", [P, KD, CH]), ph.sb("dif", [P, KD, CH]), ph.sb("hid", [P, KH, CH])
        pg, phid, po = ph.ps("pg", [P, KD, 512]), ph.ps("ph", [P, KH, 512]), ph.ps("po", [P, KD, 512])
        with nc.Block() as b:
            @b.sync
            def _(sp):
                for dst, w in ((wls, wl), (wgs, wg), (w1s, w1), (w2s, w2)):
                    sp.dma_start(dst[:, :, :], w.rearrange("(k p) n -> p k n", p=P)).then_inc(ld, 16)
                sp.dma_start(b1s[:, :], b1).then_inc(ld, 16)
                sp.dma_start(b2s[:, :], b2).then_inc(ld, 16)

            @b.tensor
            def _(pe):
                pe.wait_ge(ld, 96)
                def gate_products(i):
                    pe.wait_ge(gated, KD * i)
                    for o in range(KD):
                        for q in range(KD):
                            pe.matmul(pg[:, o, 0:CH], wls[:, q, o * P:(o + 1) * P], k.t[:, q, ds(i * CH, CH)], start=q == 0, stop=False)
                        for q in range(KD):
                            mm = pe.matmul(pg[:, o, 0:CH], wgs[:, q, o * P:(o + 1) * P], t2[:, q, ds(i * CH, CH)], start=False, stop=q == KD - 1)
                        mm.then_inc(gmul, 1)

                def chunk(i, more):
                    pe.wait_ge(hidden, KH * i)
                    pe.wait_ge(mixed, i + 1)
                    for f in range(KH):
                        for q in range(KD):
                            mm = pe.matmul(phid[:, f, 0:CH], w1s[:, q, f * P:(f + 1) * P], k.t[:, q, ds(i * CH, CH)], start=q == 0, stop=q == KD - 1)
                        mm.then_inc(hmul, 1)
                    if more:
                        gate_products(i + 1)
                    pe.wait_ge(fin, KD * i)
                    pe.wait_ge(hidden, KH * i + KH)
                    for o in range(KD):
                        for f in range(KH):
                            mm = pe.matmul(po[:, o, 0:CH], w2s[:, f, o * P:(o + 1) * P], hid[:, f, :], start=f == 0, stop=f == KH - 1)
                        mm.then_inc(omul, 1)

                gate_products(0)
                with pe.Fori(0, NCH - 1) as i:
                    chunk(i, True)
                chunk(NCH - 1, False)

            @b.scalar
            def _(a):
                a.wait_ge(ld, 96)
                def gates(i):
                    a.wait_ge(mixed, i)
                    for o in range(KD):
                        a.wait_ge(gmul, KD * i + o + 1)
                        a.activation(gate[:, o, :], pg[:, o, 0:CH], ACT.Sigmoid).then_inc(gated, 1)

                def chunk(i, more):
                    a.wait_ge(omul, KD * i)
                    for f in range(KH):
                        a.wait_ge(hmul, KH * i + f + 1)
                        a.activation(hid[:, f, :], phid[:, f, 0:CH], ACT.Relu, bias=b1s[:, f:f + 1]).then_inc(hidden, 1)
                    if more:
                        gates(i + 1)

                gates(0)
                with a.Fori(0, NCH - 1) as i:
                    chunk(i, True)
                chunk(NCH - 1, False)

            @b.vector
            def _(v):
                v.wait_ge(ld, 96)
                def mix(i):
                    one, two = k.t[:, :, ds(i * CH, CH)], t2[:, :, ds(i * CH, CH)]
                    v.wait_ge(mixed, i)
                    v.tensor_tensor(dif[:, :, :], one, two, ALU.subtract).then_inc(dve, 1)
                    v.wait_ge(gated, KD * i + KD)
                    v.wait_ge(dve, 2 * i + 1)
                    v.tensor_tensor(dif[:, :, :], dif[:, :, :], gate[:, :, :], ALU.mult).then_inc(dve, 1)
                    v.wait_ge(dve, 2 * i + 2)
                    v.wait_ge(gmul, KD * i + KD)
                    v.tensor_tensor(one, two, dif[:, :, :], ALU.add).then_inc(mixed, 1)
                    v.wait_ge(mixed, i + 1)

                def chunk(i, more):
                    if more:
                        mix(i + 1)
                    v.wait_ge(hmul, KH * i + KH)
                    for o in range(KD):
                        v.wait_ge(omul, KD * i + o + 1)
                        t = k.t[:, o, ds(i * CH, CH)]
                        v.scalar_tensor_tensor(t, po[:, o, 0:CH], b2s[:, o:o + 1], t, ALU.add, ALU.add).then_inc(fin, 1)

                mix(0)
                with v.Fori(0, NCH - 1) as i:
                    chunk(i, True)
                chunk(NCH - 1, False)


def attention_layer(nc, k, a, by_dst, drams):
    xs, ys, zs, bc, vrow, table, stable = drams

    def w(name):
        return a["L3_gnn_" + name]

    with ExitStack() as ctx:
        def sb(name, shape, dt=F32):
            return ctx.enter_context(nc.sbuf_tensor(name, shape, dt))

        k.rank, k.score, ev = sb("rank", [P, NT + G], U32), sb("score", [P, NT, 2, HEADS]), sb("ev", [P, SP_, HEADS])
        normalise(nc, "n6", k, keep=True, dest=k.t)
        transform(nc, "tg", k, k.t, w("gat_w"), "gat", table=table, heads=(w("gat_a_src"), w("gat_a_tgt")), scores=stable)
        with ExitStack() as gathering:
            fetch = ScoreGather(nc, gathering, stable, by_dst[0], ev)
            order_nodes(nc, k, a["node_vec"], vrow, xs, beside=fetch, steps=5)
            turn(nc, "tx", k, k.t, table=xs, beside=fetch, steps=1)
            with nc.sbuf_tensor("xc", [P, KD, NP + TAPS - 1], F32) as xc, nc.sbuf_tensor("dt", [P, KD, NP], F32) as dt:
                mamba_in(nc, k, w("in_proj_w"), xc, zs, beside=fetch, steps=3)
                mamba_conv(nc, k, w("conv_w"), w("conv_b"), xc, dt, beside=fetch, steps=1)
                mamba_steps(nc, k, w("x_proj_w"), w("dt_proj_w"), w("dt_proj_b"), w("D_param"), xc, dt, bc, beside=fetch, steps=9)
                mamba_scan(nc, k, w("A_log"), xc, dt, bc, beside=fetch)
            gate_rows(nc, k, zs)
            transform(nc, "tm", k, k.t, w("out_proj_w"), "rows", table=ys, beside=fetch, steps=fetch.left())
        k.rows = sb("rows", [P, NT, D])
        with nc.sbuf_tensor("ag", [P, NT, D + HEADS], F32) as ag:
            edge_scores(nc, k, by_dst, ev)
            attend(nc, k, by_dst, table, ev, ag)
            local_rows(nc, k, ag, w("gat_b"))
        affine_norm(nc, "nl", k, k.rows, w("ln_local_g"), w("ln_local_b"), k.rows, False)
        turn(nc, "tl", k, k.t, rows=k.rows)
        fetch_rows(nc, k, ys)
        affine_norm(nc, "ng", k, k.rows, w("ln_global_g"), w("ln_global_b"), k.rows, False)
        with nc.sbuf_tensor("t2", [P, KD, NP], F32) as t2:
            turn(nc, "tt", k, t2, rows=k.rows)
            gate_and_feed(nc, k, t2, w("wl"), w("wg"), w("ff1_w"), w("ff1_b"), w("ff2_w"), w("ff2_b"))
        turn_back(nc, "tb", k, k.t, k.y)
        affine_norm(nc, "n2g", k, k.y, w("ln2_g"), w("ln2_b"), k.x, True)


class Keep:
    pass


def program(nc, a, out):
    k = Keep()
    with ExitStack() as ctx:
        def sb(name, shape, dt=F32):
            return ctx.enter_context(nc.sbuf_tensor(name, shape, dt))

        def dram(name, shape, dt=F32):
            return nc.dram_tensor(name, shape, dt).ap()

        k.x, k.y, k.t = sb("x_sb", [P, NT, D]), sb("y_sb", [P, NT, D]), sb("t_sb", [P, KD, NP])
        k.ident, k.before, k.ones, k.onesmask = (sb(n, [P, P]) for n in ("ident", "before", "ones", "onesmask"))
        k.iota, k.onerow = sb("iota", [P, SP_]), sb("onerow", [P, EC])
        k.pnum, k.pnum_i, k.lastmask = sb("pnum", [P, 1]), sb("pnum_i", [P, 1], I32), sb("lastmask", [P, 1])
        k.dinv, k.deg_in, k.deg_out = sb("dinv", [P, NT]), sb("deg_in", [P, NT]), sb("deg_out", [P, NT])
        by_src = (sb("s_gi", [P, SP_], U32), sb("s_kl", [P, SP_]), sb("s_wl", [P, SP_]), sb("s_own", [1, SP_], I32))
        by_dst = (sb("d_gi", [P, SP_], U32), sb("d_kl", [P, SP_]), None, sb("d_own", [1, SP_], I32))
        k.lg, k.expert, k.small = sb("lg", [P, NT, 8]), sb("expert", [P, NT, 9]), sb("small", [P, NT])
        k.coef, k.back = sb("coef", [P, 3 * NT]), sb("back", [P, 3 * NT + G], U32)
        k.block_expert = sb("block_expert", [1, MAX_BLOCKS], I32)
        xbuf, ybuf = dram("xbuf", (MAX_BLOCKS * BLOCK + 3 * NP, D)), dram("ybuf", (MAX_BLOCKS * BLOCK, D))
        RowDma.values.clear()
        nc.row_dma = [ctx.enter_context(nc.semaphore(f"row_dma{j}", n)) for j, n in enumerate(ROW_DMAS)]
        table = dram("table", (NP, D))
        rec_s, rec_d = dram("rec_s", (P * ST, REC), I32), dram("rec_d", (P * ST, REC), I32)

        xs, ys, stable = dram("xs", (NP, D)), dram("ys", (NP, D)), dram("stable", (NP, HEADS))
        zs, bc, vrow = dram("zs", (P, KD, NP)), dram("bc", (2 * STATES, NP)), dram("vrow", (NP,))

        def edges(v):
            return v.rearrange("(p c) -> p c", c=EC)

        load_constants(nc, k, a["x"])
        sorting = ctx.enter_context(ExitStack())
        sort_d = SlotScatter(nc, "by_dst", sorting, rec_d, by_dst, k.deg_in)
        with ExitStack() as once:
            sort_s = SlotScatter(nc, "by_src", once, rec_s, by_src, k.deg_out)
            sort_edges(nc, k, edges(a["src"]), edges(a["dst"]), edges(a["edge_weight"]), sort_s, sort_d, xbuf[0:MAX_BLOCKS * BLOCK, :])
        normalise(nc, "n0", k, table=table, beside=sort_d, steps=2)
        aggregate(nc, "a0", k, by_src, table, k.t, True)
        transform(nc, "t0", k, k.t, a["L0_gnn_WT"], "add", beside=sort_d, steps=1)
        normalise(nc, "n1", k, keep=True, dest=k.t, beside=sort_d, steps=2)
        logits(nc, "g1", k, D, a["L0_ffn_gate_w"], a["L0_ffn_gate_b"], 8, k.lg[:, :, 0:8], beside=sort_d, steps=1)
        route(nc, "r1", k, k.lg[:, :, 0:8], 8, "capacity", xbuf, 16, beside=sort_d, steps=1)
        expert_blocks(nc, "e1", k, xbuf, ybuf, 16, [(a["L0_ffn_w1"], a["L0_ffn_b1"], ACT.Relu)], (a["L0_ffn_w2"], a["L0_ffn_b2"]), beside=sort_d)
        combine(nc, "c1", k, ybuf[0:16 * BLOCK, :], 1)
        finish_sort(nc, sort_d, k)
        sorting.close()
        degrees(nc, k)
        normalise(nc, "n2", k, scale=k.dinv, table=table, dest=k.t)
        for l in range(3):
            aggregate(nc, f"a2{l}", k, by_dst, table, k.t, False)
            transform(nc, f"t2{l}", k, k.t, a["L1_gnn_W"][l], "next" if l < 2 else "last", a["L1_gnn_b"][l], table)
        normalise(nc, "n3", k, keep=True, dest=k.t)
        logits(nc, "g3", k, D, a["L1_ffn_Wr"], None, 8, k.lg[:, :, 0:8])
        nb = SHARED_BLOCKS + block_count(2 * N_NODES, 8)
        nb += nb % 2
        route(nc, "r3", k, k.lg[:, :, 0:8], 8, "shared", xbuf, nb)
        expert_blocks(nc, "e3", k, xbuf, ybuf, nb, [(a["L1_ffn_W1"], a["L1_ffn_b1"], ACT.Gelu)], (a["L1_ffn_W2"], a["L1_ffn_b2"]))
        combine(nc, "c3", k, ybuf[0:nb * BLOCK, :], 2, shared=True)
        normalise(nc, "n4", k, scale=k.dinv, table=table, dest=k.t)
        aggregate(nc, "a4", k, by_dst, table, k.t, False)
        transform(nc, "t4", k, k.t, a["L2_gnn_WT"], "keep", a["L2_gnn_b"])
        batch_norm(nc, k, a["L2_gnn_gamma"], a["L2_gnn_beta"])
        normalise(nc, "n5", k, keep=True, dest=k.t)
        logits(nc, "g5", k, P, a["L2_ffn_router_w2"], a["L2_ffn_router_b2"], 6, k.lg[:, :, 0:6], ACT.Relu, a["L2_ffn_router_w1"], a["L2_ffn_router_b1"])
        nb = block_count(2 * N_NODES, 6)
        route(nc, "r5", k, k.lg[:, :, 0:6], 6, "soft2", xbuf, nb)
        expert_blocks(nc, "e5", k, xbuf, ybuf, nb, [(a["L2_ffn_expert_w1"], a["L2_ffn_expert_b1"], ACT.Relu), (a["L2_ffn_expert_w2"], a["L2_ffn_expert_b2"], ACT.Relu)],
                      (a["L2_ffn_expert_w3"], a["L2_ffn_expert_b3"]))
        combine(nc, "c5", k, ybuf[0:nb * BLOCK, :], 2)
        attention_layer(nc, k, a, by_dst, (xs, ys, zs, bc, vrow, table, stable))
        normalise(nc, "n7", k, keep=True, dest=k.t)
        logits(nc, "g7", k, 1024, a["L3_ffn_Wg"], a["L3_ffn_bg"], 8, k.lg[:, :, 0:8], ACT.Gelu, a["L3_ffn_W1"], a["L3_ffn_b1"])
        nb = block_count(N_NODES, 8)
        route(nc, "r7", k, k.lg[:, :, 0:8], 8, "top1", xbuf, nb)
        expert_blocks(nc, "e7", k, xbuf, ybuf, nb, [(a["L3_ffn_W1"].unsqueeze(0), a["L3_ffn_b1"].unsqueeze(0), ACT.Gelu)], (a["L3_ffn_Wd"], a["L3_ffn_bd"]))
        combine(nc, "c7", k, ybuf[0:nb * BLOCK, :], 1)
        store(nc, k, out)


def store(nc, k, out):
    with Phase(nc, "out") as ph:
        done = ph.sems("done", 2, "hardware")
        with nc.Block() as b:
            @b.sync
            def _(sp):
                sp.dma_start(out[0:(NT - 1) * P, :].rearrange("(t p) d -> p t d", p=P), k.x[:, 0:NT - 1, :]).then_inc(done[0], 16)
                sp.dma_start(out[(NT - 1) * P:N_NODES, :], k.x[0:LAST, NT - 1, :]).then_inc(done[1], 16)
                sp.wait_ge(done[0], 16)
                sp.wait_ge(done[1], 16)


_TRANSPOSED = ("L0_gnn_W", "L2_gnn_W")
_L3_TRANSPOSED = ("gat_w", "in_proj_w", "x_proj_w", "dt_proj_w", "out_proj_w", "wl", "wg", "ff1_w", "ff2_w")
_L3_BY_PARTITION = ("conv_b", "dt_proj_b", "D_param", "ff1_b", "ff2_b")


def host_layout(inputs):
    import numpy as np
    arrays = {}
    for name, v in inputs.items():
        v = np.asarray(v)
        if name in _TRANSPOSED:
            name, v = name + "T", v.T
        arrays[name] = np.ascontiguousarray(v)
    for n in ("L0_ffn_b1", "L1_ffn_b1s", "L1_ffn_b1p", "L2_ffn_expert_b1", "L2_ffn_expert_b2", "L2_ffn_router_b1", "L3_ffn_b1"):
        v = arrays[n]
        arrays[n] = np.ascontiguousarray(np.swapaxes(v.reshape(v.shape[:-1] + (-1, P)), -1, -2))
    for n in _L3_TRANSPOSED:
        arrays["L3_gnn_" + n] = np.ascontiguousarray(arrays["L3_gnn_" + n].T)
    for n in _L3_BY_PARTITION:
        arrays["L3_gnn_" + n] = np.ascontiguousarray(arrays["L3_gnn_" + n].reshape(-1, P).T)
    noise = np.zeros(NP, arrays["node_vec"].dtype)
    noise[:N_NODES] = arrays["node_vec"]
    arrays["node_vec"] = np.ascontiguousarray(noise.reshape(NT, P).T)
    for n in ("W1", "b1", "W2", "b2"):
        shared, private = arrays.pop(f"L1_ffn_{n}s"), arrays.pop(f"L1_ffn_{n}p")
        arrays[f"L1_ffn_{n}"] = np.concatenate([private, shared[None]], axis=0)
    return arrays


def kernel(**inputs):
    import numpy as np
    import concourse.bacc as bacc
    from concourse.bass_utils import run_bass_kernel_spmd

    nc = bacc.Bacc("TRN2", target_bir_lowering=False, num_devices=1)
    arrays, args = {}, {}
    for name, v in host_layout(inputs).items():
        arrays[f"in_{name}"] = v
        args[name] = nc.dram_tensor(f"in_{name}", v.shape, mybir.dt.from_np(v.dtype), kind="ExternalInput").ap()
    out = nc.dram_tensor("out_x", (N_NODES, D), F32, kind="ExternalOutput").ap()
    program(nc, args, out)
    r = run_bass_kernel_spmd(nc, [arrays], core_ids=[0])
    return r.results[0]["out_x"]
```
